# Optimizing a Trainium2 kernel written in Bass

```python
import numpy as np
import jax
import jax.numpy as jnp

def _softmax(x, axis=-1):
    return jax.nn.softmax(x, axis=axis)

def _gelu(x):
    return jax.nn.gelu(x, approximate=True)

def _silu(x):
    return jax.nn.silu(x)

def _sigmoid(x):
    return jax.nn.sigmoid(x)

def _layernorm(x, axis=-1, eps=1e-05):
    m = jnp.mean(x, axis=axis, keepdims=True)
    v = jnp.var(x, axis=axis, keepdims=True)
    return (x - m) / jnp.sqrt(v + eps)

def _scatter_add(tgt, idx, src, axis=0):
    return tgt.at[idx].add(src)

def _segment_sum(src, seg, n):
    return jax.ops.segment_sum(src, seg, n)
kernel_name = 'mk_conv_attn_hybrid_d4_conv_nchw512_r4_26451d'

def setup_inputs(seed: int=0):
    np.random.seed(seed)
    _w = jnp.asarray

    def _rec_inputs():
        import jax
        import jax.numpy as jnp
        _gk = jax.random.key(seed)
        x = -0.0002928 + 1 * jax.random.normal(jax.random.fold_in(_gk, 1), (8, 128, 32, 32), jnp.float32)
        return x
    x = _rec_inputs()

    def _L0_conv_setup():
        import jax, jax.numpy as jnp
        import numpy as np
        CH = 128
        HEADS = 8
        GROUPS = 32
        EPS = 1e-05
        key = jax.random.key(seed)
        ks = jax.random.split(key, 4)
        x = jax.random.normal(ks[0], (8, CH, 32, 32), dtype=jnp.float32)
        norm_w = jnp.ones((CH,), jnp.float32)
        norm_b = jnp.zeros((CH,), jnp.float32)
        qkv_w = jax.random.normal(ks[1], (3 * CH, CH), jnp.float32) * CH ** (-0.5)
        qkv_b = jnp.zeros((3 * CH,), jnp.float32)
        proj_w = jax.random.normal(ks[2], (CH, CH), jnp.float32) * 0.02
        proj_b = jnp.zeros((CH,), jnp.float32)
        return {'x': x, 'norm_w': norm_w, 'norm_b': norm_b, 'qkv_w': qkv_w, 'qkv_b': qkv_b, 'proj_w': proj_w, 'proj_b': proj_b}
    _L0_conv_all = _L0_conv_setup()
    _L0_conv_in = {k: v for k, v in _L0_conv_all.items() if k in ('norm_w', 'norm_b', 'qkv_w', 'qkv_b', 'proj_w', 'proj_b')}
    del _L0_conv_all

    def _L1_conv_setup():
        import jax, jax.numpy as jnp
        import numpy as np
        from jax import lax
        EPS = 1e-05
        DW_THRESH = 4.0
        PW_THRESH = 0.001
        C_IN = 128
        C_OUT = 128

        def _bn(x, g, b, m, v):
            inv = g * lax.rsqrt(v + EPS)
            return x * inv[None, :, None, None] + (b - m * inv)[None, :, None, None]

        def _prune(x, thresh):
            amax = jnp.max(jnp.abs(x), axis=(2, 3), keepdims=True)
            return jnp.where(amax < thresh, jnp.zeros_like(x), x)
        key = jax.random.key(seed)
        ks = jax.random.split(key, 8)
        B, H, W = (16, 28, 28)
        x = jax.random.normal(ks[0], (B, C_IN, H, W), dtype=jnp.float32)
        dw_w = jax.random.normal(ks[1], (C_IN, 1, 3, 3), dtype=jnp.float32) * 0.1
        dw_b = jax.random.normal(ks[2], (C_IN,), dtype=jnp.float32) * 0.1
        bn1_g = jnp.ones((C_IN,), jnp.float32)
        bn1_b = jnp.zeros((C_IN,), jnp.float32)
        bn1_m = jnp.zeros((C_IN,), jnp.float32)
        bn1_v = jnp.ones((C_IN,), jnp.float32)
        pw_w = jax.random.normal(ks[3], (C_OUT, C_IN, 1, 1), dtype=jnp.float32) * 0.05
        pw_b = jax.random.normal(ks[4], (C_OUT,), dtype=jnp.float32) * 0.1
        bn2_g = jnp.ones((C_OUT,), jnp.float32)
        bn2_b = jnp.zeros((C_OUT,), jnp.float32)
        bn2_m = jnp.zeros((C_OUT,), jnp.float32)
        bn2_v = jnp.ones((C_OUT,), jnp.float32)
        return dict(x=x, dw_w=dw_w, dw_b=dw_b, bn1_g=bn1_g, bn1_b=bn1_b, bn1_m=bn1_m, bn1_v=bn1_v, pw_w=pw_w, pw_b=pw_b, bn2_g=bn2_g, bn2_b=bn2_b, bn2_m=bn2_m, bn2_v=bn2_v)
    _L1_conv_all = _L1_conv_setup()
    _L1_conv_in = {k: v for k, v in _L1_conv_all.items() if k in ('dw_w', 'dw_b', 'bn1_g', 'bn1_b', 'bn1_m', 'bn1_v', 'pw_w', 'pw_b', 'bn2_g', 'bn2_b', 'bn2_m', 'bn2_v')}
    del _L1_conv_all

    def _L2_attn_setup():
        import jax, jax.numpy as jnp
        import numpy as np
        B, S, D_IN, D_OUT = (4, 1024, 128, 128)
        key = jax.random.key(seed)
        k1, k2, k3, k4 = jax.random.split(key, 4)
        sc = 1.0 / np.sqrt(D_IN)
        return {'x': jax.random.normal(k1, (B, S, D_IN), dtype=jnp.float32), 'Wq': jax.random.normal(k2, (D_OUT, D_IN), dtype=jnp.float32) * sc, 'Wk': jax.random.normal(k3, (D_OUT, D_IN), dtype=jnp.float32) * sc, 'Wv': jax.random.normal(k4, (D_OUT, D_IN), dtype=jnp.float32) * sc}
    _L2_attn_all = _L2_attn_setup()
    _L2_attn_in = {k: v for k, v in _L2_attn_all.items() if k in ('Wq', 'Wk', 'Wv')}
    del _L2_attn_all

    def _L2_ffn_setup():
        import jax, jax.numpy as jnp
        import numpy as np
        B, S, H, E, F, TOP_K = (4, 512, 128, 16, 256, 2)

        def _moe_forward(inputs, router_w, gate_w, up_w, down_w):
            b, s, h = inputs.shape
            x = inputs.reshape(-1, h)
            T = x.shape[0]
            router_logits = x @ router_w.T
            top_vals, top_idx = jax.lax.top_k(router_logits, TOP_K)
            weights = jax.nn.softmax(top_vals.astype(jnp.float32), axis=-1)
            combine = jnp.zeros((T, router_w.shape[0]), jnp.float32)
            combine = combine.at[jnp.arange(T)[:, None], top_idx].set(weights)

            def step(acc, ew):
                wg, wu, wd, ce = ew
                hid = jax.nn.silu(x @ wg) * (x @ wu)
                y = hid @ wd
                return (acc + ce[:, None] * y, None)
            out0 = jnp.zeros_like(x)
            out, _ = jax.lax.scan(step, out0, (gate_w, up_w, down_w, combine.T))
            return (out.reshape(b, s, h), router_logits, top_idx)
        key = jax.random.key(seed)
        k0, k1, k2, k3, k4 = jax.random.split(key, 5)
        scale = 0.02
        return {'inputs': jax.random.normal(k0, (B, S, H), dtype=jnp.float32), 'router_w': jax.random.normal(k1, (E, H), dtype=jnp.float32) * scale, 'gate_w': jax.random.normal(k2, (E, H, F), dtype=jnp.float32) * scale, 'up_w': jax.random.normal(k3, (E, H, F), dtype=jnp.float32) * scale, 'down_w': jax.random.normal(k4, (E, F, H), dtype=jnp.float32) * scale}
    _L2_ffn_all = _L2_ffn_setup()
    _L2_ffn_in = {k: v for k, v in _L2_ffn_all.items() if k in ('router_w', 'gate_w', 'up_w', 'down_w')}
    del _L2_ffn_all

    def _L3_attn_setup():
        import jax, jax.numpy as jnp
        import numpy as np
        TAU = 0.1
        N_HEADS = 8

        def rosa_scan(x):
            N, T, _ = x.shape
            n = jnp.arange(T)
            rows = n[:, None] + n[None, :]
            valid = rows < T
            rows_c = jnp.where(valid, rows, 0)
            cols = jnp.broadcast_to(n[:, None], (T, T))
            S = x[:, rows_c, cols]
            g = jnp.where(valid[None], S, 1.0)
            a = jnp.where(valid[None], S, 0.0)

            def comb(c1, c2):
                g0, a0 = c1
                g1, a1 = c2
                return (g1 * g0, g1 * a0 + a1)
            _, A = jax.lax.associative_scan(comb, (g, a), axis=1)
            d = n[:, None] - n[None, :]
            low = d >= 0
            dc = jnp.where(low, d, 0)
            colmat = jnp.broadcast_to(n[None, :], (T, T))
            return jnp.where(low[None], A[:, colmat, dc], 0.0)

        def rosa_attn_score(x, tau):
            T = x.shape[-1]
            r = jnp.arange(T, dtype=x.dtype)
            p = r[None, :] / (r[:, None] + 1.0)
            x = x + p
            mask = jnp.arange(T)[:, None] < jnp.arange(T)[None, :]
            x = jnp.where(mask, -jnp.inf, x)
            return jax.nn.softmax(x / tau, axis=-1)
        key = jax.random.key(seed)
        ks = jax.random.split(key, 5)
        B, T, D, Hd = (2, 256, 128, 16)
        x = jax.random.normal(ks[0], (B, T, D), dtype=jnp.float32)
        wq = jax.random.normal(ks[1], (D, D), dtype=jnp.float32) * 0.05
        wk = jax.random.normal(ks[2], (D, D), dtype=jnp.float32) * 0.05
        wv = jax.random.normal(ks[3], (D, D), dtype=jnp.float32) * 0.05
        wo = jax.random.normal(ks[4], (D, Hd), dtype=jnp.float32) * 0.05
        return {'x': x, 'wq': wq, 'wk': wk, 'wv': wv, 'wo': wo}
    _L3_attn_all = _L3_attn_setup()
    _L3_attn_in = {k: v for k, v in _L3_attn_all.items() if k in ('wq', 'wk', 'wv', 'wo')}
    del _L3_attn_all

    def _L3_ffn_setup():
        import jax, jax.numpy as jnp
        import numpy as np
        EPS = 1e-06
        SINKHORN_ITERS = 8
        TEMPERATURE = 1.0
        B, N, D = (4, 2048, 128)
        E, OUT = (8, 128)
        H = 1

        def _sinkhorn(logits):
            t = jnp.log(jnp.clip(logits, EPS)) / TEMPERATURE
            for _ in range(SINKHORN_ITERS):
                t = t - jax.nn.logsumexp(t, axis=-2, keepdims=True)
                t = t - jax.nn.logsumexp(t, axis=-1, keepdims=True)
            return jnp.exp(t)
        key = jax.random.key(seed)
        k1, k2, k3 = jax.random.split(key, 3)
        x = jax.random.normal(k1, (B, N, D), dtype=jnp.float32)
        gate_weight = jax.random.normal(k2, (H, D, E), dtype=jnp.float32)
        experts = jax.random.normal(k3, (E, D, OUT), dtype=jnp.float32) * 0.02
        return {'x': x, 'gate_weight': gate_weight, 'experts': experts}
    _L3_ffn_all = _L3_ffn_setup()
    _L3_ffn_in = {k: v for k, v in _L3_ffn_all.items() if k in ('gate_weight', 'experts')}
    del _L3_ffn_all
    return {'x': x, 'L0_conv_norm_w': _L0_conv_in['norm_w'], 'L0_conv_norm_b': _L0_conv_in['norm_b'], 'L0_conv_qkv_w': _L0_conv_in['qkv_w'], 'L0_conv_qkv_b': _L0_conv_in['qkv_b'], 'L0_conv_proj_w': _L0_conv_in['proj_w'], 'L0_conv_proj_b': _L0_conv_in['proj_b'], 'L1_conv_dw_w': _L1_conv_in['dw_w'], 'L1_conv_dw_b': _L1_conv_in['dw_b'], 'L1_conv_bn1_g': _L1_conv_in['bn1_g'], 'L1_conv_bn1_b': _L1_conv_in['bn1_b'], 'L1_conv_bn1_m': _L1_conv_in['bn1_m'], 'L1_conv_bn1_v': _L1_conv_in['bn1_v'], 'L1_conv_pw_w': _L1_conv_in['pw_w'], 'L1_conv_pw_b': _L1_conv_in['pw_b'], 'L1_conv_bn2_g': _L1_conv_in['bn2_g'], 'L1_conv_bn2_b': _L1_conv_in['bn2_b'], 'L1_conv_bn2_m': _L1_conv_in['bn2_m'], 'L1_conv_bn2_v': _L1_conv_in['bn2_v'], 'L2_attn_Wq': _L2_attn_in['Wq'], 'L2_attn_Wk': _L2_attn_in['Wk'], 'L2_attn_Wv': _L2_attn_in['Wv'], 'L2_ffn_router_w': _L2_ffn_in['router_w'], 'L2_ffn_gate_w': _L2_ffn_in['gate_w'], 'L2_ffn_up_w': _L2_ffn_in['up_w'], 'L2_ffn_down_w': _L2_ffn_in['down_w'], 'L3_attn_wq': _L3_attn_in['wq'], 'L3_attn_wk': _L3_attn_in['wk'], 'L3_attn_wv': _L3_attn_in['wv'], 'L3_attn_wo': _L3_attn_in['wo'], 'L3_ffn_gate_weight': _L3_ffn_in['gate_weight'], 'L3_ffn_experts': _L3_ffn_in['experts']}

def reference(x, L0_conv_norm_w, L0_conv_norm_b, L0_conv_qkv_w, L0_conv_qkv_b, L0_conv_proj_w, L0_conv_proj_b, L1_conv_dw_w, L1_conv_dw_b, L1_conv_bn1_g, L1_conv_bn1_b, L1_conv_bn1_m, L1_conv_bn1_v, L1_conv_pw_w, L1_conv_pw_b, L1_conv_bn2_g, L1_conv_bn2_b, L1_conv_bn2_m, L1_conv_bn2_v, L2_attn_Wq, L2_attn_Wk, L2_attn_Wv, L2_ffn_router_w, L2_ffn_gate_w, L2_ffn_up_w, L2_ffn_down_w, L3_attn_wq, L3_attn_wk, L3_attn_wv, L3_attn_wo, L3_ffn_gate_weight, L3_ffn_experts):
    import jax
    import jax.numpy as jnp

    def _L0_conv_ref(x, norm_w, norm_b, qkv_w, qkv_b, proj_w, proj_b):
        import jax, jax.numpy as jnp
        import numpy as np
        CH = 128
        HEADS = 8
        GROUPS = 32
        EPS = 1e-05
        b, c, H, W = x.shape
        L = H * W
        xf = x.reshape(b, c, L)
        xg = xf.astype(jnp.float32).reshape(b, GROUPS, c // GROUPS, L)
        mean = xg.mean(axis=(2, 3), keepdims=True)
        var = xg.var(axis=(2, 3), keepdims=True)
        xn = ((xg - mean) * jax.lax.rsqrt(var + EPS)).reshape(b, c, L)
        xn = (xn * norm_w[:, None] + norm_b[:, None]).astype(x.dtype)
        qkv = jnp.einsum('oc,bcl->bol', qkv_w, xn) + qkv_b[:, None]
        ch = c // HEADS
        qkv = qkv.reshape(b * HEADS, 3 * ch, L)
        q, k, v = jnp.split(qkv, 3, axis=1)
        scale = ch ** (-0.25)
        w = jnp.einsum('bct,bcs->bts', q * scale, k * scale)
        w = jax.nn.softmax(w.astype(jnp.float32), axis=-1).astype(w.dtype)
        a = jnp.einsum('bts,bcs->bct', w, v).reshape(b, c, L)
        h = jnp.einsum('oc,bcl->bol', proj_w, a) + proj_b[:, None]
        return (xf + h).reshape(b, c, H, W)

    def _L1_conv_ref(x, dw_w, dw_b, bn1_g, bn1_b, bn1_m, bn1_v, pw_w, pw_b, bn2_g, bn2_b, bn2_m, bn2_v):
        import jax, jax.numpy as jnp
        import numpy as np
        from jax import lax
        EPS = 1e-05
        DW_THRESH = 4.0
        PW_THRESH = 0.001
        C_IN = 128
        C_OUT = 128

        def _bn(x, g, b, m, v):
            inv = g * lax.rsqrt(v + EPS)
            return x * inv[None, :, None, None] + (b - m * inv)[None, :, None, None]

        def _prune(x, thresh):
            amax = jnp.max(jnp.abs(x), axis=(2, 3), keepdims=True)
            return jnp.where(amax < thresh, jnp.zeros_like(x), x)
        dn = ('NCHW', 'OIHW', 'NCHW')
        h = lax.conv_general_dilated(x, dw_w, window_strides=(1, 1), padding=((1, 1), (1, 1)), feature_group_count=C_IN, dimension_numbers=dn)
        h = h + dw_b[None, :, None, None]
        h = jax.nn.relu(_bn(h, bn1_g, bn1_b, bn1_m, bn1_v))
        h = _prune(h, DW_THRESH)
        h = lax.conv_general_dilated(h, pw_w, window_strides=(1, 1), padding=((0, 0), (0, 0)), dimension_numbers=dn)
        h = h + pw_b[None, :, None, None]
        h = jax.nn.relu(_bn(h, bn2_g, bn2_b, bn2_m, bn2_v))
        h = _prune(h, PW_THRESH)
        return h

    def _L2_attn_ref(x, Wq, Wk, Wv):
        import jax, jax.numpy as jnp
        import numpy as np
        B, S, D_IN, D_OUT = (4, 1024, 128, 128)
        q = jnp.einsum('bsd,ed->bse', x, Wq)
        k = jnp.einsum('bsd,ed->bse', x, Wk)
        v = jnp.einsum('bsd,ed->bse', x, Wv)
        scale = 1.0 / jnp.sqrt(jnp.asarray(k.shape[-1], dtype=x.dtype))
        scores = jnp.einsum('bqe,bke->bqk', q, k) * scale
        s = x.shape[1]
        causal = jnp.tril(jnp.ones((s, s), dtype=bool))
        scores = jnp.where(causal[None, :, :], scores, -jnp.inf)
        attn = jax.nn.softmax(scores, axis=-1)
        return jnp.einsum('bqk,bke->bqe', attn, v)

    def _L2_ffn_ref(inputs, router_w, gate_w, up_w, down_w):
        import jax, jax.numpy as jnp
        import numpy as np
        B, S, H, E, F, TOP_K = (4, 512, 128, 16, 256, 2)

        def _moe_forward(inputs, router_w, gate_w, up_w, down_w):
            b, s, h = inputs.shape
            x = inputs.reshape(-1, h)
            T = x.shape[0]
            router_logits = x @ router_w.T
            top_vals, top_idx = jax.lax.top_k(router_logits, TOP_K)
            weights = jax.nn.softmax(top_vals.astype(jnp.float32), axis=-1)
            combine = jnp.zeros((T, router_w.shape[0]), jnp.float32)
            combine = combine.at[jnp.arange(T)[:, None], top_idx].set(weights)

            def step(acc, ew):
                wg, wu, wd, ce = ew
                hid = jax.nn.silu(x @ wg) * (x @ wu)
                y = hid @ wd
                return (acc + ce[:, None] * y, None)
            out0 = jnp.zeros_like(x)
            out, _ = jax.lax.scan(step, out0, (gate_w, up_w, down_w, combine.T))
            return (out.reshape(b, s, h), router_logits, top_idx)
        out, router_logits, selected_experts = _moe_forward(inputs, router_w, gate_w, up_w, down_w)
        return out

    def _L3_attn_ref(x, wq, wk, wv, wo):
        import jax, jax.numpy as jnp
        import numpy as np
        TAU = 0.1
        N_HEADS = 8

        def rosa_scan(x):
            N, T, _ = x.shape
            n = jnp.arange(T)
            rows = n[:, None] + n[None, :]
            valid = rows < T
            rows_c = jnp.where(valid, rows, 0)
            cols = jnp.broadcast_to(n[:, None], (T, T))
            S = x[:, rows_c, cols]
            g = jnp.where(valid[None], S, 1.0)
            a = jnp.where(valid[None], S, 0.0)

            def comb(c1, c2):
                g0, a0 = c1
                g1, a1 = c2
                return (g1 * g0, g1 * a0 + a1)
            _, A = jax.lax.associative_scan(comb, (g, a), axis=1)
            d = n[:, None] - n[None, :]
            low = d >= 0
            dc = jnp.where(low, d, 0)
            colmat = jnp.broadcast_to(n[None, :], (T, T))
            return jnp.where(low[None], A[:, colmat, dc], 0.0)

        def rosa_attn_score(x, tau):
            T = x.shape[-1]
            r = jnp.arange(T, dtype=x.dtype)
            p = r[None, :] / (r[:, None] + 1.0)
            x = x + p
            mask = jnp.arange(T)[:, None] < jnp.arange(T)[None, :]
            x = jnp.where(mask, -jnp.inf, x)
            return jax.nn.softmax(x / tau, axis=-1)
        B, T, D = x.shape
        H = N_HEADS
        Hd = D // H
        tau = TAU
        iq = jax.nn.softmax((x @ wq).reshape(B, T, H, Hd) / tau, axis=-1)
        ik = jax.nn.softmax((x @ wk).reshape(B, T, H, Hd) / tau, axis=-1)
        iv = jax.nn.softmax((x @ wv).reshape(B, T, H, Hd) / tau, axis=-1)
        a = jnp.einsum('bthd,bshd->bhts', iq, ik)
        a = rosa_scan(a.reshape(B * H, T, T)).reshape(B, H, T, T)
        a = rosa_attn_score(a, tau)
        o = jnp.einsum('bhts,bshd->bhtd', a, iv)
        xv = wo.reshape(H, Hd, Hd)
        o = jnp.einsum('bhtd,hde->bhte', o, xv)
        return o.transpose(0, 2, 1, 3).reshape(B, T, D)

    def _L3_ffn_ref(x, gate_weight, experts):
        import jax, jax.numpy as jnp
        import numpy as np
        EPS = 1e-06
        SINKHORN_ITERS = 8
        TEMPERATURE = 1.0
        B, N, D = (4, 2048, 128)
        E, OUT = (8, 128)
        H = 1

        def _sinkhorn(logits):
            t = jnp.log(jnp.clip(logits, EPS)) / TEMPERATURE
            for _ in range(SINKHORN_ITERS):
                t = t - jax.nn.logsumexp(t, axis=-2, keepdims=True)
                t = t - jax.nn.logsumexp(t, axis=-1, keepdims=True)
            return jnp.exp(t)
        b, n, d = x.shape
        e = experts.shape[0]
        m = n // e
        xh = x[:, None, :, :]
        gate_logits = jnp.einsum('bhnd,hde->bhne', xh, gate_weight)
        gates = _sinkhorn(gate_logits)
        g_t = jnp.swapaxes(gates, -1, -2)
        vals, idx = jax.lax.top_k(g_t, m)
        gate_values = jnp.transpose(vals, (2, 0, 1, 3))[..., None]
        routed = jnp.take_along_axis(xh[:, :, None, :, :], idx[..., None], axis=3)
        routed = jnp.transpose(routed, (2, 0, 1, 3, 4))
        expert_w = experts[:, None, :, :]
        outputs = jnp.einsum('ebhmi,ehio->ebhmo', routed, expert_w)
        outputs = outputs * gate_values
        bh_idx = idx.reshape(b, 1, e * m)
        bh_vals = jnp.transpose(outputs, (1, 2, 0, 3, 4)).reshape(b, 1, e * m, outputs.shape[-1])

        def scat(i1, v1):
            return jnp.zeros((n, v1.shape[-1]), dtype=v1.dtype).at[i1].set(v1)
        routed_back = jax.vmap(jax.vmap(scat))(bh_idx, bh_vals)
        return routed_back[:, 0]

    def _gn(v, G=32, eps=1e-05):
        B_, C_, H_, W_ = v.shape
        g = v.reshape(B_, G, C_ // G, H_, W_)
        m = jnp.mean(g, axis=(2, 3, 4), keepdims=True)
        s = jnp.var(g, axis=(2, 3, 4), keepdims=True)
        return ((g - m) / jnp.sqrt(s + eps)).reshape(v.shape)

    def _ln_c(v, eps=1e-06):
        m = jnp.mean(v, axis=1, keepdims=True)
        s = jnp.var(v, axis=1, keepdims=True)
        return (v - m) / jnp.sqrt(s + eps)

    def _ln_t(v, eps=1e-05):
        m = jnp.mean(v, axis=-1, keepdims=True)
        s = jnp.var(v, axis=-1, keepdims=True)
        return (v - m) / jnp.sqrt(s + eps)

    def _to_tokens(v):
        B_, C_, H_, W_ = v.shape
        return v.reshape(B_, C_, H_ * W_).transpose(0, 2, 1)

    def _from_tokens(t, like):
        B_, C_, H_, W_ = like.shape
        return t.transpose(0, 2, 1).reshape(B_, C_, H_, W_)
    x = _L0_conv_ref(x, L0_conv_norm_w, L0_conv_norm_b, L0_conv_qkv_w, L0_conv_qkv_b, L0_conv_proj_w, L0_conv_proj_b)
    x = x + _L1_conv_ref(_gn(x), L1_conv_dw_w, L1_conv_dw_b, L1_conv_bn1_g, L1_conv_bn1_b, L1_conv_bn1_m, L1_conv_bn1_v, L1_conv_pw_w, L1_conv_pw_b, L1_conv_bn2_g, L1_conv_bn2_b, L1_conv_bn2_m, L1_conv_bn2_v)
    t = _to_tokens(x)
    t = t + _L2_attn_ref(_ln_t(t), L2_attn_Wq, L2_attn_Wk, L2_attn_Wv)
    t = t + _L2_ffn_ref(_ln_t(t), L2_ffn_router_w, L2_ffn_gate_w, L2_ffn_up_w, L2_ffn_down_w)
    t = t + _L3_attn_ref(_ln_t(t), L3_attn_wq, L3_attn_wk, L3_attn_wv, L3_attn_wo)
    t = t + _L3_ffn_ref(_ln_t(t), L3_ffn_gate_weight, L3_ffn_experts)
    x = _from_tokens(t, x)
    return x

_drawn_inputs = setup_inputs


def setup_inputs(seed=0):
    import zlib

    import numpy as np

    out = dict(_drawn_inputs(seed))
    spreads = {'L0_conv_norm_w': (1.0, 0.6),
     'L0_conv_norm_b': (0.0, 0.1),
     'L0_conv_qkv_b': (0.0, 0.1),
     'L0_conv_proj_b': (0.0, 0.1),
     'L1_conv_bn1_g': (1.0, 0.2),
     'L1_conv_bn1_b': (0.0, 0.1),
     'L1_conv_bn1_m': (0.0, 0.1),
     'L1_conv_bn1_v': (1.0, 0.2),
     'L1_conv_bn2_g': (1.0, 0.6),
     'L1_conv_bn2_b': (0.0, 0.1),
     'L1_conv_bn2_m': (0.0, 0.1),
     'L1_conv_bn2_v': (1.0, 0.6)}
    factors = {'L2_ffn_router_w': 5.695,
     'L2_ffn_gate_w': 5.808,
     'L2_ffn_up_w': 6.044,
     'L2_ffn_down_w': 6.118,
     'L3_attn_wq': 4.027,
     'L3_attn_wk': 3.971,
     'L3_attn_wv': 3.858,
     'L3_attn_wo': 3.614}
    for name, (base, spread) in spreads.items():
        noise = np.random.default_rng([zlib.crc32(name.encode()), seed]).standard_normal(out[name].shape)
        drawn = base * np.exp(spread * noise) if base else spread * noise
        out[name] = jnp.asarray(drawn.astype(out[name].dtype))
    for name, factor in factors.items():
        out[name] = (out[name] * factor).astype(out[name].dtype)
    return out
```

```python
from contextlib import ExitStack

import numpy as np

import concourse.bass as bass
from concourse import mybir

F32 = mybir.dt.float32
BF16 = mybir.dt.bfloat16
U32 = mybir.dt.uint32
ALU = mybir.AluOpType
ACT = mybir.ActivationFunctionType
AX_X = mybir.AxisListType.X

B, C, T = 8, 128, 1024
N = B * T
P = 128
HEADS, HD = 8, 16
NT = T // P
HALF = 512
EPS5, EPS6 = 1e-5, 1e-6

VECS = ["norm_w", "norm_b", "q_b", "k_b", "v_b", "proj_b"] + [f"dw{i}" for i in range(9)] + [
    "dw_b", "bn1_g", "bn1_b", "bn1_m", "bn1_v", "pw_b", "bn2_g", "bn2_b", "bn2_m", "bn2_v", "eps5"]
VI = {n: i for i, n in enumerate(VECS)}
MATS = ["ident", "gavg", "num0", "num1", "den0", "den1", "qT", "kT", "vT", "projT", "pwT",
        "Wq", "Wk", "WvT"]
MI = {n: i for i, n in enumerate(MATS)}

Q_PARTS = [0, 0, 1, 1, 0, 2]
K_PARTS = [0, 1, 0, 1, 2, 0]
NPROD = len(Q_PARTS)
KROWS = NPROD * HD
MROWS = 2
XPAD = 16


def group_norm(nc, t, tag, affine, loads=()):
    with ExitStack() as ctx:
        def sb(name, shape, dt=F32):
            return ctx.enter_context(nc.sbuf_tensor(tag + name, shape, dt))

        def sem(name):
            return ctx.enter_context(nc.semaphore(tag + name))

        stats = sb("g_stats", [P, B, 2, 6])
        mv = sb("g_mv", [P, B, 2])
        dev = sb("g_dev", [P, B])
        work = sb("g_work", [P, B])
        ps = ctx.enter_context(nc.psum_tensor(tag + "g_ps", [P, HALF], F32))
        x_in, w_in = [sem(f"g_x{b}") for b in range(B)], sem("g_w")
        chain, avg = sem("g_chain"), sem("g_avg")
        ready, root = sem("g_ready"), sem("g_root")
        with nc.Block() as block:
            @block.sync
            def _(sp):
                for dst, src in loads[:-B]:
                    sp.dma_start(dst, src).then_inc(w_in, 16)
                for b, (dst, src) in enumerate(loads[-B:]):
                    sp.dma_start(dst, src).then_inc(x_in[b], 16)

            @block.vector
            def _(dve):
                for b in range(B):
                    if loads:
                        dve.wait_ge(x_in[b], 16)
                    for h in range(2):
                        c0 = b * T + h * HALF
                        dve.bn_stats(stats[:, b, h, :], t.resid[:, c0:c0 + HALF]).then_inc(chain, 1)
                dve.wait_ge(chain, 2 * B)
                for b in range(B):
                    dve.bn_aggr(mv[:, b, :], stats[:, b, :, :]).then_inc(chain, 1)
                dve.wait_ge(chain, 3 * B)
                if loads:
                    dve.wait_ge(w_in, 16 * (len(loads) - B))
                dve.tensor_copy(work[:, :], mv[:, :, 0]).then_inc(ready, 1)
                dve.wait_ge(avg, 1)
                dve.tensor_tensor(dev[:, :], mv[:, :, 0], ps[:, 0:B], ALU.subtract).then_inc(chain, 1)
                dve.tensor_copy(t.gshift[:, :], ps[:, 0:B]).then_inc(chain, 1)
                dve.wait_ge(chain, 3 * B + 2)
                dve.tensor_tensor(dev[:, :], dev[:, :], dev[:, :], ALU.mult).then_inc(chain, 1)
                dve.wait_ge(chain, 3 * B + 3)
                dve.tensor_tensor(work[:, :], dev[:, :], mv[:, :, 1], ALU.add).then_inc(ready, 1)
                dve.wait_ge(avg, 2)
                dve.tensor_scalar(work[:, :], ps[:, B:2 * B], EPS5, None, ALU.add).then_inc(ready, 1)
                dve.wait_ge(root, 1)
                dve.reciprocal(dev[:, :], work[:, :]).then_inc(ready, 1)
                dve.wait_ge(ready, 4)
                dve.tensor_scalar(t.gscale[:, :], dev[:, :], t.vec(affine[0]) if affine else 1.0, None, ALU.mult
                                  ).then_inc(chain, 1)
                dve.wait_ge(chain, 3 * B + 4)
                dve.tensor_tensor(work[:, :], t.gshift[:, :], t.gscale[:, :], ALU.mult).then_inc(chain, 1)
                dve.wait_ge(chain, 3 * B + 5)
                dve.tensor_scalar(t.gshift[:, :], work[:, :], -1.0, t.vec(affine[1]) if affine else 0.0,
                                  ALU.mult, ALU.add).then_inc(chain, 1)
                dve.tensor_tensor(t.projb[:, :], ps[:, 2 * B:2 * B + 1], t.vec("proj_b"), ALU.add)

            @block.scalar
            def _(act):
                act.wait_ge(ready, 3)
                act.activation(work[:, :], work[:, :], ACT.Sqrt).then_inc(root, 1)

            @block.tensor
            def _(pe):
                if loads:
                    pe.wait_ge(w_in, 16 * (len(loads) - B))
                pe.matmul(ps[:, 2 * B:2 * B + 1], t.mat("projT"), t.vec("v_b"), start=True, stop=True)
                pe.wait_ge(ready, 1)
                pe.matmul(ps[:, 0:B], t.mat("gavg"), work[:, :], start=True, stop=True).then_inc(avg, 1)
                pe.wait_ge(ready, 2)
                pe.matmul(ps[:, B:2 * B], t.mat("gavg"), work[:, :], start=True, stop=True).then_inc(avg, 1)


def layer0_attention(nc, t, d_parts, d_max):
    with ExitStack() as ctx:
        def sb(name, shape, dt=F32):
            return ctx.enter_context(nc.sbuf_tensor(name, shape, dt))

        def sem(name):
            return ctx.enter_context(nc.semaphore("a_" + name))

        xnb = sb("xnb", [P, T])
        parts = sb("parts", [P, 2, 3, T], BF16)
        rest = sb("rest", [P, 2, T])
        qs = [sb(f"qs{i}", [KROWS + MROWS, HEADS, T], BF16) for i in range(2)]
        ks = [sb(f"ks{i}", [KROWS + MROWS, HEADS, T], BF16) for i in range(2)]
        vx = [sb(f"vx{i}", [P, NT, HEADS, 32]) for i in range(2)]
        half_max = sb("half_max", [P, HEADS * NT, 2])
        row_max = sb("row_max", [P, P])
        neg_max = sb("neg_max", [HEADS * NT, MROWS, P], BF16)
        E = sb("E", [P, 2, 4, 2 * HALF])
        acc_sb = sb("acc_sb", [P, 2, HALF])
        rden = sb("rden", [P, HALF])
        attn = sb("attn", [P, HALF])

        def psum(name, n):
            return ctx.enter_context(nc.psum_tensor(name, [P, n], F32))

        sc = [psum(f"sc{i}", 2 * HALF) for i in range(2)]
        acc = psum("acc", HALF)
        misc = psum("misc", HALF)
        bm = [psum(f"bm{i}", HALF) for i in range(2)]

        ones_set = sem("ones")
        xn_ready, mm_a, hi_done, rest_done, v_done, low_done = (
            sem("xn_ready"), sem("mm_a"), sem("hi_done"), sem("rest_done"), sem("v_done"), sem("low_done"))
        parts_out, stacked = sem("parts_out"), sem("stacked")
        mm_b, max_done, rowmax_done, maxT, negmax_hi, negmax_done = (
            sem("mm_b"), sem("max_done"), sem("rowmax_done"), sem("maxT"), sem("negmax_hi"), sem("negmax_done"))
        max_out, max_in = sem("max_out"), sem("max_in")
        mm_c, exp_done, av_done, acc_out, mm_n, norm_done = (
            sem("mm_c"), sem("exp_done"), sem("av_done"), sem("acc_out"), sem("mm_n"), sem("norm_done"))
        woke = sem("woke")
        PIECES = 4
        UB = HEADS * NT * 2
        UC = 64
        GC = 16
        QW = [t.mat("qT"), t.mat("kT")]

        with nc.Block() as block:
            def pe_a(pe, b, par, i):
                n = b * 6 + i
                if i == 0:
                    pe.wait_ge(xn_ready, b + 1)
                if i < PIECES:
                    if i >= 2:
                        pe.wait_ge(rest_done, b * PIECES + i - 1)
                    else:
                        pe.wait_ge(maxT, b + 1)
                        pe.wait_ge(negmax_done, b + 1)
                    pe.matmul(bm[i % 2][:, :], QW[i // 2], xnb[:, (i % 2) * HALF:(i % 2 + 1) * HALF],
                              start=True, stop=True).then_inc(mm_a, 1)
                else:
                    pe.wait_ge(rest_done, b * PIECES + i - 1)
                    for j in range(4):
                        tile = (i - PIECES) * 4 + j
                        mm = pe.matmul(bm[i % 2][:, j * P:(j + 1) * P], xnb[:, tile * P:(tile + 1) * P],
                                       t.mat("vT"), start=True, stop=True)
                    mm.then_inc(mm_a, 1)

            def pe_b(pe, b, par, u):
                if u == 0:
                    pe.wait_ge(stacked, 16 * 12 * (b + 1))
                if u < 2:
                    pe.wait_ge(v_done, 2 * b + 1 + u)
                else:
                    pe.wait_ge(max_done, b * UB + u - 1)
                h, tile, k = u // (2 * NT), u // 2 % NT, u % 2
                pe.matmul(bm[u % 2][:, :], qs[par][0:KROWS, h, tile * P:(tile + 1) * P],
                          ks[par][0:KROWS, h, k * HALF:(k + 1) * HALF], start=True, stop=True).then_inc(mm_b, 1)

            def pe_b_end(pe, b):
                pe.wait_ge(rowmax_done, b + 1)
                pe.transpose(bm[0][:, 0:P], row_max[:, :], t.mat("ident")).then_inc(maxT, 1)

            def pe_scores(pe, b, par, g):
                th, hg, sp = g // 8, g // 4 % 2, g % 4
                for h4 in range(4):
                    u = 4 * g + h4
                    pe.wait_ge(exp_done, b * UC + u + 1)
                    for j in range(2):
                        s0 = (2 * sp + j) * P
                        mm = pe.matmul(sc[u % 2][:, j * HALF:(j + 1) * HALF], ks[par][:, 4 * hg + h4, s0:s0 + P],
                                       qs[par][:, 4 * hg + h4, th * HALF:(th + 1) * HALF], start=True, stop=True)
                    mm.then_inc(mm_c, 1)

            def pe_av(pe, b, par, g):
                hg, sp = g // 4 % 2, g % 4
                pe.wait_ge(exp_done, b * UC + 4 * g + 4 + 2)
                if sp == 0:
                    pe.wait_ge(acc_out, b * 4 + g // 4 + 1)
                for j in range(2):
                    for h4 in range(4):
                        mm = pe.matmul(acc[32 * h4:32 * h4 + 32, :], vx[par][:, 2 * sp + j, 4 * hg + h4, :],
                                       E[:, g % 2, h4, j * HALF:(j + 1) * HALF],
                                       start=(sp == 0 and j == 0), stop=(sp == 3 and j == 1))
                mm.then_inc(av_done, 1)

            def pe_norm(pe, b, th, step):
                if step == 0:
                    pe.wait_ge(acc_out, b * 4 + 2 * th + 2 + 1)
                pe.wait_ge(norm_done, b * 6 + th * 3 + step + 1)
                if step < 2:
                    for hg in range(2):
                        mm = pe.matmul(misc[:, :], t.mat(f"{('den', 'num')[step]}{hg}"), acc_sb[:, hg, :],
                                       start=(hg == 0), stop=(hg == 1))
                else:
                    mm = pe.matmul(misc[:, :], t.mat("projT"), attn[:, :], start=True, stop=True)
                mm.then_inc(mm_n, 1)

            A_GROUPS = 6
            def b_units(g):
                n = GC - A_GROUPS
                return range(UB * (g - A_GROUPS) // n, UB * (g - A_GROUPS + 1) // n) if g >= A_GROUPS else range(0)

            def pe_iter(pe, b, par, more):
                for g in range(GC):
                    pe_scores(pe, b, par, g)
                    if more and g < A_GROUPS:
                        pe_a(pe, b + 1, 1 - par, g)
                    units = b_units(g) if more else range(0)
                    for u in units[:len(units) // 2]:
                        pe_b(pe, b + 1, 1 - par, u)
                    if g:
                        pe_av(pe, b, par, g - 1)
                    for u in units[len(units) // 2:]:
                        pe_b(pe, b + 1, 1 - par, u)
                    if g in (9, 10, 11):
                        pe_norm(pe, b, 0, g - 9)
                if more:
                    pe_b_end(pe, b + 1)
                pe_av(pe, b, par, GC - 1)
                for step in range(3):
                    pe_norm(pe, b, 1, step)

            def iterations(eng, body, first=None):
                with eng.Fori(0, B // 2 - 1) as pair:
                    body(eng, 2 * pair, 0, True)
                    body(eng, 2 * pair + 1, 1, True)
                body(eng, B - 2, 0, True)
                body(eng, B - 1, 1, False)

            @block.tensor
            def _(pe):
                for i in range(6):
                    pe_a(pe, 0, 0, i)
                for u in range(UB):
                    pe_b(pe, 0, 0, u)
                pe_b_end(pe, 0)
                pe.wait_ge(max_in, 16)
                iterations(pe, lambda e, b, par, more: (pe_iter(e, b, par, more),
                           e.wait_ge(max_in, 16 * (b + 2)) if more else None))

            def dve_xn(dve, b):
                dve.wait_ge(mm_a, b * 6 + 1)
                dve.tensor_scalar(xnb[:, :], t.resid[:, bass.ds(b * T, T)], t.gscale[:, bass.ds(b, 1)],
                                  t.gshift[:, bass.ds(b, 1)], ALU.mult, ALU.add).then_inc(xn_ready, 1)

            def dve_a(dve, b, par, i):
                if i < PIECES:
                    w, h = i // 2, i % 2
                    dve.wait_ge(hi_done, b * PIECES + i + 1)
                    dve.wait_ge(parts_out, 16 * (b + 1))
                    dve.scalar_tensor_tensor(rest[:, w, h * HALF:(h + 1) * HALF], bm[i % 2][:, :],
                                             t.vec(("q_b", "k_b")[w]), parts[:, w, 0, h * HALF:(h + 1) * HALF],
                                             ALU.add, ALU.subtract).then_inc(rest_done, 1)
                else:
                    j = i - PIECES
                    dve.wait_ge(mm_a, b * 6 + i + 1 + 1)
                    dve.tensor_copy(vx[par][:, 4 * j:4 * j + 4, :, 0:HD],
                                    bm[i % 2][:, :].rearrange("p (t h d) -> p t h d", t=4, h=HEADS)
                                    ).then_inc(v_done, 1)

            def dve_b(dve, b, u):
                dve.wait_ge(mm_b, b * UB + u + 1)
                dve.tensor_reduce(half_max[:, u // 2, u % 2:u % 2 + 1], bm[u % 2][:, :], AX_X, ALU.max
                                  ).then_inc(max_done, 1)

            def dve_b_end(dve, b):
                dve.wait_ge(max_done, b * UB + UB)
                dve.wait_ge(maxT, b + 1)
                dve.tensor_tensor(row_max[:, 0:HEADS * NT], half_max[:, :, 0], half_max[:, :, 1], ALU.max
                                  ).then_inc(rowmax_done, 1)

            def dve_b_low(dve, b):
                dve.wait_ge(negmax_hi, b + 1)
                dve.scalar_tensor_tensor(neg_max[:, 1, :], bm[0][0:HEADS * NT, 0:P], -1.0, neg_max[:, 0, :],
                                         ALU.mult, ALU.subtract).then_inc(negmax_done, 1)

            def dve_acc(dve, b, q):
                dve.wait_ge(av_done, b * GC + 4 * q + 4 + 2)
                if q % 2 == 0:
                    dve.wait_ge(norm_done, b * 6 + (q // 2) * 3 + 1)
                dve.tensor_copy(acc_sb[:, q % 2, :], acc[:, :]).then_inc(acc_out, 1)

            def dve_norm(dve, b, th, step):
                n = b * 6 + th * 3 + step
                dve.wait_ge(mm_n, n + 1)
                if step == 0:
                    dve.reciprocal(rden[:, :], misc[:, :]).then_inc(norm_done, 1)
                elif step == 1:
                    dve.wait_ge(norm_done, n + 1)
                    dve.tensor_tensor(attn[:, :], misc[:, :], rden[:, :], ALU.mult).then_inc(norm_done, 1)
                else:
                    r = t.resid[:, bass.ds(b * T + th * HALF, HALF)]
                    dve.scalar_tensor_tensor(r, misc[:, :], t.projb[:, 0:1], r, ALU.add, ALU.add
                                             ).then_inc(norm_done, 1)

            def dve_iter(dve, b, par, more):
                for g in range(GC):
                    if more:
                        if g == 0:
                            dve_xn(dve, b + 1)
                        if g < A_GROUPS:
                            dve_a(dve, b + 1, 1 - par, g)
                    units = b_units(g) if more else range(0)
                    for u in units[:len(units) // 2]:
                        dve_b(dve, b + 1, u)
                    if g in (4, 8, 12):
                        dve_acc(dve, b, g // 4 - 1)
                    for u in units[len(units) // 2:]:
                        dve_b(dve, b + 1, u)
                    if g in (9, 10, 11):
                        dve_norm(dve, b, 0, g - 9)
                if more:
                    dve_b_end(dve, b + 1)
                    dve_b_low(dve, b + 1)
                dve_acc(dve, b, 3)
                for step in range(3):
                    dve_norm(dve, b, 1, step)

            @block.vector
            def _(dve):
                for i in range(2):
                    dve.memset(vx[i][:, :, :, :], 0.0).then_inc(ones_set, 1)
                    dve.memset(ks[i][KROWS:KROWS + MROWS, :, :], 1.0).then_inc(ones_set, 1)
                dve.memset(row_max[:, :], 0.0).then_inc(ones_set, 1)
                dve.wait_ge(ones_set, 5)
                for i in range(2):
                    dve.memset(vx[i][:, :, :, HD:HD + 1], 1.0).then_inc(ones_set, 1)
                dve.wait_ge(ones_set, 7)
                dve.sem_inc(mm_a, 1)
                dve.sem_inc(exp_done, 2)
                dve.sem_inc(av_done, 2)
                dve.sem_inc(acc_out, 1)
                dve.sem_inc(norm_done, 1)
                dve.sem_inc(maxT, 1)
                dve.sem_inc(negmax_done, 1)
                dve.sem_inc(parts_out, 16)
                dve_xn(dve, 0)
                for i in range(6):
                    dve_a(dve, 0, 0, i)
                for u in range(UB):
                    dve_b(dve, 0, u)
                dve_b_end(dve, 0)
                dve_b_low(dve, 0)
                iterations(dve, dve_iter)

            def act_a(act, b, i):
                if i < PIECES:
                    w, h = i // 2, i % 2
                    act.wait_ge(mm_a, b * 6 + i + 1 + 1)
                    act.wait_ge(parts_out, 16 * (b + 1))
                    act.activation(parts[:, w, 0, h * HALF:(h + 1) * HALF], bm[i % 2][:, :], ACT.Identity,
                                   bias=t.vec(("q_b", "k_b")[w])).then_inc(hi_done, 1)

            def act_b_hi(act, b):
                act.wait_ge(maxT, b + 1 + 1)
                act.wait_ge(max_out, 16 * b + 16)
                act.activation(neg_max[:, 0, :], bm[0][0:HEADS * NT, 0:P], ACT.Copy, scale=-1.0
                               ).then_inc(negmax_hi, 1)

            def act_exp(act, b, g):
                act.wait_ge(av_done, b * GC + g + 1)
                for h4 in range(4):
                    u = 4 * g + h4
                    act.wait_ge(mm_c, b * UC + u + 1)
                    act.activation(E[:, g % 2, h4, :], sc[u % 2][:, :], ACT.Exp, scale=0.25).then_inc(exp_done, 1)

            def act_iter(act, b, par, more):
                for g in range(GC):
                    act_exp(act, b, g)
                    if more and g < A_GROUPS:
                        act_a(act, b + 1, g)
                if more:
                    act_b_hi(act, b + 1)

            @block.scalar
            def _(act):
                for i in range(6):
                    act_a(act, 0, i)
                act.sem_inc(max_out, 16)
                act_b_hi(act, 0)
                iterations(act, act_iter)

            def pool_a(pool, b):
                for w in range(2):
                    pool.wait_ge(rest_done, b * PIECES + 2 * w + 2)
                    pool.sem_inc(woke, 1)
                    pool.tensor_copy(parts[:, w, 1, :], rest[:, w, :]).then_inc(low_done, 1)
                    pool.wait_ge(low_done, b * 4 + 2 * w + 1)
                    pool.tensor_tensor(parts[:, w, 2, :], rest[:, w, :], parts[:, w, 1, :], ALU.subtract
                                       ).then_inc(low_done, 1)

            @block.gpsimd
            def _(pool):
                pool_a(pool, 0)
                with pool.Fori(1, B) as b:
                    pool_a(pool, b)

            def sp_ab(sp, b, par):
                sp.wait_ge(low_done, b * 4 + 4)
                sp.dma_start(d_parts.rearrange("w s p t -> p w s t"), parts[:, :, :, :]).then_inc(parts_out, 16)
                sp.wait_ge(parts_out, 16 * (b + 2))
                for dst, w, which in ((qs[par], 0, Q_PARTS), (ks[par], 1, K_PARTS)):
                    for i, s in enumerate(which):
                        sp.dma_start(dst[i * HD:(i + 1) * HD, :, :],
                                     d_parts[w, s].rearrange("(h d) t -> d h t", d=HD)).then_inc(stacked, 16)
                sp.wait_ge(negmax_done, b + 1 + 1)
                sp.dma_start(d_max.rearrange("r (u p) -> u r p", p=P), neg_max[:, :, :]).then_inc(max_out, 16)
                sp.wait_ge(max_out, 16 * (b + 2))
                sp.dma_start(qs[par][KROWS:KROWS + MROWS, :, :],
                             d_max.rearrange("r (h t) -> r h t", h=HEADS)).then_inc(max_in, 16)

            @block.sync
            def _(sp):
                sp_ab(sp, 0, 0)
                with sp.Fori(0, B // 2 - 1) as pair:
                    sp_ab(sp, 2 * pair + 1, 1)
                    sp_ab(sp, 2 * pair + 2, 0)
                sp_ab(sp, B - 1, 1)
                sp.wait_ge(max_in, 16 * B)


def layer1_conv(nc, t):
    SIDE, PAD = 32, 34
    with ExitStack() as ctx:
        def sb(name, shape, dt=F32):
            return ctx.enter_context(nc.sbuf_tensor(name, shape, dt))

        def sem(name):
            return ctx.enter_context(nc.semaphore("c_" + name))

        pad = sb("pad", [P, PAD, PAD])
        conv = sb("conv", [P, T])
        hidden = sb("hidden", [P, T])
        second = sb("second", [P, T])
        pw = sb("pw", [P, P])
        amax = sb("amax", [P, 2])
        keep = sb("keep", [P, 2])
        inv = sb("inv", [P, 2])
        off = sb("off", [P, 2])
        tmp = sb("tmp", [P, 4])
        ps = ctx.enter_context(nc.psum_tensor("c_ps", [P, 2 * HALF], F32))
        folded, root = sem("folded"), sem("root")
        padded, tap, hidden_done, kept, mm, second_done, added = (
            sem("padded"), sem("tap"), sem("hidden_done"), sem("kept"), sem("mm"), sem("second_done"), sem("added"))
        with nc.Block() as block:
            @block.vector
            def _(dve):
                dve.memset(pad[:, :, :], 0.0).then_inc(folded, 1)
                for n, bn in enumerate(("bn1", "bn2")):
                    dve.tensor_scalar(tmp[:, n:n + 1], t.vec(bn + "_v"), EPS5, None, ALU.add).then_inc(folded, 1)
                dve.wait_ge(root, 2)
                dve.reciprocal(tmp[:, 2:4], tmp[:, 0:2]).then_inc(folded, 1)
                dve.wait_ge(folded, 4)
                for n, (bn, bias) in enumerate((("bn1", "dw_b"), ("bn2", "pw_b"))):
                    dve.tensor_tensor(inv[:, n:n + 1], tmp[:, 2 + n:3 + n], t.vec(bn + "_g"), ALU.mult).then_inc(folded, 1)
                    dve.tensor_tensor(tmp[:, n:n + 1], t.vec(bias), t.vec(bn + "_m"), ALU.subtract).then_inc(folded, 1)
                dve.wait_ge(folded, 8)
                for n, bn in enumerate(("bn1", "bn2")):
                    dve.scalar_tensor_tensor(off[:, n:n + 1], tmp[:, n:n + 1], inv[:, n:n + 1], t.vec(bn + "_b"),
                                             ALU.mult, ALU.add).then_inc(folded, 1)
                with dve.Fori(0, B) as b:
                    r = t.resid[:, bass.ds(b * T, T)]
                    dve.tensor_scalar(pad[:, 1:SIDE + 1, 1:SIDE + 1], r.rearrange("p (y x) -> p y x", y=SIDE),
                                      t.gscale[:, bass.ds(b, 1)], t.gshift[:, bass.ds(b, 1)],
                                      ALU.mult, ALU.add).then_inc(padded, 1)
                    dve.wait_ge(padded, b + 1)
                    cv = conv[:, :].rearrange("p (y x) -> p y x", y=SIDE)
                    for n in range(9):
                        win = pad[:, n // 3:n // 3 + SIDE, n % 3:n % 3 + SIDE]
                        if n == 0:
                            dve.tensor_scalar(cv, win, t.vec("dw0"), None, ALU.mult).then_inc(tap, 1)
                        else:
                            dve.wait_ge(tap, b * 9 + n)
                            dve.scalar_tensor_tensor(cv, win, t.vec(f"dw{n}"), cv, ALU.mult, ALU.add).then_inc(tap, 1)
                    dve.wait_ge(hidden_done, b + 1)
                    dve.tensor_reduce(amax[:, 0:1], hidden[:, :], AX_X, ALU.max).then_inc(kept, 1)
                    dve.wait_ge(kept, b * 5 + 1)
                    dve.tensor_scalar(keep[:, 0:1], amax[:, 0:1], 4.0, None, ALU.is_ge).then_inc(kept, 1)
                    dve.wait_ge(kept, b * 5 + 2)
                    dve.tensor_scalar(pw[:, :], t.mat("pwT"), keep[:, 0:1], None, ALU.mult).then_inc(kept, 1)
                    dve.wait_ge(second_done, 2 * b + 2)
                    dve.tensor_reduce(amax[:, 1:2], second[:, :], AX_X, ALU.max).then_inc(kept, 1)
                    dve.wait_ge(kept, b * 5 + 4)
                    dve.tensor_scalar(keep[:, 1:2], amax[:, 1:2], 0.001, None, ALU.is_ge).then_inc(kept, 1)
                    dve.wait_ge(kept, b * 5 + 5)
                    dve.scalar_tensor_tensor(r, second[:, :], keep[:, 1:2], r, ALU.mult, ALU.add).then_inc(added, 1)

            @block.scalar
            def _(act):
                act.wait_ge(folded, 3)
                for n in range(2):
                    act.activation(tmp[:, n:n + 1], tmp[:, n:n + 1], ACT.Sqrt).then_inc(root, 1)
                act.wait_ge(folded, 10)
                with act.Fori(0, B) as b:
                    act.wait_ge(tap, 9 * b + 9)
                    act.activation(hidden[:, :], conv[:, :], ACT.Relu, bias=off[:, 0:1], scale=inv[:, 0:1]
                                   ).then_inc(hidden_done, 1)
                    for h in range(2):
                        act.wait_ge(mm, 2 * b + h + 1)
                        act.activation(second[:, h * HALF:(h + 1) * HALF], ps[:, h * HALF:(h + 1) * HALF], ACT.Relu,
                                       bias=off[:, 1:2], scale=inv[:, 1:2]).then_inc(second_done, 1)

            @block.tensor
            def _(pe):
                with pe.Fori(0, B) as b:
                    pe.wait_ge(kept, 5 * b + 3)
                    for h in range(2):
                        pe.matmul(ps[:, h * HALF:(h + 1) * HALF], pw[:, :], hidden[:, h * HALF:(h + 1) * HALF],
                                  start=True, stop=True).then_inc(mm, 1)


def pairs(eng, body):
    with eng.Fori(0, B // 2) as pair:
        body(2 * pair, 0)
        body(2 * pair + 1, 1)


def token_norm(nc, t, tag, eps):
    with ExitStack() as ctx:
        def sb(name, shape, dt=F32):
            return ctx.enter_context(nc.sbuf_tensor(tag + name, shape, dt))

        def sem(name):
            return ctx.enter_context(nc.semaphore(tag + name))

        xb = [sb(f"xb{i}", [P, T]) for i in range(2)]
        xt = [sb(f"xt{i}", [P, NT, P]) for i in range(2)]
        stats = sb("stats", [P, NT, 6])
        mv = sb("mv", [P, NT, 2])
        std = sb("std", [P, NT])
        rstd = sb("rstd", [P, NT])
        turned_in = [ctx.enter_context(nc.psum_tensor(f"{tag}in{i}", [P, NT, P], F32)) for i in range(2)]
        turned_out = [ctx.enter_context(nc.psum_tensor(f"{tag}out{i}", [P, T], F32)) for i in range(2)]
        copied, turned, stat, root, recip, normed, back, stored = (
            sem("copied"), sem("turned"), sem("stat"), sem("root"), sem("recip"), sem("normed"), sem("back"),
            sem("stored"))
        woke, waited = sem("woke"), sem("waited")
        with nc.Block() as block:
            @block.gpsimd
            def _(pool):
                pool.sem_inc(turned, 2)
                pool.sem_inc(normed, 2)
                pool.sem_inc(stored, 2)
                pool.sem_inc(back, 2)

                def body(b, i):
                    pool.wait_ge(turned, b + 1)
                    pool.sem_inc(woke, 1)
                    pool.tensor_copy(xb[i][:, :], t.resid[:, bass.ds(b * T, T)]).then_inc(copied, 1)
                pairs(pool, body)

            @block.tensor
            def _(pe):
                def body(b, i):
                    pe.wait_ge(copied, b + 1)
                    pe.wait_ge(normed, b + 1)
                    for j in range(NT):
                        tr = pe.transpose(turned_in[i][:, j, :], xb[i][:, j * P:(j + 1) * P], t.mat("ident"))
                    tr.then_inc(turned, 1)
                    pe.wait_ge(normed, b + 1 + 2)
                    pe.wait_ge(stored, b + 1)
                    for j in range(NT):
                        tr = pe.transpose(turned_out[i][:, j * P:(j + 1) * P], xt[i][:, j, :], t.mat("ident"))
                    tr.then_inc(back, 1)
                pairs(pe, body)

            @block.vector
            def _(dve):
                def body(b, i):
                    dve.wait_ge(turned, b + 1 + 2)
                    for j in range(NT):
                        bn = dve.bn_stats(stats[:, j, :], turned_in[i][:, j, :])
                    bn.then_inc(stat, 1)
                    dve.wait_ge(stat, 2 * b + 1)
                    dve.sem_inc(waited, 1)
                    for j in range(NT):
                        bn = dve.bn_aggr(mv[:, j, :], stats[:, j, :])
                    bn.then_inc(stat, 1)
                    dve.wait_ge(root, b + 1)
                    dve.reciprocal(rstd[:, :], std[:, :]).then_inc(recip, 1)
                    dve.wait_ge(recip, b + 1)
                    dve.wait_ge(back, b + 1)
                    for j in range(NT):
                        ts = dve.tensor_scalar(xt[i][:, j, :], turned_in[i][:, j, :], mv[:, j, 0:1],
                                               rstd[:, j:j + 1], ALU.subtract, ALU.mult)
                    ts.then_inc(normed, 1)
                pairs(dve, body)

            @block.scalar
            def _(act):
                def body(b, i):
                    act.wait_ge(stat, 2 * b + 2)
                    act.activation(std[:, :], mv[:, :, 1], ACT.Sqrt, bias=t.vec(eps)).then_inc(root, 1)
                    act.wait_ge(back, b + 1 + 2)
                    act.activation(t.xn[:, bass.ds(b * T, T)], turned_out[i][:, :], ACT.Copy).then_inc(stored, 1)
                pairs(act, body)


def layer2_attention(nc, t):
    NEG = -1e30
    with ExitStack() as ctx:
        def sb(name, shape, dt=F32):
            return ctx.enter_context(nc.sbuf_tensor("b_" + name, shape, dt))

        def sem(name):
            return ctx.enter_context(nc.semaphore("b_" + name))

        def psum(name, n):
            return ctx.enter_context(nc.psum_tensor("b_" + name, [P, n], F32))

        wqk = sb("wqk", [P, P])
        identb = sb("identb", [P, P], BF16)
        future = sb("future", [P, HALF], BF16)
        xb = [sb(f"xb{i}", [P, T]) for i in range(2)]
        q = [sb(f"q{i}", [P, T]) for i in range(2)]
        v = [sb(f"v{i}", [P, NT, P]) for i in range(2)]
        prob = [sb(f"prob{i}", [P, T]) for i in range(2)]
        probT = [sb(f"probT{i}", [P, NT, P]) for i in range(2)]
        peak = sb("peak", [P, NT])
        top = sb("top", [P, NT])
        total = sb("total", [P, NT])
        inv = sb("inv", [P, NT])
        s_ps = [psum(f"s_ps{i}", T) for i in range(2)]
        t_ps = psum("t_ps", T)
        o_ps = psum("o_ps", HALF)
        x_ps = psum("x_ps", HALF)
        ready, wdone, copied, mm_p, q_out, v_out = (
            sem("ready"), sem("wdone"), sem("copied"), sem("mm_p"), sem("q_out"), sem("v_out"))
        mm_s, maxed, topped, exped, inverted, scaled, turned, tout, mm_o, added = (
            sem("mm_s"), sem("maxed"), sem("topped"), sem("exped"), sem("inverted"), sem("scaled"), sem("turned"), sem("tout"),
            sem("mm_o"), sem("added"))
        SCALE = 1.0 / float(np.sqrt(C))
        woke = sem("woke")
        banks = [o_ps, x_ps]
        with nc.Block() as block:
            @block.gpsimd
            def _(pool):
                pool.memset(future[:, :], 0.0).then_inc(ready, 1)
                pool.wait_ge(ready, 1)
                pool.affine_select(future[:, HALF - P:], future[:, HALF - P:], pattern=[[-1, P]], compare_op=ALU.is_ge, fill=NEG,
                                   base=0, channel_multiplier=1).then_inc(ready, 1)
                pool.tensor_copy(identb[:, :], t.mat("ident")).then_inc(ready, 1)
                pool.sem_inc(topped, 2)
                pool.sem_inc(exped, 2)
                pool.sem_inc(tout, 1)
                pool.sem_inc(turned, 2)
                pool.sem_inc(mm_o, 2)
                pool.sem_inc(added, 2)

                def body(b, i):
                    pool.wait_ge(mm_o, b * NT + 1)
                    pool.sem_inc(woke, 1)
                    pool.tensor_copy(xb[i][:, :], t.xn[:, bass.ds(b * T, T)]).then_inc(copied, 1)
                pairs(pool, body)

            @block.tensor
            def _(pe):
                pe.matmul(o_ps[:, 0:P], t.mat("Wq"), t.mat("Wk"), start=True, stop=True).then_inc(mm_p, 1)
                pe.wait_ge(ready, 3)
                pe.wait_ge(wdone, 1)

                def project(b, i):
                    pe.wait_ge(copied, b + 1)
                    for n in range(4):
                        if n < 2:
                            pe.wait_ge(added, b * NT + 2)
                        else:
                            pe.wait_ge(q_out, 2 * b + n - 1)
                        bank = banks[n % 2]
                        if n < 2:
                            mm = pe.matmul(bank[:, :], wqk[:, :], xb[i][:, n * HALF:(n + 1) * HALF], start=True, stop=True)
                        else:
                            for j in range(4):
                                k = 4 * (n - 2) + j
                                mm = pe.matmul(bank[:, j * P:(j + 1) * P], xb[i][:, k * P:(k + 1) * P], t.mat("WvT"),
                                               start=True, stop=True)
                        mm.then_inc(mm_p, 1)

                def scores(b, i, m):
                    g = b * NT + m
                    if m < 2:
                        pe.wait_ge(q_out, 2 * b + 2)
                    pe.wait_ge(exped, g + 1)
                    lhsT = q[i][:, m * P:(m + 1) * P]
                    keys = (m + 1) * P
                    for k0 in range(0, keys, HALF):
                        n = min(HALF, keys - k0)
                        diagonal = k0 + n == keys
                        pe.matmul(s_ps[m % 2][:, k0:k0 + n], lhsT, xb[i][:, k0:k0 + n], start=True, stop=not diagonal)
                    mm = pe.matmul(s_ps[m % 2][:, k0:keys], identb[:, :], future[:, HALF - n:], start=False, stop=True)
                    mm.then_inc(mm_s, 1)

                def values(b, i, m):
                    g = b * NT + m
                    pe.wait_ge(scaled, g + 1)
                    pe.wait_ge(tout, g + 1)
                    for k in range(m + 1):
                        tr = pe.transpose(t_ps[:, k * P:(k + 1) * P], prob[m % 2][:, k * P:(k + 1) * P], t.mat("ident"))
                    tr.then_inc(turned, 1)
                    if m == 0:
                        pe.wait_ge(v_out, 2 * b + 2)
                    pe.wait_ge(tout, g + 1 + 1)
                    pe.wait_ge(added, g + 1)
                    for k in range(m + 1):
                        mm = pe.matmul(banks[m % 2][:, 0:P], v[i][:, k, :], probT[m % 2][:, k, :],
                                       start=(k == 0), stop=(k == m))
                    mm.then_inc(mm_o, 1)

                def body(b, i):
                    project(b, i)
                    scores(b, i, 0)
                    for m in range(NT):
                        if m + 1 < NT:
                            scores(b, i, m + 1)
                        values(b, i, m)
                pairs(pe, body)

            @block.vector
            def _(dve):
                dve.wait_ge(mm_p, 1)
                dve.tensor_copy(wqk[:, :], o_ps[:, 0:P]).then_inc(wdone, 1)

                def topmost(b, i, m):
                    g = b * NT + m
                    dve.wait_ge(mm_s, g + 1)
                    dve.tensor_reduce(peak[:, m:m + 1], s_ps[m % 2][:, 0:(m + 1) * P], AX_X, ALU.max).then_inc(maxed, 1)
                    dve.wait_ge(maxed, g + 1)
                    dve.tensor_scalar(top[:, m:m + 1], peak[:, m:m + 1], -SCALE, None, ALU.mult).then_inc(topped, 1)

                def scale(b, i, m):
                    g = b * NT + m
                    dve.wait_ge(exped, g + 1 + 2)
                    dve.reciprocal(inv[:, m:m + 1], total[:, m:m + 1]).then_inc(inverted, 1)
                    dve.wait_ge(inverted, g + 1)
                    pr = prob[m % 2][:, 0:(m + 1) * P]
                    dve.tensor_scalar(pr, pr, inv[:, m:m + 1], None, ALU.mult).then_inc(scaled, 1)

                def finish(b, i, m):
                    g = b * NT + m
                    dve.wait_ge(mm_o, g + 1 + 2)
                    r = t.resid[:, bass.ds(b * T + m * P, P)]
                    dve.tensor_tensor(r, banks[m % 2][:, 0:P], r, ALU.add).then_inc(added, 1)

                def body(b, i):
                    for n in range(2, 4):
                        dve.wait_ge(mm_p, 4 * b + n + 1 + 1)
                        dve.tensor_copy(v[i][:, 4 * n - 8:4 * n - 4, :], banks[n % 2][:, :]).then_inc(v_out, 1)
                    topmost(b, i, 0)
                    for m in range(NT):
                        if m + 1 < NT:
                            topmost(b, i, m + 1)
                        scale(b, i, m)
                        if m:
                            finish(b, i, m - 1)
                    finish(b, i, NT - 1)
                pairs(dve, body)

            @block.scalar
            def _(act):
                def exp(b, i, m):
                    g = b * NT + m
                    act.wait_ge(topped, g + 1 + 2)
                    act.wait_ge(turned, g + 1)
                    act.activation(prob[m % 2][:, 0:(m + 1) * P], s_ps[m % 2][:, 0:(m + 1) * P], ACT.Exp,
                                   bias=top[:, m:m + 1], scale=SCALE, accum_out=total[:, m:m + 1]).then_inc(exped, 1)

                def turn(b, i, m):
                    g = b * NT + m
                    act.wait_ge(turned, g + 1 + 2)
                    act.wait_ge(mm_o, g + 1)
                    act.activation(probT[m % 2][:, 0:m + 1, :], t_ps[:, 0:(m + 1) * P], ACT.Copy).then_inc(tout, 1)

                def body(b, i):
                    for n in range(2):
                        act.wait_ge(mm_p, 4 * b + n + 1 + 1)
                        act.activation(q[i][:, n * HALF:(n + 1) * HALF], banks[n % 2][:, :], ACT.Copy).then_inc(q_out, 1)
                    exp(b, i, 0)
                    for m in range(NT):
                        if m + 1 < NT:
                            exp(b, i, m + 1)
                        turn(b, i, m)
                pairs(act, body)


def moe(nc, t, router, gate_up, down, sel):
    NE, F = 16, 256
    with ExitStack() as ctx:
        def sb(name, shape, dt=F32):
            return ctx.enter_context(nc.sbuf_tensor("m_" + name, shape, dt))

        def sem(name):
            return ctx.enter_context(nc.semaphore("m_" + name))

        def psum(name, shape):
            return ctx.enter_context(nc.psum_tensor("m_" + name, shape, F32))

        w_router = sb("w_router", [P, NE])
        w_gu = sb("w_gu", [P, NE, 2, F])
        w_down = sb("w_down", [P, NE, 2, P])
        w_sel = sb("w_sel", [NE, NE, P])
        iota = sb("iota", [P, NE])
        xb = [sb(f"xb{i}", [P, T]) for i in range(2)]
        logit = sb("logit", [P, NT, NE])
        top = sb("top", [P, NT, 8])
        index = sb("index", [P, NT, 8], U32)
        indexf = sb("indexf", [P, NT, 8])
        wt = sb("wt", [P, 3, NT])
        pick = sb("pick", [P, 2, NT, NE])
        comb = sb("comb", [P, NT, NE])
        combT = sb("combT", [NE, T])
        silu = sb("silu", [P, 2, HALF])
        prod = sb("prod", [P, 2, HALF])
        hid = sb("hid", [P, 2, HALF])
        g_ps = [psum(f"g{i}", [P, HALF]) for i in range(2)]
        u_ps = [psum(f"u{i}", [P, HALF]) for i in range(2)]
        ce_ps = [psum(f"ce{i}", [P, HALF]) for i in range(2)]
        y_ps = psum("y", [P, HALF])
        r_ps = psum("r", [P, HALF])
        loaded, const, woke, waited, copied = sem("loaded"), sem("const"), sem("woke"), sem("waited"), sem("copied")
        mm_r, route, expd, turned, tout = sem("mm_r"), sem("route"), sem("expd"), sem("turned"), sem("tout")
        mm_gu, silu_done, prod_done, hid_done, mm_down, added = (
            sem("mm_gu"), sem("silu_done"), sem("prod_done"), sem("hid_done"), sem("mm_down"), sem("added"))
        UNITS = 2 * NE * 2
        ROUTE = 3 * NT + 7
        with nc.Block() as block:
            @block.sync
            def _(sp):
                for dst, src in ((w_router[:, :], router), (w_gu[:, :, :, :], gate_up), (w_down[:, :, :, :], down),
                                 (w_sel[:, :, :], sel)):
                    sp.dma_start(dst, src).then_inc(loaded, 16)

            @block.gpsimd
            def _(pool):
                pool.iota(iota[:, :], pattern=[[1, NE]], base=0, channel_multiplier=0,
                          allow_small_or_imprecise_dtypes=True).then_inc(const, 1)
                pool.sem_inc(hid_done, 2)
                pool.sem_inc(mm_down, 2)
                pool.sem_inc(added, 1)
                pool.sem_inc(tout, 1)

                def body(b, i):
                    pool.wait_ge(mm_down, b * UNITS + 1)
                    pool.sem_inc(woke, 1)
                    pool.tensor_copy(xb[i][:, :], t.xn[:, bass.ds(b * T, T)]).then_inc(copied, 1)
                pairs(pool, body)

            @block.tensor
            def _(pe):
                pe.wait_ge(loaded, 64)

                def gate_up_mm(b, i, k):
                    h, e, f = k // (2 * NE), k // 2 % NE, k % 2
                    x = xb[i][:, h * HALF:(h + 1) * HALF]
                    pe.wait_ge(hid_done, b * UNITS + k + 1)
                    pe.matmul(g_ps[k % 2][:, :], w_gu[:, e, 0, f * P:(f + 1) * P], x, start=True, stop=True)
                    mm = pe.matmul(u_ps[k % 2][:, :], w_gu[:, e, 1, f * P:(f + 1) * P], x, start=True, stop=True)
                    if f == 0:
                        mm = pe.matmul(ce_ps[e % 2][:, :], w_sel[:, e, :], combT[:, h * HALF:(h + 1) * HALF],
                                       start=True, stop=True)
                    mm.then_inc(mm_gu, 1)

                def down_mm(b, i, k):
                    h, e, f = k // (2 * NE), k // 2 % NE, k % 2
                    pe.wait_ge(hid_done, b * UNITS + k + 1 + 2)
                    if e == 0 and f == 0:
                        pe.wait_ge(added, 2 * b + h + 1)
                    pe.matmul(y_ps[:, :], w_down[:, e, f, :], hid[:, k % 2, :], start=(e + f == 0),
                              stop=(e == NE - 1 and f == 1)).then_inc(mm_down, 1)

                def body(b, i):
                    pe.wait_ge(copied, b + 1)
                    pe.wait_ge(tout, 2 * b + 1)
                    for j in range(NT):
                        mm = pe.matmul(r_ps[:, j * NE:(j + 1) * NE], xb[i][:, j * P:(j + 1) * P], w_router[:, :],
                                       start=True, stop=True)
                    mm.then_inc(mm_r, 1)
                    pe.wait_ge(route, (b + 1) * ROUTE)
                    for h in range(2):
                        pe.wait_ge(tout, 2 * b + h + 1)
                        for j in range(4):
                            tr = pe.transpose(r_ps[0:NE, j * P:(j + 1) * P], comb[:, 4 * h + j, :], t.mat("ident"))
                        tr.then_inc(turned, 1)
                    pe.wait_ge(tout, 2 * b + 2 + 1)
                    for k in range(UNITS):
                        gate_up_mm(b, i, k)
                        if k:
                            down_mm(b, i, k - 1)
                    down_mm(b, i, UNITS - 1)
                pairs(pe, body)

            @block.vector
            def _(dve):
                dve.wait_ge(const, 1)

                def routing(b):
                    n = b * ROUTE
                    dve.wait_ge(mm_r, b + 1)
                    dve.tensor_copy(logit[:, :, :], r_ps[:, 0:NT * NE]).then_inc(route, 1)
                    dve.wait_ge(route, n + 1)
                    dve.sem_inc(waited, 1)
                    for j in range(NT):
                        dve.max(top[:, j, :], logit[:, j, :]).then_inc(route, 1)
                    dve.wait_ge(route, n + 1 + NT)
                    dve.sem_inc(waited, 1)
                    for j in range(NT):
                        dve.max_index(index[:, j, :], top[:, j, :], logit[:, j, :]).then_inc(route, 1)
                    dve.wait_ge(route, n + 1 + 2 * NT)
                    dve.tensor_copy(indexf[:, :, :], index[:, :, :]).then_inc(route, 1)
                    dve.tensor_tensor(wt[:, 0, :], top[:, :, 1], top[:, :, 0], ALU.subtract).then_inc(route, 1)
                    dve.wait_ge(expd, b + 1)
                    dve.tensor_scalar(wt[:, 0, :], wt[:, 2, :], 1.0, None, ALU.add).then_inc(route, 1)
                    dve.wait_ge(route, n + 4 + 2 * NT)
                    dve.reciprocal(wt[:, 1, :], wt[:, 0, :]).then_inc(route, 1)
                    dve.wait_ge(route, n + 5 + 2 * NT)
                    dve.tensor_tensor(wt[:, 2, :], wt[:, 2, :], wt[:, 1, :], ALU.mult).then_inc(route, 1)
                    dve.wait_ge(route, n + 6 + 2 * NT)
                    for j in range(NT):
                        for c in range(2):
                            ts = dve.tensor_scalar(pick[:, c, j, :], iota[:, :], indexf[:, j, c:c + 1],
                                                   wt[:, 1 + c, j:j + 1], ALU.is_equal, ALU.mult)
                        ts.then_inc(route, 1)

                def body(b, i):
                    routing(b)
                    dve.wait_ge(route, b * ROUTE + 6 + 3 * NT)
                    dve.tensor_tensor(comb[:, :, :], pick[:, 0, :, :], pick[:, 1, :, :], ALU.add).then_inc(route, 1)
                    for h in range(2):
                        dve.wait_ge(turned, 2 * b + h + 1)
                        dve.tensor_copy(combT[:, h * HALF:(h + 1) * HALF], r_ps[0:NE, :]).then_inc(tout, 1)
                    for k in range(UNITS):
                        h, e = k // (2 * NE), k // 2 % NE
                        g = b * UNITS + k
                        dve.wait_ge(silu_done, g + 1)
                        dve.tensor_tensor(prod[:, k % 2, :], u_ps[k % 2][:, :], silu[:, k % 2, :], ALU.mult
                                          ).then_inc(prod_done, 1)
                        dve.wait_ge(prod_done, g + 1)
                        dve.wait_ge(mm_down, g + 1)
                        dve.tensor_tensor(hid[:, k % 2, :], ce_ps[e % 2][:, :], prod[:, k % 2, :], ALU.mult
                                          ).then_inc(hid_done, 1)
                        if k % (2 * NE) == 0 and k:
                            finish(b, h - 1)
                    finish(b, 1)

                def finish(b, h):
                    dve.wait_ge(mm_down, b * UNITS + (h + 1) * 2 * NE + 2)
                    r = t.resid[:, bass.ds(b * T + h * HALF, HALF)]
                    dve.tensor_tensor(r, y_ps[:, :], r, ALU.add).then_inc(added, 1)
                pairs(dve, body)

            @block.scalar
            def _(act):
                def body(b, i):
                    act.wait_ge(route, b * ROUTE + 3 + 2 * NT)
                    act.activation(wt[:, 2, :], wt[:, 0, :], ACT.Exp).then_inc(expd, 1)
                    for k in range(UNITS):
                        g = b * UNITS + k
                        act.wait_ge(mm_gu, g + 1)
                        act.wait_ge(hid_done, g + 1)
                        act.activation(silu[:, k % 2, :], g_ps[k % 2][:, :], ACT.Silu).then_inc(silu_done, 1)
                pairs(act, body)


def spill_residual(nc, t, d_resid, back):
    with nc.semaphore(f"spilled{back}") as spilled, nc.Block() as block:
        @block.sync
        def _(sp):
            for b in range(B):
                dram, sbuf = d_resid[:, b * T:(b + 1) * T], t.resid[:, b * T:(b + 1) * T]
                sp.dma_start(*((sbuf, dram) if back else (dram, sbuf))).then_inc(spilled, 16)
            sp.wait_ge(spilled, 16 * B)


D = 4
NB = 4
HH = NB * HEADS
JM = T // D
CHUNK = 16
QUADS = CHUNK // D
SEG = 128
WIN = CHUNK + D - 1
OP = SEG + D - 1 + 1
TAU = 0.1
TINY = 1e-16


class Semaphores:

    def __init__(self, nc, tag):
        self.nc, self.tag, self.taken = nc, tag, []

    def __call__(self, name):
        self.taken.append(self.nc.alloc_semaphore(self.tag + name))
        return self.taken[-1]

    def give_back(self):
        self.nc.clear_and_free_semaphores(self.taken)
        self.nc.all_engine_barrier()


class Scan:

    def __init__(self, nc, ctx):
        def sb(name, shape, dt=F32):
            return ctx.enter_context(nc.sbuf_tensor("s_" + name, shape, dt))
        self.w3 = sb("w3", [P, 3 * P])
        self.head_mask = sb("head_mask", [P, HEADS])
        self.col = sb("col", [P, 8])
        self.inv = sb("inv", [P, T + SEG + D])
        self.causal = sb("causal", [P, 32, 32])
        self.sel = sb("sel", [HH, 2 * NB, P])
        self.wo = sb("wo", [P, 2, P])
        self.ik = sb("ik", [P, NB, D, 2, P])
        self.iv = sb("iv", [P, D, 2, HH, HD + 1])
        self.O = sb("O", [P, 2 * NB, D * (OP + 1)])
        self.Mw = sb("Mw", [HH, D * (OP + 1)])
        self.Mseg = sb("Mseg", [P, SEG])

    def add_work(self, nc, ctx, grp):
        def sb(name, shape, dt=F32):
            return ctx.enter_context(nc.sbuf_tensor(f"s{grp}_" + name, shape, dt))
        self.iqm = [sb(f"iqm{i}", [P, NB, HEADS, WIN]) for i in range(2)]
        self.X = [sb(f"X{i}", [P, D, 2, QUADS, P]) for i in range(2)]
        self.Y = sb("Y", [P, 2 * D, 1 + JM])
        self.E = sb("E", [P, 2, D, 2 * P])
        self.mx = sb("mx", [P, D])
        self.negm = sb("negm", [P, 2, CHUNK])
        self.W = sb("W", [P, 2, D * SEG])
        self.warg = sb("warg", [P, 2, D, SEG])
        self.mx_full = sb("mx_full", [HH, D - 1, SEG])
        self.F = sb("F", [HH, D, SEG])


def scan_projection(nc, t, s, grp):
    with ExitStack() as ctx:
        def sb(name, shape, dt=F32):
            return ctx.enter_context(nc.sbuf_tensor(f"p{grp}_{name}", shape, dt))

        sem = Semaphores(nc, f"p{grp}_")
        ctx.callback(sem.give_back)

        NG = 3 * HEADS
        z = [sb(f"z{i}", [P, NG, HD]) for i in range(2)]
        mx = sb("mx", [P, NG])
        den = sb("den", [P, NG])
        rden = sb("rden", [P, NG])
        soft = [sb(f"soft{i}", [P, NG, HD]) for i in range(2)]
        z_ps = [ctx.enter_context(nc.psum_tensor(f"p{grp}_zp{i}", [P, HALF // HD, HD], F32))[:, 0:NG, :] for i in range(2)]
        t_ps = [ctx.enter_context(nc.psum_tensor(f"p{grp}_tp{i}", [P, 4, P], F32)) for i in range(2)]
        mm, maxed, less, expd, summed, recip, done, turned, out = (
            sem("mm"), sem("maxed"), sem("less"), sem("expd"), sem("summed"), sem("recip"), sem("done"),
            sem("turned"), sem("out"))
        tiles = [(b, rho, jt) for b in range(NB) for rho in range(D) for jt in range(2)]

        def tokens(tile):
            b, rho, jt = tile
            c0 = (grp * NB + b) * T + jt * P * D + rho
            return t.xn[:, c0:c0 + (P - 1) * D + 1:D]

        with nc.Block() as block:
            @block.tensor
            def _(pe):
                def project(n):
                    if n >= 2:
                        pe.wait_ge(less, n - 1)
                    pe.matmul(z_ps[n % 2][:, :, :], tokens(tiles[n]), s.w3[:, :], start=True, stop=True).then_inc(mm, 1)

                def turn(n):
                    pe.wait_ge(done, 2 * n + 1)
                    if n >= 2:
                        pe.wait_ge(out, n - 1)
                    for m in range(2):
                        tr = pe.transpose(t_ps[n % 2][:, m, :], soft[n % 2][:, m * HEADS:(m + 1) * HEADS, :], t.mat("ident"))
                    tr.then_inc(turned, 1)
                project(0)
                for n in range(len(tiles)):
                    if n + 1 < len(tiles):
                        project(n + 1)
                    turn(n)

            @block.vector
            def _(dve):
                for k in range(2):
                    dve.memset(s.iv[:, 2 * k:2 * k + 2, :, :, HD:HD + 1], 1.0)

                def second(n):
                    dve.wait_ge(expd, n + 1)
                    if n:
                        dve.wait_ge(done, 2 * n)
                    dve.tensor_reduce(den[:, :], z[n % 2][:, :, :], AX_X, ALU.add).then_inc(summed, 1)
                    dve.wait_ge(summed, n + 1)
                    dve.reciprocal(rden[:, :], den[:, :]).then_inc(recip, 1)
                    dve.wait_ge(recip, n + 1)
                    if n >= 2:
                        dve.wait_ge(turned, n - 1)
                    b, rho, jt = tiles[n]
                    Q = 2 * HEADS
                    dve.scalar_tensor_tensor(soft[n % 2][:, 0:Q, :], z[n % 2][:, 0:Q, :], TINY,
                                             rden[:, 0:Q].unsqueeze(2).to_broadcast([P, Q, HD]), ALU.max, ALU.mult
                                             ).then_inc(done, 1)
                    dve.scalar_tensor_tensor(s.iv[:, rho, jt, b * HEADS:(b + 1) * HEADS, 0:HD], z[n % 2][:, Q:NG, :], TINY,
                                             rden[:, Q:NG].unsqueeze(2).to_broadcast([P, HEADS, HD]), ALU.max, ALU.mult
                                             ).then_inc(done, 1)
                for n in range(len(tiles)):
                    dve.wait_ge(mm, n + 1)
                    if n:
                        dve.wait_ge(less, n)
                    if n >= 2:
                        dve.wait_ge(done, 2 * (n - 1))
                    dve.tensor_reduce(mx[:, :], z_ps[n % 2][:, :, :], AX_X, ALU.max).then_inc(maxed, 1)
                    dve.wait_ge(maxed, n + 1)
                    dve.tensor_tensor(z[n % 2][:, :, :], z_ps[n % 2][:, :, :],
                                      mx[:, :].unsqueeze(2).to_broadcast([P, NG, HD]), ALU.subtract).then_inc(less, 1)
                    if n:
                        second(n - 1)
                second(len(tiles) - 1)

            @block.scalar
            def _(act):
                def store(n):
                    b, rho, jt = tiles[n]
                    act.wait_ge(turned, n + 1)
                    act.activation(tokens(tiles[n]), t_ps[n % 2][:, 0, :], ACT.Copy)
                    act.activation(s.ik[:, b, rho, jt, :], t_ps[n % 2][:, 1, :], ACT.Copy).then_inc(out, 1)
                for n in range(len(tiles)):
                    act.wait_ge(less, n + 1)
                    act.activation(z[n % 2][:, :, :], z[n % 2][:, :, :], ACT.Exp, scale=1 / TAU).then_inc(expd, 1)
                    if n:
                        store(n - 1)
                store(len(tiles) - 1)


def scan_segment(nc, t, s, grp, seg):
    tail = seg == T // SEG
    JT = 1 if seg < 4 else 2
    K = min(32 * (seg + 1), JM)
    quads = 1 if tail else QUADS
    chunks = 1 if tail else SEG // CHUNK
    row0 = seg * SEG
    tag = f"g{grp}s{seg}_"
    with ExitStack() as ctx:
        def sb(name, shape, dt=F32):
            return ctx.enter_context(nc.sbuf_tensor(tag + name, shape, dt))

        sem = Semaphores(nc, tag)
        ctx.callback(sem.give_back)

        def psum(name, shape):
            return ctx.enter_context(nc.psum_tensor(tag + name, shape, F32))

        iqm, X, Y, E = s.iqm, s.X, s.Y, s.E
        mx, negm, W = s.mx, s.negm, s.W
        Pv = t.resid[:, :].rearrange("p (k a r h n i) -> p k a r h n i", k=2, a=2, r=D, h=HH, n=QUADS)
        x_ps = [psum(f"x{i}", [P, D, JT * P]) for i in range(2)]
        p_ps = [psum(f"p{i}", [P, D * D, HH]) for i in range(2)]
        s_ps = psum("s", [P, HH, CHUNK])
        o_ps = psum("o", [P, 2 * NB, CHUNK, D])
        masked_q, sc_mm, x_out, turned, y_done, causal_done, mx_done, negm_done = (
            sem("masked_q"), sem("sc_mm"), sem("x_out"), sem("turned"), sem("y_done"), sem("causal_done"),
            sem("mx_done"), sem("negm_done"))
        exp_done, back, p_done, av_mm, o_out, m_copied, arg_done, w_done, zeroed, woke = (
            sem("exp_done"), sem("back"), sem("p_done"), sem("av_mm"), sem("o_out"), sem("m_copied"),
            sem("arg_done"), sem("w_done"), sem("zeroed"), sem("woke"))
        UNITS = D * JT
        ZEROED = 5 if seg == 0 else 1
        xs = quads * D

        def run(eng, body):
            body(0, 0, True)
            if chunks > 1:
                body(1, 1, False)
                with eng.Fori(1, chunks // 2) as pair:
                    body(2 * pair, 0, False)
                    body(2 * pair + 1, 1, False)

        AHEAD = ((0, 1), (2,), (3,), ())

        with nc.Block() as block:
            @block.gpsimd
            def _(pool):
                pool.sem_inc(m_copied, 2)

                def mask(q, i):
                    pool.wait_ge(sc_mm, UNITS * (q + 1))
                    for b in range(NB):
                        c0 = (grp * NB + b) * T + row0 + XPAD - (D - 1)
                        iq = t.xnp[:, bass.ds(c0 + CHUNK * q, WIN)]
                        pt = pool.tensor_tensor(iqm[i][:, b, :, :], iq.unsqueeze(1).to_broadcast([P, HEADS, WIN]),
                                                s.head_mask[:, :].unsqueeze(2).to_broadcast([P, HEADS, WIN]), ALU.mult)
                    pt.then_inc(masked_q, 1)

                def keep(q, i):
                    pool.wait_ge(negm_done, quads * (q + 1) + 1)
                    pool.sem_inc(woke, 1)
                    pool.tensor_copy(s.Mseg[:, bass.ds(CHUNK * q, xs)], negm[:, i, 0:xs]).then_inc(m_copied, 1)
                mask(0, 0)
                def body(q, i, first):
                    if not tail:
                        mask(q + 1, 1 - i)
                    keep(q, i)
                run(pool, body)

            @block.tensor
            def _(pe):
                pe.sem_inc(sc_mm, 2 * UNITS)
                pe.sem_inc(turned, 8)
                pe.sem_inc(back, 2 * JT)
                pe.sem_inc(av_mm, 2)

                def scores(q, i, rho):
                    if rho == 0:
                        pe.wait_ge(masked_q, q + 1)
                    for jt in range(JT):
                        pe.wait_ge(x_out, UNITS * q + rho * JT + jt + 1)
                        for b in range(NB):
                            mm = pe.matmul(s_ps[:, b * HEADS:(b + 1) * HEADS, :], s.ik[:, b, rho, jt, :],
                                           iqm[i][:, b, :, rho:rho + CHUNK], start=True, stop=True)
                        mm.then_inc(sc_mm, 1)

                def turn(q, i, k):
                    if k == 0:
                        pe.wait_ge(x_out, UNITS * (q + 1) + 1)
                    pe.wait_ge(y_done, 4 * (quads * q + k) + 4)
                    for rho in range(D):
                        for jt in range(JT):
                            tr = pe.transpose(x_ps[k % 2][:, rho, jt * P:(jt + 1) * P], X[i][:, rho, jt, k, :], t.mat("ident"))
                    tr.then_inc(turned, 1)

                def turn_back(q, i, k):
                    g = quads * q + k
                    pe.wait_ge(exp_done, 4 * (g + 1) + 8)
                    for jt in range(JT):
                        pe.wait_ge(p_done, JT * g + jt + 1)
                        for rho in range(D):
                            tr = pe.transpose(p_ps[(JT * k + jt) % 2][:, rho * D:(rho + 1) * D, :],
                                              E[:, k % 2, rho, jt * P:(jt + 1) * P], t.mat("ident"))
                        tr.then_inc(back, 1)

                def values(q, i):
                    pe.wait_ge(p_done, JT * quads * (q + 1) + 2)
                    pe.wait_ge(o_out, q + 1)
                    for b in range(2 * NB):
                        for rho in range(D):
                            for jt in range(JT):
                                for h4 in range(4):
                                    hh = 4 * b + h4
                                    mm = pe.matmul(o_ps[32 * h4:32 * h4 + HD + 1, b, rho:CHUNK:D, :],
                                                   s.iv[:, rho, jt, hh, :],
                                                   Pv[:, i, jt, rho, hh, :, :],
                                                   start=jt == 0, stop=jt == JT - 1)
                    mm.then_inc(av_mm, 1)

                pe.wait_ge(zeroed, ZEROED)
                for rho in range(D):
                    scores(0, 0, rho)
                turn(0, 0, 0)

                def body(q, i, first):
                    for k in range(quads):
                        if not tail:
                            for rho in AHEAD[k]:
                                scores(q + 1, 1 - i, rho)
                            if k < quads - 1:
                                turn(q, i, k + 1)
                        turn_back(q, i, k)
                        if not tail and k == quads - 1:
                            turn(q + 1, 1 - i, 0)
                        if k == 1 and not first:
                            values(q - 1, 1 - i)
                run(pe, body)
                values(chunks - 1, (chunks - 1) % 2)

            @block.vector
            def _(dve):
                dve.sem_inc(y_done, 8)
                dve.sem_inc(p_done, 2)
                dve.sem_inc(negm_done, 1)
                dve.memset(o_ps[:, :, :, :], 0.0).then_inc(zeroed, 1)
                if seg == 0:
                    dve.memset(E[:, :, :, :], 0.0).then_inc(zeroed, 1)
                    dve.memset(Y[:, :, :], 0.0).then_inc(zeroed, 1)
                    dve.memset(s.O[:, :, :], 0.0).then_inc(zeroed, 1)
                    dve.memset(s.Mw[:, :], 0.0).then_inc(zeroed, 1)
                dve.wait_ge(zeroed, ZEROED)
                for jt in range(JT):
                    for rho in range(D):
                        n = jt * D + rho
                        dve.tensor_scalar(s.warg[:, jt, rho, :], s.inv[:, row0 + rho:row0 + rho + SEG],
                                          s.col[:, n:n + 1], 10.0, ALU.mult, ALU.min).then_inc(arg_done, 1)

                def recur(q, i, k, first):
                    g = quads * q + k
                    dve.wait_ge(turned, g + 1 + 8)
                    dve.wait_ge(exp_done, 4 * g + 4)
                    for rho in range(D):
                        slot = 4 * (k % 2) + rho if not tail else rho
                        last = (slot - 1) % 8
                        if rho:
                            dve.wait_ge(y_done, 8 + 4 * g + rho)
                        elif not (first and k == 0):
                            dve.wait_ge(causal_done, g)
                        dve.scalar_tensor_tensor(Y[:, slot, 1:1 + K], Y[:, last, (1 if rho else 0):(1 if rho else 0) + K],
                                                 1.0, x_ps[k % 2][:, rho, 0:K], ALU.add, ALU.mult).then_inc(y_done, 1)
                    s0 = 4 * (k % 2)
                    dve.wait_ge(y_done, 8 + 4 * (g + 1))
                    if not tail:
                        u = bass.ds(QUADS * q + k, 1)
                        w = Y[:, s0:s0 + D, 1 + K - 32:1 + K]
                        dve.tensor_tensor(w, w, s.causal[:, u, :].to_broadcast([P, D, 32]), ALU.min).then_inc(causal_done, 1)
                        dve.wait_ge(causal_done, g + 1)
                    dve.wait_ge(negm_done, g + 1)
                    dve.tensor_reduce(mx[:, :], Y[:, s0:s0 + D, 1:1 + K], AX_X, ALU.max).then_inc(mx_done, 1)
                    dve.wait_ge(mx_done, g + 1)
                    if k == 0:
                        dve.wait_ge(m_copied, q + 1)
                    dve.tensor_scalar(negm[:, i, 4 * k:4 * k + 4], mx[:, :], 0.0, -1 / TAU, ALU.max, ALU.mult
                                      ).then_inc(negm_done, 1)

                def weigh(q, i, k):
                    g = quads * q + k
                    for jt in range(JT):
                        dve.wait_ge(back, JT * g + jt + 1 + 2 * JT)
                        if k == 0 and jt == 0:
                            dve.wait_ge(av_mm, q + 1)
                        w = W[:, jt, bass.ds(D * D * (QUADS * q + k), D * D)].rearrange("p (r i) -> p r i", r=D)
                        dve.tensor_tensor(Pv[:, i, jt, :, :, k, :],
                                          p_ps[(JT * k + jt) % 2][:, :, :].rearrange("p (r i) h -> p r h i", r=D),
                                          w.unsqueeze(2).to_broadcast([P, D, HH, D]), ALU.mult).then_inc(p_done, 1)

                dve.wait_ge(w_done, UNITS)

                def body(q, i, first):
                    for k in range(quads):
                        recur(q, i, k, first)
                        if k:
                            weigh(q, i, k - 1)
                        elif not first:
                            weigh(q - 1, 1 - i, quads - 1)
                run(dve, body)
                weigh(chunks - 1, (chunks - 1) % 2, quads - 1)

            @block.scalar
            def _(act):
                act.sem_inc(x_out, 1)
                act.sem_inc(exp_done, 8)
                act.sem_inc(o_out, 1)
                act.wait_ge(zeroed, ZEROED)
                for jt in range(JT):
                    for rho in range(D):
                        act.wait_ge(arg_done, jt * D + rho + 1)
                        act.activation(W[:, jt, :].rearrange("p (u r i) -> p u r i", r=D, i=D)[:, :, rho, :],
                                       s.warg[:, jt, rho, :].rearrange("p (u i) -> p u i", i=D), ACT.Exp).then_inc(w_done, 1)

                def lay_out(q, i, rho):
                    for jt in range(JT):
                        act.wait_ge(sc_mm, UNITS * q + rho * JT + jt + 1 + 2 * UNITS)
                        if rho == 0 and jt == 0:
                            act.wait_ge(turned, quads * (q - 1) + 8)
                        act.activation(X[i][:, rho, jt, :, :].rearrange("p n (i h) -> p (n i) h", h=HH),
                                       s_ps[:, :, :].rearrange("p h n -> p n h"), ACT.Copy).then_inc(x_out, 1)

                def exps(q, i, k):
                    g = quads * q + k
                    act.wait_ge(negm_done, g + 1 + 1)
                    act.wait_ge(back, JT * (g + 1))
                    for rho in range(D):
                        act.activation(E[:, k % 2, rho, 0:K], Y[:, 4 * (k % 2) + rho, 1:1 + K], ACT.Exp,
                                       bias=negm[:, i, 4 * k + rho:4 * k + rho + 1], scale=1 / TAU).then_inc(exp_done, 1)

                def output(q, i):
                    act.wait_ge(av_mm, q + 1 + 2)
                    view = s.O[:, :, :].rearrange("p g (i w) -> p g w i", i=D)
                    act.activation(view[:, :, bass.ds(D - 1 + CHUNK * q, CHUNK), :], o_ps[:, :, :, :], ACT.Copy
                                   ).then_inc(o_out, 1)

                for rho in range(D):
                    lay_out(0, 0, rho)

                def body(q, i, first):
                    for k in range(quads):
                        if not tail:
                            for rho in AHEAD[k]:
                                lay_out(q + 1, 1 - i, rho)
                        exps(q, i, k)
                        if k == 2 and not first:
                            output(q - 1, 1 - i)
                run(act, body)
                output(chunks - 1, (chunks - 1) % 2)


def scan_finish(nc, t, s, grp, seg, d_resid):
    tail = seg == T // SEG
    tag = f"f{grp}s{seg}_"
    n_steps = D if tail else SEG
    w0 = D - 1 if seg == 0 else 0
    w1 = D - 1 if tail else SEG
    NW = w1 - w0
    with ExitStack() as ctx:
        def sb(name, shape, dt=F32):
            return ctx.enter_context(nc.sbuf_tensor(tag + name, shape, dt))

        sem = Semaphores(nc, tag)
        ctx.callback(sem.give_back)

        def psum(name, shape):
            return ctx.enter_context(nc.psum_tensor(tag + name, shape, F32))

        full = s.mx_full
        F = s.F
        tmp = [s.X[1][:, k, 0, :, :] for k in range(2)]
        r = s.X[0][:, 0, 0, :, :].rearrange("p n c -> p (n c)").rearrange("p (b w) -> p b w", b=NB)
        o = s.X[0][:, 1, 0, :, :].rearrange("p n c -> p (n c)").rearrange("p (b w) -> p b w", b=NB)
        rd = s.X[0][:, 2, 0, :, :].rearrange("p n c -> p (n c)").rearrange("p (b w) -> p b w", b=NB)
        m_ps = psum("m", [HH, D, SEG])
        f_ps = [psum(f"f{i}", [P, D, SEG]) for i in range(2)]
        num = psum("num", [P, NB, SEG])
        den = psum("den", [P, NB, SEG])
        loaded, stored = sem("loaded"), sem("stored")
        moved, mins, less, f_done, spread, scaled, half, summed, mm, rec, quot, added, shifted = (
            sem("moved"), sem("mins"), sem("less"), sem("f_done"), sem("spread"), sem("scaled"), sem("half"),
            sem("summed"), sem("mm"), sem("rec"), sem("quot"), sem("added"), sem("shifted"))
        by_step = lambda ap: ap.rearrange("p (i w) -> p i w", i=D)
        rows = s.Mw[:, 0:D * OP].rearrange("p (i w) -> p i w", i=D)
        res = d_resid[:, :].rearrange("p (b c) -> p b c", b=B)[:, grp * NB:(grp + 1) * NB,
                                                             seg * SEG - (D - 1) + w0:seg * SEG - (D - 1) + w1]
        with nc.Block() as block:
            @block.sync
            def _(sp):
                sp.dma_start(r[:, :, w0:w1], res).then_inc(loaded, 16)
                sp.wait_ge(added, 1)
                sp.dma_start(res, r[:, :, w0:w1]).then_inc(stored, 16)
                sp.wait_ge(stored, 16)

            @block.tensor
            def _(pe):
                for i in range(D):
                    mm_ = pe.matmul(m_ps[:, i, 0:n_steps], t.mat("ident")[:, i * HH:(i + 1) * HH], s.Mseg[:, 0:n_steps],
                                    start=True, stop=True)
                mm_.then_inc(mm, 1)
                pe.wait_ge(f_done, 1)

                def spread_out(g):
                    if g >= 2:
                        pe.wait_ge(scaled, g - 1)
                    pe.matmul(f_ps[g % 2][:, :, :], s.sel[:, g, :], F[:, :, :], start=True, stop=True).then_inc(spread, 1)

                spread_out(0)
                for g in range(2 * NB):
                    if g + 1 < 2 * NB:
                        spread_out(g + 1)
                    pe.wait_ge(summed, g + 1)
                    b, hg = g // 2, g % 2
                    pe.matmul(num[:, b, :], s.wo[:, hg, :], tmp[g % 2][:, 0, :], start=hg == 0, stop=hg == 1)
                    mm_ = pe.matmul(den[:, b, :], t.mat(f"den{hg}"), tmp[g % 2][:, 0, :], start=hg == 0, stop=hg == 1)
                    mm_.then_inc(mm, 1)

            @block.vector
            def _(dve):
                dve.wait_ge(mm, 1)
                dve.tensor_copy(by_step(s.Mw[:, :])[:, :, D - 1:D - 1 + n_steps], m_ps[:, :, 0:n_steps]).then_inc(moved, 1)
                dve.wait_ge(moved, 1)
                dve.tensor_tensor(full[:, 0, :], rows[:, 0, 3:3 + SEG], rows[:, 1, 3:3 + SEG], ALU.min).then_inc(mins, 1)
                dve.tensor_tensor(full[:, 1, :], rows[:, 2, 3:3 + SEG], rows[:, 3, 3:3 + SEG], ALU.min).then_inc(mins, 1)
                dve.wait_ge(mins, 2)
                dve.tensor_tensor(full[:, 2, :], full[:, 0, :], full[:, 1, :], ALU.min).then_inc(mins, 1)
                dve.wait_ge(mins, 3)
                dve.tensor_tensor(F[:, :, :], full[:, 2:3, :].to_broadcast([HH, D, SEG]), rows[:, :, 3:3 + SEG],
                                  ALU.subtract).then_inc(less, 1)
                for g in range(2 * NB):
                    dve.wait_ge(spread, g + 1)
                    if g >= 2:
                        dve.wait_ge(mm, g)
                    o_rows = s.O[:, g, 0:D * OP].rearrange("p (i w) -> p i w", i=D)
                    dve.tensor_tensor(tmp[g % 2][:, :, :], f_ps[g % 2][:, :, :], o_rows[:, :, 3:3 + SEG], ALU.mult
                                      ).then_inc(scaled, 1)
                dve.wait_ge(mm, 1 + 2 * NB)
                dve.reciprocal(rd[:, :, w0:w1], den[:, :, w0:w1]).then_inc(rec, 1)
                dve.wait_ge(rec, 1)
                dve.tensor_tensor(o[:, :, w0:w1], num[:, :, w0:w1], rd[:, :, w0:w1], ALU.mult).then_inc(quot, 1)
                dve.wait_ge(quot, 1)
                dve.wait_ge(loaded, 16)
                dve.tensor_tensor(r[:, :, w0:w1], o[:, :, w0:w1], r[:, :, w0:w1], ALU.add).then_inc(added, 1)
                if not tail:
                    dve.tensor_copy(by_step(s.Mw[:, :])[:, :, 0:D - 1], by_step(s.Mw[:, :])[:, :, SEG:SEG + D - 1]
                                    ).then_inc(shifted, 1)
                    ov = s.O[:, :, :].rearrange("p g (i w) -> p g i w", i=D)
                    dve.tensor_copy(ov[:, :, :, 0:D - 1], ov[:, :, :, SEG:SEG + D - 1]).then_inc(shifted, 1)

            @block.gpsimd
            def _(pool):
                for g in range(2 * NB):
                    x = tmp[g % 2]
                    pool.wait_ge(scaled, g + 1)
                    pool.tensor_tensor(x[:, 0:2, :], x[:, 0:2, :], x[:, 2:4, :], ALU.add).then_inc(half, 1)
                    pool.wait_ge(half, g + 1)
                    pool.tensor_tensor(x[:, 0, :], x[:, 0, :], x[:, 1, :], ALU.add).then_inc(summed, 1)

            @block.scalar
            def _(act):
                act.wait_ge(less, 1)
                act.activation(F[:, :, :], F[:, :, :], ACT.Exp).then_inc(f_done, 1)


def layer3_attention(nc, t, io, d_resid):
    spill_residual(nc, t, d_resid, 0)
    with ExitStack() as ctx:
        s = Scan(nc, ctx)
        loads = [(s.w3[:, :], io["w3"]), (s.head_mask[:, :], io["head_mask"]), (s.col[:, :], io["col"]),
                 (s.inv[:, :], io["inv"]), (s.causal[:, :, :], io["causal"]), (s.sel[:, :, :], io["spread"]),
                 (s.wo[:, :, :], io["wo"])]
        with nc.semaphore("s_loaded") as loaded, nc.Block() as block:
            @block.sync
            def _(sp):
                for dst, src in loads:
                    sp.dma_start(dst, src).then_inc(loaded, 16)
                sp.wait_ge(loaded, 16 * len(loads))

            @block.gpsimd
            def _(pool):
                pool.memset(t.xnp[:, 0:XPAD], 0.0)
                pool.memset(t.xnp[:, XPAD + N:], 0.0)
        for grp in range(B // NB):
            scan_projection(nc, t, s, grp)
            with ExitStack() as work:
                s.add_work(nc, work, grp)
                for seg in range(T // SEG + 1):
                    scan_segment(nc, t, s, grp, seg)
                    scan_finish(nc, t, s, grp, seg, d_resid)
    spill_residual(nc, t, d_resid, 1)


NEX = 8
SINKHORN = 8
CLIP = 1e-6


def sinkhorn_gates(nc, t, f):
    with ExitStack() as ctx:
        def sb(name, shape, dt=F32):
            return ctx.enter_context(nc.sbuf_tensor("k_" + name, shape, dt))

        sem = Semaphores(nc, "k_")
        ctx.callback(sem.give_back)

        BE = B * NEX
        ones = sb("ones", [P, P])
        gate = sb("gate", [P, NT, B, NEX])
        rcol = sb("rcol", [P, B, NEX])
        rsum = sb("rsum", [P, NT, B])
        rrow = sb("rrow", [P, NT, B])
        G = sb("G", [BE, T])
        left = [sb(f"left{i}", [BE, T]) for i in range(2)]
        top = sb("top", [BE, 8])
        need = sb("need", [BE, 2])
        above = sb("above", [BE, T])
        equal = sb("equal", [BE, T])
        rank = sb("rank", [BE, T])
        chosen = sb("chosen", [P, NT, B, NEX])
        free = sb("free", [P, NT, B, NEX])
        rest = sb("rest", [P, NT, B, NEX])
        l_ps = ctx.enter_context(nc.psum_tensor("k_l", [P, NT, B, NEX], F32))
        c_ps = ctx.enter_context(nc.psum_tensor("k_c", [P, HALF // NEX, NEX], F32))
        g_ps = ctx.enter_context(nc.psum_tensor("k_g", [BE, T], F32))
        loaded, const, mm, step, colsum, turned, picked, chain, back = (
            sem("loaded"), sem("const"), sem("mm"), sem("step"), sem("colsum"), sem("turned"), sem("picked"), sem("chain"), sem("back"))
        with nc.Block() as block:
            @block.sync
            def _(sp):
                sp.dma_start(f.gate_w[:, :], f.io["ffn_gate"]).then_inc(loaded, 16)
                sp.dma_start(f.experts[:, :, :], f.io["ffn_experts"]).then_inc(loaded, 16)
                sp.wait_ge(loaded, 32)

            @block.gpsimd
            def _(pool):
                pool.memset(ones[:, :], 1.0).then_inc(const, 1)

            @block.tensor
            def _(pe):
                pe.wait_ge(loaded, 32)
                pe.wait_ge(const, 1)
                for b in range(B):
                    for j in range(NT):
                        c0 = b * T + j * P
                        mm_ = pe.matmul(l_ps[:, j, b, :], t.xn[:, c0:c0 + P], f.gate_w[:, :], start=True, stop=True)
                mm_.then_inc(mm, 1)
                for n in range(SINKHORN):
                    pe.wait_ge(step, n + 1)
                    for j in range(NT):
                        mm_ = pe.matmul(c_ps[:, 0:B, :], ones[:, :], gate[:, j, :, :], start=j == 0, stop=j == NT - 1)
                    mm_.then_inc(colsum, 1)
                pe.wait_ge(step, SINKHORN + 1)
                for j in range(NT):
                    tr = pe.transpose(g_ps[:, j * P:(j + 1) * P], gate[:, j, :, :], t.mat("ident"))
                tr.then_inc(turned, 1)
                pe.wait_ge(picked, 1)
                for j in range(NT):
                    tr = pe.transpose(l_ps[:, j, :, :], above[:, j * P:(j + 1) * P], t.mat("ident")[0:BE, 0:BE])
                tr.then_inc(back, 1)

            @block.vector
            def _(dve):
                dve.wait_ge(mm, 1)
                dve.tensor_scalar(gate[:, :, :, :], l_ps[:, :, :, :], CLIP, None, ALU.max).then_inc(step, 1)
                for n in range(SINKHORN):
                    dve.wait_ge(colsum, n + 1)
                    dve.reciprocal(rcol[:, :, :], c_ps[:, 0:B, :]).then_inc(chain, 1)
                    dve.wait_ge(chain, 4 * n + 1)
                    dve.tensor_tensor(gate[:, :, :, :], gate[:, :, :, :],
                                      rcol[:, :, :].unsqueeze(1).to_broadcast([P, NT, B, NEX]), ALU.mult).then_inc(chain, 1)
                    dve.wait_ge(chain, 4 * n + 2)
                    dve.tensor_reduce(rsum[:, :, :], gate[:, :, :, :], AX_X, ALU.add).then_inc(chain, 1)
                    dve.wait_ge(chain, 4 * n + 3)
                    dve.reciprocal(rrow[:, :, :], rsum[:, :, :]).then_inc(chain, 1)
                    dve.wait_ge(chain, 4 * n + 4)
                    dve.tensor_tensor(gate[:, :, :, :], gate[:, :, :, :],
                                      rrow[:, :, :].unsqueeze(3).to_broadcast([P, NT, B, NEX]), ALU.mult).then_inc(step, 1)
                    dve.wait_ge(step, n + 2)
                c = 4 * SINKHORN
                dve.wait_ge(turned, 1)
                dve.tensor_copy(G[:, :], g_ps[:, :]).then_inc(chain, 1)
                dve.wait_ge(chain, c + 1)
                c += 1
                ROUNDS = T // NEX // 8
                for n in range(ROUNDS):
                    src = left[(n - 1) % 2] if n else G
                    dve.max(top[:, :], src[:, :]).then_inc(chain, 1)
                    dve.wait_ge(chain, c + 1)
                    c += 1
                    if n < ROUNDS - 1:
                        dve.match_replace(left[n % 2][:, :], top[:, :], src[:, :], -1.0).then_inc(chain, 1)
                        dve.wait_ge(chain, c + 1)
                        c += 1
                thr = top[:, 7:8]
                dve.tensor_scalar(above[:, :], G[:, :], thr, None, ALU.is_gt).then_inc(chain, 1)
                dve.tensor_scalar(equal[:, :], G[:, :], thr, None, ALU.is_equal).then_inc(chain, 1)
                dve.wait_ge(chain, c + 2)
                dve.tensor_reduce(need[:, 0:1], above[:, :], AX_X, ALU.add).then_inc(chain, 1)
                dve.tensor_tensor_scan(rank[:, :], equal[:, :], equal[:, :], 0.0, ALU.add, ALU.max).then_inc(chain, 1)
                dve.wait_ge(chain, c + 4)
                dve.tensor_scalar(need[:, 1:2], need[:, 0:1], -1.0, T / NEX, ALU.mult, ALU.add).then_inc(chain, 1)
                dve.wait_ge(chain, c + 5)
                dve.scalar_tensor_tensor(rank[:, :], rank[:, :], need[:, 1:2], equal[:, :], ALU.is_le, ALU.mult).then_inc(chain, 1)
                dve.wait_ge(chain, c + 6)
                dve.tensor_tensor(above[:, :], above[:, :], rank[:, :], ALU.add).then_inc(picked, 1)
                c += 6
                dve.wait_ge(back, 1)
                dve.tensor_copy(chosen[:, :, :, :], l_ps[:, :, :, :]).then_inc(chain, 1)
                dve.wait_ge(chain, c + 1)
                dve.tensor_scalar(free[:, :, :, :], chosen[:, :, :, :], -1.0, 1.0, ALU.mult, ALU.add).then_inc(chain, 1)
                dve.memset(rest[:, :, :, NEX - 1:NEX], 1.0).then_inc(chain, 1)
                c += 3
                for e in range(NEX - 2, -1, -1):
                    dve.wait_ge(chain, c)
                    dve.tensor_tensor(rest[:, :, :, e], rest[:, :, :, e + 1], free[:, :, :, e + 1], ALU.mult).then_inc(chain, 1)
                    c += 1
                dve.tensor_tensor(chosen[:, :, :, :], chosen[:, :, :, :], gate[:, :, :, :], ALU.mult).then_inc(chain, 1)
                dve.wait_ge(chain, c + 1)
                dve.tensor_tensor(f.weight[:, :, :, :], chosen[:, :, :, :], rest[:, :, :, :], ALU.mult)


def routed_experts(nc, t, f):
    with ExitStack() as ctx:
        def sb(name, shape, dt=F32):
            return ctx.enter_context(nc.sbuf_tensor("e_" + name, shape, dt))

        def psum(name, shape):
            return ctx.enter_context(nc.psum_tensor("e_" + name, shape, F32))

        sem = Semaphores(nc, "e_")
        ctx.callback(sem.give_back)
        xb = [sb(f"xb{i}", [P, T]) for i in range(2)]
        prod = [sb(f"prod{i}", [P, NEX, P]) for i in range(2)]
        y_ps = [psum(f"y{i}", [P, NEX, P]) for i in range(2)]
        z_ps = [psum(f"z{i}", [P, HALF]) for i in range(2)]
        copied, mm_y, prod_done, mm_z, added, woke = (
            sem("copied"), sem("mm_y"), sem("prod_done"), sem("mm_z"), sem("added"), sem("woke"))
        with nc.Block() as block:
            @block.gpsimd
            def _(pool):
                def body(b, i):
                    pool.wait_ge(mm_y, NT * (b + 1))
                    pool.sem_inc(woke, 1)
                    pool.tensor_copy(xb[i][:, :], t.xn[:, bass.ds(b * T, T)]).then_inc(copied, 1)
                pairs(pool, body)

            @block.tensor
            def _(pe):
                pe.sem_inc(mm_y, 2 * NT)
                pe.sem_inc(mm_z, 2)

                def project(b, i, j):
                    pe.wait_ge(prod_done, NT * b + j + 1)
                    for k in range(2):
                        mm = pe.matmul(y_ps[j % 2][:, 4 * k:4 * k + 4, :], xb[i][:, j * P:(j + 1) * P],
                                       f.experts[:, 4 * k:4 * k + 4, :], start=True, stop=True)
                    mm.then_inc(mm_y, 1)

                def turn(b, i, j):
                    pe.wait_ge(prod_done, NT * b + j + 1 + 2)
                    if j % 4 == 0:
                        pe.wait_ge(added, 2 * b + j // 4 + 1)
                    for e in range(NEX):
                        mm = pe.matmul(z_ps[j // 4][:, (j % 4) * P:(j % 4 + 1) * P], prod[j % 2][:, e, :], t.mat("ident"),
                                       start=e == 0, stop=e == NEX - 1)
                    mm.then_inc(mm_z, 1)

                def body(b, i):
                    pe.wait_ge(copied, b + 1)
                    project(b, i, 0)
                    for j in range(NT):
                        if j < NT - 1:
                            project(b, i, j + 1)
                        turn(b, i, j)
                pairs(pe, body)

            @block.vector
            def _(dve):
                dve.sem_inc(prod_done, 2)
                dve.sem_inc(added, 2)

                def body(b, i):
                    for j in range(NT):
                        n = NT * b + j
                        dve.wait_ge(mm_y, n + 1 + 2 * NT)
                        dve.wait_ge(mm_z, n + 1)
                        w = f.weight[:, j, bass.ds(b, 1), :].rearrange("p a e -> p (a e)")
                        dve.tensor_tensor(prod[j % 2][:, :, :], y_ps[j % 2][:, :, :],
                                          w.unsqueeze(2).to_broadcast([P, NEX, P]), ALU.mult).then_inc(prod_done, 1)
                        if j == 5:
                            add(b, 0)
                    add(b, 1)

                def add(b, h):
                    dve.wait_ge(mm_z, NT * b + 4 * (h + 1) + 2)
                    r = t.resid[:, bass.ds(b * T + h * HALF, HALF)]
                    dve.tensor_tensor(r, z_ps[h][:, :], r, ALU.add).then_inc(added, 1)
                pairs(dve, body)


class RoutedTensors:
    def __init__(self, nc, ctx, io):
        self.io = io
        self.gate_w = ctx.enter_context(nc.sbuf_tensor("r_gate_w", [P, NEX], F32))
        self.experts = ctx.enter_context(nc.sbuf_tensor("r_experts", [P, NEX, P], F32))
        self.weight = ctx.enter_context(nc.sbuf_tensor("r_weight", [P, NT, B, NEX], F32))


def layer3_ffn(nc, t, io):
    with ExitStack() as ctx:
        f = RoutedTensors(nc, ctx, io)
        sinkhorn_gates(nc, t, f)
        routed_experts(nc, t, f)


def store_result(nc, t, out):
    with nc.semaphore("stored") as stored, nc.Block() as block:
        @block.sync
        def _(sp):
            for b in range(B):
                sp.dma_start(out[b], t.resid[:, b * T:(b + 1) * T]).then_inc(stored, 16)
            sp.wait_ge(stored, 16 * B)


class Tensors:

    def __init__(self, nc, ctx):
        def sb(name, shape, dt=F32):
            return ctx.enter_context(nc.sbuf_tensor(name, shape, dt))
        self.resid = sb("resid", [P, N])
        self.vecs = sb("vecs", [P, len(VECS)])
        self.mats = sb("mats", [P, len(MATS) * P])
        self.gscale = sb("gscale", [P, B])
        self.gshift = sb("gshift", [P, B])
        self.projb = sb("projb", [P, 1])

    def add_xn(self, nc, ctx):
        self.xnp = ctx.enter_context(nc.sbuf_tensor("xnp", [P, XPAD + N + XPAD], F32))
        self.xn = self.xnp[:, XPAD:XPAD + N]

    def vec(self, name):
        return self.vecs[:, VI[name]:VI[name] + 1]

    def mat(self, name):
        return self.mats[:, MI[name] * P:(MI[name] + 1) * P]


def build(nc, io, out):
    d_parts = nc.dram_tensor("d_parts", (2, 3, P, T), BF16, kind="Internal").ap()
    d_max = nc.dram_tensor("d_max", (MROWS, HEADS * T), BF16, kind="Internal").ap()
    d_resid = nc.dram_tensor("d_resid", (P, N), F32, kind="Internal").ap()
    with ExitStack() as ctx:
        t = Tensors(nc, ctx)
        loads = [(t.vecs[:, :], io["vecs"]), (t.mats[:, :], io["mats"])]
        loads += [(t.resid[:, b * T:(b + 1) * T], io["x"][b]) for b in range(B)]
        group_norm(nc, t, "n0", ("norm_w", "norm_b"), loads)
        layer0_attention(nc, t, d_parts, d_max)
        group_norm(nc, t, "n1", None)
        layer1_conv(nc, t)
        t.add_xn(nc, ctx)
        token_norm(nc, t, "n2", "eps5")
        layer2_attention(nc, t)
        token_norm(nc, t, "n3", "eps5")
        moe(nc, t, io["router"], io["gate_up"], io["down"], io["sel"])
        token_norm(nc, t, "n4", "eps5")
        layer3_attention(nc, t, io, d_resid)
        token_norm(nc, t, "n5", "eps5")
        layer3_ffn(nc, t, io)
        store_result(nc, t, out)


def constants():
    ident = np.eye(P, dtype=np.float32)
    gavg = np.kron(np.eye(32), np.full((4, 4), 0.25)).astype(np.float32)
    mats = {"ident": ident, "gavg": gavg}
    for hg in range(2):
        num, den = np.zeros((P, P), np.float32), np.zeros((P, P), np.float32)
        for h4 in range(4):
            for d in range(HD):
                num[32 * h4 + d, (4 * hg + h4) * HD + d] = 1
                den[32 * h4 + HD, (4 * hg + h4) * HD + d] = 1
        mats[f"num{hg}"], mats[f"den{hg}"] = num, den
    return mats


def scan_constants():
    part = np.arange(P)
    col = np.stack([D * (P * jt + part) + rho for jt in range(2) for rho in range(D)], 1).astype(np.float32)
    r = np.arange(T + SEG + D) - (D - 1)
    inv = np.where(r >= 0, 10.0 / np.maximum(r + 1, 1), 0).astype(np.float32)
    u, j = np.arange(32)[:, None], np.arange(32)[None, :]
    last_row = (part >= (D - 1) * HH)[:, None, None]
    causal = np.where(np.where(last_row, j <= u, j <= u - 1), np.float32(1e30), np.float32(-1e30)).astype(np.float32)
    spread = np.zeros((HH, 2 * NB, P), np.float32)
    for g in range(2 * NB):
        for h4 in range(4):
            spread[4 * g + h4, g, 32 * h4:32 * (h4 + 1)] = 1
    head_mask = np.kron(np.eye(HEADS), np.ones((HD, 1))).astype(np.float32)
    return {"col": col, "inv": np.ascontiguousarray(np.broadcast_to(inv, (P, len(inv)))), "causal": causal,
            "spread": spread, "head_mask": head_mask}


def layout(inputs):
    i = {k: np.asarray(v) for k, v in inputs.items()}
    w = i["L0_conv_qkv_w"].reshape(HEADS, 3, HD, C).transpose(1, 0, 2, 3).reshape(3, C, C)
    qb = i["L0_conv_qkv_b"].reshape(HEADS, 3, HD).transpose(1, 0, 2).reshape(3, C)
    vec = {"norm_w": i["L0_conv_norm_w"], "norm_b": i["L0_conv_norm_b"], "q_b": qb[0], "k_b": qb[1], "v_b": qb[2],
           "proj_b": i["L0_conv_proj_b"], "dw_b": i["L1_conv_dw_b"], "pw_b": i["L1_conv_pw_b"]}
    for n in range(9):
        vec[f"dw{n}"] = i["L1_conv_dw_w"].reshape(C, 9)[:, n]
    for n in ("bn1", "bn2"):
        for s in "gbmv":
            vec[f"{n}_{s}"] = i[f"L1_conv_{n}_{s}"]
    vec["eps5"] = np.full(C, EPS5, np.float32)
    mats = constants()
    mats |= {"qT": w[0].T, "kT": w[1].T, "vT": w[2].T, "projT": i["L0_conv_proj_w"].T,
             "pwT": i["L1_conv_pw_w"].reshape(C, C).T,
             "Wq": i["L2_attn_Wq"], "Wk": i["L2_attn_Wk"], "WvT": i["L2_attn_Wv"].T}
    NE = i["L2_ffn_router_w"].shape[0]
    gate_up = np.stack([i["L2_ffn_gate_w"], i["L2_ffn_up_w"]]).transpose(2, 1, 0, 3)
    down = i["L2_ffn_down_w"].reshape(NE, 2, P, C).transpose(2, 0, 1, 3)
    w3 = np.concatenate([i["L3_attn_wq"], i["L3_attn_wk"], i["L3_attn_wv"]], 1)
    wo = np.zeros((P, 2, P), np.float32)
    for h in range(HEADS):
        wo[32 * (h % 4):32 * (h % 4) + HD, h // 4, h * HD:(h + 1) * HD] = i["L3_attn_wo"].reshape(HEADS, HD, HD)[h]
    return {"x": i["x"].reshape(B, C, T), "w3": np.ascontiguousarray(w3), "wo": wo, **scan_constants(),
            "ffn_gate": i["L3_ffn_gate_weight"].reshape(C, NEX),
            "ffn_experts": np.ascontiguousarray(i["L3_ffn_experts"].transpose(1, 0, 2)),
            "router": np.ascontiguousarray(i["L2_ffn_router_w"].T),
            "gate_up": np.ascontiguousarray(gate_up), "down": np.ascontiguousarray(down),
            "sel": np.ascontiguousarray(np.repeat(np.eye(NE, dtype=np.float32)[:, :, None], P, 2)),
            "vecs": np.ascontiguousarray(np.stack([vec[n] for n in VECS], 1)),
            "mats": np.ascontiguousarray(np.concatenate([mats[n] for n in MATS], 1))}


def kernel(**inputs):
    import concourse.bacc as bacc
    from concourse.bass_utils import run_bass_kernel_spmd

    nc = bacc.Bacc("TRN2", target_bir_lowering=False, num_devices=1)
    arrays = layout(inputs)
    io = {n: nc.dram_tensor(f"in_{n}", a.shape, mybir.dt.from_np(a.dtype), kind="ExternalInput").ap()
          for n, a in arrays.items()}
    out = nc.dram_tensor("out_0_dram", (B, C, T), F32, kind="ExternalOutput").ap()
    build(nc, io, out)
    r = run_bass_kernel_spmd(nc, [{f"in_{n}": a for n, a in arrays.items()}], core_ids=[0])
    return r.results[0]["out_0_dram"].reshape(B, C, 32, 32)
```

```python
from contextlib import ExitStack

import numpy as np

import concourse.bass as bass
from concourse import mybir

F32 = mybir.dt.float32
BF16 = mybir.dt.bfloat16
U32 = mybir.dt.uint32
ALU = mybir.AluOpType
ACT = mybir.ActivationFunctionType
AX_X = mybir.AxisListType.X

B, C, T = 8, 128, 1024
N = B * T
P = 128
HEADS, HD = 8, 16
NT = T // P
HALF = 512
EPS5, EPS6 = 1e-5, 1e-6

VECS = ["norm_w", "norm_b", "q_b", "k_b", "v_b", "proj_b"] + [f"dw{i}" for i in range(9)] + [
    "dw_b", "bn1_g", "bn1_b", "bn1_m", "bn1_v", "pw_b", "bn2_g", "bn2_b", "bn2_m", "bn2_v", "eps5"]
VI = {n: i for i, n in enumerate(VECS)}
MATS = ["ident", "gavg", "num0", "num1", "den0", "den1", "qT", "kT", "vT", "projT", "pwT",
        "Wq", "Wk", "WvT"]
MI = {n: i for i, n in enumerate(MATS)}

Q_PARTS = [0, 0, 1, 1, 0, 2]
K_PARTS = [0, 1, 0, 1, 2, 0]
NPROD = len(Q_PARTS)
KROWS = NPROD * HD
MROWS = 2
XPAD = 16


def group_norm(nc, t, tag, affine, loads=()):
    with ExitStack() as ctx:
        def sb(name, shape, dt=F32):
            return ctx.enter_context(nc.sbuf_tensor(tag + name, shape, dt))

        def sem(name):
            return ctx.enter_context(nc.semaphore(tag + name))

        stats = sb("g_stats", [P, B, 2, 6])
        mv = sb("g_mv", [P, B, 2])
        dev = sb("g_dev", [P, B])
        work = sb("g_work", [P, B])
        ps = ctx.enter_context(nc.psum_tensor(tag + "g_ps", [P, HALF], F32))
        x_in, w_in = [sem(f"g_x{b}") for b in range(B)], sem("g_w")
        chain, avg = sem("g_chain"), sem("g_avg")
        ready, root = sem("g_ready"), sem("g_root")
        with nc.Block() as block:
            @block.sync
            def _(sp):
                for dst, src in loads[:-B]:
                    sp.dma_start(dst, src).then_inc(w_in, 16)
                for b, (dst, src) in enumerate(loads[-B:]):
                    sp.dma_start(dst, src).then_inc(x_in[b], 16)

            @block.vector
            def _(dve):
                for b in range(B):
                    if loads:
                        dve.wait_ge(x_in[b], 16)
                    for h in range(2):
                        c0 = b * T + h * HALF
                        dve.bn_stats(stats[:, b, h, :], t.resid[:, c0:c0 + HALF]).then_inc(chain, 1)
                dve.wait_ge(chain, 2 * B)
                for b in range(B):
                    dve.bn_aggr(mv[:, b, :], stats[:, b, :, :]).then_inc(chain, 1)
                dve.wait_ge(chain, 3 * B)
                if loads:
                    dve.wait_ge(w_in, 16 * (len(loads) - B))
                dve.tensor_copy(work[:, :], mv[:, :, 0]).then_inc(ready, 1)
                dve.wait_ge(avg, 1)
                dve.tensor_tensor(dev[:, :], mv[:, :, 0], ps[:, 0:B], ALU.subtract).then_inc(chain, 1)
                dve.tensor_copy(t.gshift[:, :], ps[:, 0:B]).then_inc(chain, 1)
                dve.wait_ge(chain, 3 * B + 2)
                dve.tensor_tensor(dev[:, :], dev[:, :], dev[:, :], ALU.mult).then_inc(chain, 1)
                dve.wait_ge(chain, 3 * B + 3)
                dve.tensor_tensor(work[:, :], dev[:, :], mv[:, :, 1], ALU.add).then_inc(ready, 1)
                dve.wait_ge(avg, 2)
                dve.tensor_scalar(work[:, :], ps[:, B:2 * B], EPS5, None, ALU.add).then_inc(ready, 1)
                dve.wait_ge(root, 1)
                dve.reciprocal(dev[:, :], work[:, :]).then_inc(ready, 1)
                dve.wait_ge(ready, 4)
                dve.tensor_scalar(t.gscale[:, :], dev[:, :], t.vec(affine[0]) if affine else 1.0, None, ALU.mult
                                  ).then_inc(chain, 1)
                dve.wait_ge(chain, 3 * B + 4)
                dve.tensor_tensor(work[:, :], t.gshift[:, :], t.gscale[:, :], ALU.mult).then_inc(chain, 1)
                dve.wait_ge(chain, 3 * B + 5)
                dve.tensor_scalar(t.gshift[:, :], work[:, :], -1.0, t.vec(affine[1]) if affine else 0.0,
                                  ALU.mult, ALU.add).then_inc(chain, 1)
                dve.tensor_tensor(t.projb[:, :], ps[:, 2 * B:2 * B + 1], t.vec("proj_b"), ALU.add)

            @block.scalar
            def _(act):
                act.wait_ge(ready, 3)
                act.activation(work[:, :], work[:, :], ACT.Sqrt).then_inc(root, 1)

            @block.tensor
            def _(pe):
                if loads:
                    pe.wait_ge(w_in, 16 * (len(loads) - B))
                pe.matmul(ps[:, 2 * B:2 * B + 1], t.mat("projT"), t.vec("v_b"), start=True, stop=True)
                pe.wait_ge(ready, 1)
                pe.matmul(ps[:, 0:B], t.mat("gavg"), work[:, :], start=True, stop=True).then_inc(avg, 1)
                pe.wait_ge(ready, 2)
                pe.matmul(ps[:, B:2 * B], t.mat("gavg"), work[:, :], start=True, stop=True).then_inc(avg, 1)


def layer0_attention(nc, t, d_parts, d_max):
    with ExitStack() as ctx:
        def sb(name, shape, dt=F32):
            return ctx.enter_context(nc.sbuf_tensor(name, shape, dt))

        def sem(name):
            return ctx.enter_context(nc.semaphore("a_" + name))

        xnb = sb("xnb", [P, T])
        parts = sb("parts", [P, 2, 3, T], BF16)
        rest = sb("rest", [P, 2, T])
        qs = [sb(f"qs{i}", [KROWS + MROWS, HEADS, T], BF16) for i in range(2)]
        ks = [sb(f"ks{i}", [KROWS + MROWS, HEADS, T], BF16) for i in range(2)]
        vx = [sb(f"vx{i}", [P, NT, HEADS, 32]) for i in range(2)]
        half_max = sb("half_max", [P, HEADS * NT, 2])
        row_max = sb("row_max", [P, P])
        neg_max = sb("neg_max", [HEADS * NT, MROWS, P], BF16)
        E = sb("E", [P, 2, 4, 2 * HALF])
        acc_sb = sb("acc_sb", [P, 2, HALF])
        rden = sb("rden", [P, HALF])
        attn = sb("attn", [P, HALF])

        def psum(name, n):
            return ctx.enter_context(nc.psum_tensor(name, [P, n], F32))

        sc = [psum(f"sc{i}", 2 * HALF) for i in range(2)]
        acc = psum("acc", HALF)
        misc = psum("misc", HALF)
        bm = [psum(f"bm{i}", HALF) for i in range(2)]

        ones_set = sem("ones")
        xn_ready, mm_a, hi_done, rest_done, v_done, low_done = (
            sem("xn_ready"), sem("mm_a"), sem("hi_done"), sem("rest_done"), sem("v_done"), sem("low_done"))
        parts_out, stacked = sem("parts_out"), sem("stacked")
        mm_b, max_done, rowmax_done, maxT, negmax_hi, negmax_done = (
            sem("mm_b"), sem("max_done"), sem("rowmax_done"), sem("maxT"), sem("negmax_hi"), sem("negmax_done"))
        max_out, max_in = sem("max_out"), sem("max_in")
        mm_c, exp_done, av_done, acc_out, mm_n, norm_done = (
            sem("mm_c"), sem("exp_done"), sem("av_done"), sem("acc_out"), sem("mm_n"), sem("norm_done"))
        woke = sem("woke")
        PIECES = 4
        UB = HEADS * NT * 2
        UC = 64
        GC = 16
        QW = [t.mat("qT"), t.mat("kT")]

        with nc.Block() as block:
            def pe_a(pe, b, par, i):
                n = b * 6 + i
                if i == 0:
                    pe.wait_ge(xn_ready, b + 1)
                if i < PIECES:
                    if i >= 2:
                        pe.wait_ge(rest_done, b * PIECES + i - 1)
                    else:
                        pe.wait_ge(maxT, b + 1)
                        pe.wait_ge(negmax_done, b + 1)
                    pe.matmul(bm[i % 2][:, :], QW[i // 2], xnb[:, (i % 2) * HALF:(i % 2 + 1) * HALF],
                              start=True, stop=True).then_inc(mm_a, 1)
                else:
                    pe.wait_ge(rest_done, b * PIECES + i - 1)
                    for j in range(4):
                        tile = (i - PIECES) * 4 + j
                        mm = pe.matmul(bm[i % 2][:, j * P:(j + 1) * P], xnb[:, tile * P:(tile + 1) * P],
                                       t.mat("vT"), start=True, stop=True)
                    mm.then_inc(mm_a, 1)

            def pe_b(pe, b, par, u):
                if u == 0:
                    pe.wait_ge(stacked, 16 * 12 * (b + 1))
                if u < 2:
                    pe.wait_ge(v_done, 2 * b + 1 + u)
                else:
                    pe.wait_ge(max_done, b * UB + u - 1)
                h, tile, k = u // (2 * NT), u // 2 % NT, u % 2
                pe.matmul(bm[u % 2][:, :], qs[par][0:KROWS, h, tile * P:(tile + 1) * P],
                          ks[par][0:KROWS, h, k * HALF:(k + 1) * HALF], start=True, stop=True).then_inc(mm_b, 1)

            def pe_b_end(pe, b):
                pe.wait_ge(rowmax_done, b + 1)
                pe.transpose(bm[0][:, 0:P], row_max[:, :], t.mat("ident")).then_inc(maxT, 1)

            def pe_scores(pe, b, par, g, between):
                th, hg, sp = g // 8, g // 4 % 2, g % 4
                for h4 in range(4):
                    u = 4 * g + h4
                    pe.wait_ge(exp_done, b * UC + u + 1)
                    for j in range(2):
                        s0 = (2 * sp + j) * P
                        mm = pe.matmul(sc[u % 2][:, j * HALF:(j + 1) * HALF], ks[par][:, 4 * hg + h4, s0:s0 + P],
                                       qs[par][:, 4 * hg + h4, th * HALF:(th + 1) * HALF], start=True, stop=True)
                    mm.then_inc(mm_c, 1)
                    between()

            def pe_av(pe, b, par, g, between):
                hg, sp = g // 4 % 2, g % 4
                pe.wait_ge(exp_done, b * UC + 4 * g + 4 + 2)
                if sp == 0:
                    pe.wait_ge(acc_out, b * 4 + g // 4 + 1)
                for j in range(2):
                    for h4 in range(4):
                        mm = pe.matmul(acc[32 * h4:32 * h4 + 32, :], vx[par][:, 2 * sp + j, 4 * hg + h4, :],
                                       E[:, g % 2, h4, j * HALF:(j + 1) * HALF],
                                       start=(sp == 0 and j == 0), stop=(sp == 3 and j == 1))
                        if j + h4 < 4:
                            between()
                mm.then_inc(av_done, 1)

            def pe_norm(pe, b, th, step):
                if step == 0:
                    pe.wait_ge(acc_out, b * 4 + 2 * th + 2 + 1)
                pe.wait_ge(norm_done, b * 6 + th * 3 + step + 1)
                if step < 2:
                    for hg in range(2):
                        mm = pe.matmul(misc[:, :], t.mat(f"{('den', 'num')[step]}{hg}"), acc_sb[:, hg, :],
                                       start=(hg == 0), stop=(hg == 1))
                else:
                    mm = pe.matmul(misc[:, :], t.mat("projT"), attn[:, :], start=True, stop=True)
                mm.then_inc(mm_n, 1)

            A_GROUPS = 6
            def b_units(g):
                n = GC - A_GROUPS
                return range(UB * (g - A_GROUPS) // n, UB * (g - A_GROUPS + 1) // n) if g >= A_GROUPS else range(0)

            def pe_iter(pe, b, par, more):
                for g in range(GC):
                    units = list(b_units(g)) if more else []

                    def between():
                        if units:
                            pe_b(pe, b + 1, 1 - par, units.pop(0))

                    pe_scores(pe, b, par, g, between)
                    if more and g < A_GROUPS:
                        pe_a(pe, b + 1, 1 - par, g)
                    if g:
                        pe_av(pe, b, par, g - 1, between)
                    while units:
                        between()
                    if g in (9, 10, 11):
                        pe_norm(pe, b, 0, g - 9)
                if more:
                    pe_b_end(pe, b + 1)
                pe_av(pe, b, par, GC - 1, lambda: None)
                for step in range(3):
                    pe_norm(pe, b, 1, step)

            def iterations(eng, body, first=None):
                with eng.Fori(0, B // 2 - 1) as pair:
                    body(eng, 2 * pair, 0, True)
                    body(eng, 2 * pair + 1, 1, True)
                body(eng, B - 2, 0, True)
                body(eng, B - 1, 1, False)

            @block.tensor
            def _(pe):
                for i in range(6):
                    pe_a(pe, 0, 0, i)
                for u in range(UB):
                    pe_b(pe, 0, 0, u)
                pe_b_end(pe, 0)
                pe.wait_ge(max_in, 16)
                iterations(pe, lambda e, b, par, more: (pe_iter(e, b, par, more),
                           e.wait_ge(max_in, 16 * (b + 2)) if more else None))

            def dve_xn(dve, b):
                dve.wait_ge(mm_a, b * 6 + 1)
                dve.tensor_scalar(xnb[:, :], t.resid[:, bass.ds(b * T, T)], t.gscale[:, bass.ds(b, 1)],
                                  t.gshift[:, bass.ds(b, 1)], ALU.mult, ALU.add).then_inc(xn_ready, 1)

            def dve_a(dve, b, par, i):
                if i < PIECES:
                    w, h = i // 2, i % 2
                    dve.wait_ge(hi_done, b * PIECES + i + 1)
                    dve.wait_ge(parts_out, 16 * (b + 1))
                    dve.scalar_tensor_tensor(rest[:, w, h * HALF:(h + 1) * HALF], bm[i % 2][:, :],
                                             t.vec(("q_b", "k_b")[w]), parts[:, w, 0, h * HALF:(h + 1) * HALF],
                                             ALU.add, ALU.subtract).then_inc(rest_done, 1)
                else:
                    j = i - PIECES
                    dve.wait_ge(mm_a, b * 6 + i + 1 + 1)
                    dve.tensor_copy(vx[par][:, 4 * j:4 * j + 4, :, 0:HD],
                                    bm[i % 2][:, :].rearrange("p (t h d) -> p t h d", t=4, h=HEADS)
                                    ).then_inc(v_done, 1)

            def dve_b(dve, b, u):
                dve.wait_ge(mm_b, b * UB + u + 1)
                dve.tensor_reduce(half_max[:, u // 2, u % 2:u % 2 + 1], bm[u % 2][:, :], AX_X, ALU.max
                                  ).then_inc(max_done, 1)

            def dve_b_end(dve, b):
                dve.wait_ge(max_done, b * UB + UB)
                dve.wait_ge(maxT, b + 1)
                dve.tensor_tensor(row_max[:, 0:HEADS * NT], half_max[:, :, 0], half_max[:, :, 1], ALU.max
                                  ).then_inc(rowmax_done, 1)

            def dve_b_low(dve, b):
                dve.wait_ge(negmax_hi, b + 1)
                dve.scalar_tensor_tensor(neg_max[:, 1, :], bm[0][0:HEADS * NT, 0:P], -1.0, neg_max[:, 0, :],
                                         ALU.mult, ALU.subtract).then_inc(negmax_done, 1)

            def dve_acc(dve, b, q):
                dve.wait_ge(av_done, b * GC + 4 * q + 4 + 2)
                if q % 2 == 0:
                    dve.wait_ge(norm_done, b * 6 + (q // 2) * 3 + 1)
                dve.tensor_copy(acc_sb[:, q % 2, :], acc[:, :]).then_inc(acc_out, 1)

            def dve_norm(dve, b, th, step):
                n = b * 6 + th * 3 + step
                dve.wait_ge(mm_n, n + 1)
                if step == 0:
                    dve.reciprocal(rden[:, :], misc[:, :]).then_inc(norm_done, 1)
                elif step == 1:
                    dve.wait_ge(norm_done, n + 1)
                    dve.tensor_tensor(attn[:, :], misc[:, :], rden[:, :], ALU.mult).then_inc(norm_done, 1)
                else:
                    r = t.resid[:, bass.ds(b * T + th * HALF, HALF)]
                    dve.scalar_tensor_tensor(r, misc[:, :], t.projb[:, 0:1], r, ALU.add, ALU.add
                                             ).then_inc(norm_done, 1)

            def dve_iter(dve, b, par, more):
                for g in range(GC):
                    if more:
                        if g == 0:
                            dve_xn(dve, b + 1)
                        if g < A_GROUPS:
                            dve_a(dve, b + 1, 1 - par, g)
                    units = b_units(g) if more else range(0)
                    for u in units:
                        dve_b(dve, b + 1, u)
                    if g in (4, 8, 12):
                        dve_acc(dve, b, g // 4 - 1)
                    if g in (9, 10, 11):
                        dve_norm(dve, b, 0, g - 9)
                if more:
                    dve_b_end(dve, b + 1)
                    dve_b_low(dve, b + 1)
                dve_acc(dve, b, 3)
                for step in range(3):
                    dve_norm(dve, b, 1, step)

            @block.vector
            def _(dve):
                for i in range(2):
                    dve.memset(vx[i][:, :, :, :], 0.0).then_inc(ones_set, 1)
                    dve.memset(ks[i][KROWS:KROWS + MROWS, :, :], 1.0).then_inc(ones_set, 1)
                dve.memset(row_max[:, :], 0.0).then_inc(ones_set, 1)
                dve.wait_ge(ones_set, 5)
                for i in range(2):
                    dve.memset(vx[i][:, :, :, HD:HD + 1], 1.0).then_inc(ones_set, 1)
                dve.wait_ge(ones_set, 7)
                dve.sem_inc(mm_a, 1)
                dve.sem_inc(exp_done, 2)
                dve.sem_inc(av_done, 2)
                dve.sem_inc(acc_out, 1)
                dve.sem_inc(norm_done, 1)
                dve.sem_inc(maxT, 1)
                dve.sem_inc(negmax_done, 1)
                dve.sem_inc(parts_out, 16)
                dve_xn(dve, 0)
                for i in range(6):
                    dve_a(dve, 0, 0, i)
                for u in range(UB):
                    dve_b(dve, 0, u)
                dve_b_end(dve, 0)
                dve_b_low(dve, 0)
                iterations(dve, dve_iter)

            def act_a(act, b, i):
                if i < PIECES:
                    w, h = i // 2, i % 2
                    act.wait_ge(mm_a, b * 6 + i + 1 + 1)
                    act.wait_ge(parts_out, 16 * (b + 1))
                    act.activation(parts[:, w, 0, h * HALF:(h + 1) * HALF], bm[i % 2][:, :], ACT.Identity,
                                   bias=t.vec(("q_b", "k_b")[w])).then_inc(hi_done, 1)

            def act_b_hi(act, b):
                act.wait_ge(maxT, b + 1 + 1)
                act.wait_ge(max_out, 16 * b + 16)
                act.activation(neg_max[:, 0, :], bm[0][0:HEADS * NT, 0:P], ACT.Copy, scale=-1.0
                               ).then_inc(negmax_hi, 1)

            def act_exp(act, b, g):
                act.wait_ge(av_done, b * GC + g + 1)
                for h4 in range(4):
                    u = 4 * g + h4
                    act.wait_ge(mm_c, b * UC + u + 1)
                    act.activation(E[:, g % 2, h4, :], sc[u % 2][:, :], ACT.Exp, scale=0.25).then_inc(exp_done, 1)

            def act_iter(act, b, par, more):
                for g in range(GC):
                    act_exp(act, b, g)
                    if more and g < A_GROUPS:
                        act_a(act, b + 1, g)
                if more:
                    act_b_hi(act, b + 1)

            @block.scalar
            def _(act):
                for i in range(6):
                    act_a(act, 0, i)
                act.sem_inc(max_out, 16)
                act_b_hi(act, 0)
                iterations(act, act_iter)

            def pool_a(pool, b):
                for w in range(2):
                    pool.wait_ge(rest_done, b * PIECES + 2 * w + 2)
                    pool.sem_inc(woke, 1)
                    pool.tensor_copy(parts[:, w, 1, :], rest[:, w, :]).then_inc(low_done, 1)
                    pool.wait_ge(low_done, b * 4 + 2 * w + 1)
                    pool.tensor_tensor(parts[:, w, 2, :], rest[:, w, :], parts[:, w, 1, :], ALU.subtract
                                       ).then_inc(low_done, 1)

            @block.gpsimd
            def _(pool):
                pool_a(pool, 0)
                with pool.Fori(1, B) as b:
                    pool_a(pool, b)

            def sp_ab(sp, b, par):
                sp.wait_ge(low_done, b * 4 + 4)
                sp.dma_start(d_parts.rearrange("w s p t -> p w s t"), parts[:, :, :, :]).then_inc(parts_out, 16)
                sp.wait_ge(parts_out, 16 * (b + 2))
                for dst, w, which in ((qs[par], 0, Q_PARTS), (ks[par], 1, K_PARTS)):
                    for i, s in enumerate(which):
                        sp.dma_start(dst[i * HD:(i + 1) * HD, :, :],
                                     d_parts[w, s].rearrange("(h d) t -> d h t", d=HD)).then_inc(stacked, 16)
                sp.wait_ge(negmax_done, b + 1 + 1)
                sp.dma_start(d_max.rearrange("r (u p) -> u r p", p=P), neg_max[:, :, :]).then_inc(max_out, 16)
                sp.wait_ge(max_out, 16 * (b + 2))
                sp.dma_start(qs[par][KROWS:KROWS + MROWS, :, :],
                             d_max.rearrange("r (h t) -> r h t", h=HEADS)).then_inc(max_in, 16)

            @block.sync
            def _(sp):
                sp_ab(sp, 0, 0)
                with sp.Fori(0, B // 2 - 1) as pair:
                    sp_ab(sp, 2 * pair + 1, 1)
                    sp_ab(sp, 2 * pair + 2, 0)
                sp_ab(sp, B - 1, 1)
                sp.wait_ge(max_in, 16 * B)


def layer1_conv(nc, t):
    SIDE, PAD = 32, 34
    with ExitStack() as ctx:
        def sb(name, shape, dt=F32):
            return ctx.enter_context(nc.sbuf_tensor(name, shape, dt))

        def sem(name):
            return ctx.enter_context(nc.semaphore("c_" + name))

        pad = sb("pad", [P, PAD, PAD])
        conv = sb("conv", [P, T])
        hidden = sb("hidden", [P, T])
        second = sb("second", [P, T])
        pw = sb("pw", [P, P])
        amax = sb("amax", [P, 2])
        keep = sb("keep", [P, 2])
        inv = sb("inv", [P, 2])
        off = sb("off", [P, 2])
        tmp = sb("tmp", [P, 4])
        ps = ctx.enter_context(nc.psum_tensor("c_ps", [P, 2 * HALF], F32))
        folded, root = sem("folded"), sem("root")
        padded, tap, hidden_done, kept, mm, second_done, added = (
            sem("padded"), sem("tap"), sem("hidden_done"), sem("kept"), sem("mm"), sem("second_done"), sem("added"))
        with nc.Block() as block:
            @block.vector
            def _(dve):
                dve.memset(pad[:, :, :], 0.0).then_inc(folded, 1)
                for n, bn in enumerate(("bn1", "bn2")):
                    dve.tensor_scalar(tmp[:, n:n + 1], t.vec(bn + "_v"), EPS5, None, ALU.add).then_inc(folded, 1)
                dve.wait_ge(root, 2)
                dve.reciprocal(tmp[:, 2:4], tmp[:, 0:2]).then_inc(folded, 1)
                dve.wait_ge(folded, 4)
                for n, (bn, bias) in enumerate((("bn1", "dw_b"), ("bn2", "pw_b"))):
                    dve.tensor_tensor(inv[:, n:n + 1], tmp[:, 2 + n:3 + n], t.vec(bn + "_g"), ALU.mult).then_inc(folded, 1)
                    dve.tensor_tensor(tmp[:, n:n + 1], t.vec(bias), t.vec(bn + "_m"), ALU.subtract).then_inc(folded, 1)
                dve.wait_ge(folded, 8)
                for n, bn in enumerate(("bn1", "bn2")):
                    dve.scalar_tensor_tensor(off[:, n:n + 1], tmp[:, n:n + 1], inv[:, n:n + 1], t.vec(bn + "_b"),
                                             ALU.mult, ALU.add).then_inc(folded, 1)
                with dve.Fori(0, B) as b:
                    r = t.resid[:, bass.ds(b * T, T)]
                    dve.tensor_scalar(pad[:, 1:SIDE + 1, 1:SIDE + 1], r.rearrange("p (y x) -> p y x", y=SIDE),
                                      t.gscale[:, bass.ds(b, 1)], t.gshift[:, bass.ds(b, 1)],
                                      ALU.mult, ALU.add).then_inc(padded, 1)
                    dve.wait_ge(padded, b + 1)
                    cv = conv[:, :].rearrange("p (y x) -> p y x", y=SIDE)
                    for n in range(9):
                        win = pad[:, n // 3:n // 3 + SIDE, n % 3:n % 3 + SIDE]
                        if n == 0:
                            dve.tensor_scalar(cv, win, t.vec("dw0"), None, ALU.mult).then_inc(tap, 1)
                        else:
                            dve.wait_ge(tap, b * 9 + n)
                            dve.scalar_tensor_tensor(cv, win, t.vec(f"dw{n}"), cv, ALU.mult, ALU.add).then_inc(tap, 1)
                    dve.wait_ge(hidden_done, b + 1)
                    dve.tensor_reduce(amax[:, 0:1], hidden[:, :], AX_X, ALU.max).then_inc(kept, 1)
                    dve.wait_ge(kept, b * 5 + 1)
                    dve.tensor_scalar(keep[:, 0:1], amax[:, 0:1], 4.0, None, ALU.is_ge).then_inc(kept, 1)
                    dve.wait_ge(kept, b * 5 + 2)
                    dve.tensor_scalar(pw[:, :], t.mat("pwT"), keep[:, 0:1], None, ALU.mult).then_inc(kept, 1)
                    dve.wait_ge(second_done, 2 * b + 2)
                    dve.tensor_reduce(amax[:, 1:2], second[:, :], AX_X, ALU.max).then_inc(kept, 1)
                    dve.wait_ge(kept, b * 5 + 4)
                    dve.tensor_scalar(keep[:, 1:2], amax[:, 1:2], 0.001, None, ALU.is_ge).then_inc(kept, 1)
                    dve.wait_ge(kept, b * 5 + 5)
                    dve.scalar_tensor_tensor(r, second[:, :], keep[:, 1:2], r, ALU.mult, ALU.add).then_inc(added, 1)

            @block.scalar
            def _(act):
                act.wait_ge(folded, 3)
                for n in range(2):
                    act.activation(tmp[:, n:n + 1], tmp[:, n:n + 1], ACT.Sqrt).then_inc(root, 1)
                act.wait_ge(folded, 10)
                with act.Fori(0, B) as b:
                    act.wait_ge(tap, 9 * b + 9)
                    act.activation(hidden[:, :], conv[:, :], ACT.Relu, bias=off[:, 0:1], scale=inv[:, 0:1]
                                   ).then_inc(hidden_done, 1)
                    for h in range(2):
                        act.wait_ge(mm, 2 * b + h + 1)
                        act.activation(second[:, h * HALF:(h + 1) * HALF], ps[:, h * HALF:(h + 1) * HALF], ACT.Relu,
                                       bias=off[:, 1:2], scale=inv[:, 1:2]).then_inc(second_done, 1)

            @block.tensor
            def _(pe):
                with pe.Fori(0, B) as b:
                    pe.wait_ge(kept, 5 * b + 3)
                    for h in range(2):
                        pe.matmul(ps[:, h * HALF:(h + 1) * HALF], pw[:, :], hidden[:, h * HALF:(h + 1) * HALF],
                                  start=True, stop=True).then_inc(mm, 1)


def pairs(eng, body):
    with eng.Fori(0, B // 2) as pair:
        body(2 * pair, 0)
        body(2 * pair + 1, 1)


def token_norm(nc, t, tag, eps):
    with ExitStack() as ctx:
        def sb(name, shape, dt=F32):
            return ctx.enter_context(nc.sbuf_tensor(tag + name, shape, dt))

        def sem(name):
            return ctx.enter_context(nc.semaphore(tag + name))

        xb = [sb(f"xb{i}", [P, T]) for i in range(2)]
        xt = [sb(f"xt{i}", [P, NT, P]) for i in range(2)]
        stats = sb("stats", [P, NT, 6])
        mv = sb("mv", [P, NT, 2])
        std = sb("std", [P, NT])
        rstd = sb("rstd", [P, NT])
        turned_in = [ctx.enter_context(nc.psum_tensor(f"{tag}in{i}", [P, NT, P], F32)) for i in range(2)]
        turned_out = [ctx.enter_context(nc.psum_tensor(f"{tag}out{i}", [P, T], F32)) for i in range(2)]
        copied, turned, stat, root, recip, normed, back, stored = (
            sem("copied"), sem("turned"), sem("stat"), sem("root"), sem("recip"), sem("normed"), sem("back"),
            sem("stored"))
        woke, waited = sem("woke"), sem("waited")
        with nc.Block() as block:
            @block.gpsimd
            def _(pool):
                pool.sem_inc(turned, 2)
                pool.sem_inc(normed, 2)
                pool.sem_inc(stored, 2)
                pool.sem_inc(back, 2)

                def body(b, i):
                    pool.wait_ge(turned, b + 1)
                    pool.sem_inc(woke, 1)
                    pool.tensor_copy(xb[i][:, :], t.resid[:, bass.ds(b * T, T)]).then_inc(copied, 1)
                pairs(pool, body)

            @block.tensor
            def _(pe):
                def body(b, i):
                    pe.wait_ge(copied, b + 1)
                    pe.wait_ge(normed, b + 1)
                    for j in range(NT):
                        tr = pe.transpose(turned_in[i][:, j, :], xb[i][:, j * P:(j + 1) * P], t.mat("ident"))
                    tr.then_inc(turned, 1)
                    pe.wait_ge(normed, b + 1 + 2)
                    pe.wait_ge(stored, b + 1)
                    for j in range(NT):
                        tr = pe.transpose(turned_out[i][:, j * P:(j + 1) * P], xt[i][:, j, :], t.mat("ident"))
                    tr.then_inc(back, 1)
                pairs(pe, body)

            @block.vector
            def _(dve):
                def body(b, i):
                    dve.wait_ge(turned, b + 1 + 2)
                    for j in range(NT):
                        bn = dve.bn_stats(stats[:, j, :], turned_in[i][:, j, :])
                    bn.then_inc(stat, 1)
                    dve.wait_ge(stat, 2 * b + 1)
                    dve.sem_inc(waited, 1)
                    for j in range(NT):
                        bn = dve.bn_aggr(mv[:, j, :], stats[:, j, :])
                    bn.then_inc(stat, 1)
                    dve.wait_ge(root, b + 1)
                    dve.reciprocal(rstd[:, :], std[:, :]).then_inc(recip, 1)
                    dve.wait_ge(recip, b + 1)
                    dve.wait_ge(back, b + 1)
                    for j in range(NT):
                        ts = dve.tensor_scalar(xt[i][:, j, :], turned_in[i][:, j, :], mv[:, j, 0:1],
                                               rstd[:, j:j + 1], ALU.subtract, ALU.mult)
                    ts.then_inc(normed, 1)
                pairs(dve, body)

            @block.scalar
            def _(act):
                def body(b, i):
                    act.wait_ge(stat, 2 * b + 2)
                    act.activation(std[:, :], mv[:, :, 1], ACT.Sqrt, bias=t.vec(eps)).then_inc(root, 1)
                    act.wait_ge(back, b + 1 + 2)
                    act.activation(t.xn[:, bass.ds(b * T, T)], turned_out[i][:, :], ACT.Copy).then_inc(stored, 1)
                pairs(act, body)


def layer2_attention(nc, t):
    NEG = -1e30
    with ExitStack() as ctx:
        def sb(name, shape, dt=F32):
            return ctx.enter_context(nc.sbuf_tensor("b_" + name, shape, dt))

        def sem(name):
            return ctx.enter_context(nc.semaphore("b_" + name))

        def psum(name, n):
            return ctx.enter_context(nc.psum_tensor("b_" + name, [P, n], F32))

        wqk = sb("wqk", [P, P])
        identb = sb("identb", [P, P], BF16)
        future = sb("future", [P, HALF], BF16)
        xb = [sb(f"xb{i}", [P, T]) for i in range(2)]
        q = [sb(f"q{i}", [P, T]) for i in range(2)]
        v = [sb(f"v{i}", [P, NT, P]) for i in range(2)]
        prob = [sb(f"prob{i}", [P, T]) for i in range(2)]
        probT = [sb(f"probT{i}", [P, NT, P]) for i in range(2)]
        peak = sb("peak", [P, NT])
        top = sb("top", [P, NT])
        total = sb("total", [P, NT])
        inv = sb("inv", [P, NT])
        s_ps = [psum(f"s_ps{i}", T) for i in range(2)]
        t_ps = psum("t_ps", T)
        o_ps = psum("o_ps", HALF)
        x_ps = psum("x_ps", HALF)
        ready, wdone, copied, mm_p, q_out, v_out = (
            sem("ready"), sem("wdone"), sem("copied"), sem("mm_p"), sem("q_out"), sem("v_out"))
        mm_s, maxed, topped, exped, inverted, scaled, turned, tout, mm_o, added = (
            sem("mm_s"), sem("maxed"), sem("topped"), sem("exped"), sem("inverted"), sem("scaled"), sem("turned"), sem("tout"),
            sem("mm_o"), sem("added"))
        SCALE = 1.0 / float(np.sqrt(C))
        woke = sem("woke")
        banks = [o_ps, x_ps]
        with nc.Block() as block:
            @block.gpsimd
            def _(pool):
                pool.memset(future[:, :], 0.0).then_inc(ready, 1)
                pool.wait_ge(ready, 1)
                pool.affine_select(future[:, HALF - P:], future[:, HALF - P:], pattern=[[-1, P]], compare_op=ALU.is_ge, fill=NEG,
                                   base=0, channel_multiplier=1).then_inc(ready, 1)
                pool.tensor_copy(identb[:, :], t.mat("ident")).then_inc(ready, 1)
                pool.sem_inc(topped, 2)
                pool.sem_inc(exped, 2)
                pool.sem_inc(tout, 1)
                pool.sem_inc(turned, 2)
                pool.sem_inc(mm_o, 2)
                pool.sem_inc(added, 2)

                def body(b, i):
                    pool.wait_ge(mm_o, b * NT + 1)
                    pool.sem_inc(woke, 1)
                    pool.tensor_copy(xb[i][:, :], t.xn[:, bass.ds(b * T, T)]).then_inc(copied, 1)
                pairs(pool, body)

            @block.tensor
            def _(pe):
                pe.matmul(o_ps[:, 0:P], t.mat("Wq"), t.mat("Wk"), start=True, stop=True).then_inc(mm_p, 1)
                pe.wait_ge(ready, 3)
                pe.wait_ge(wdone, 1)

                def project(b, i):
                    pe.wait_ge(copied, b + 1)
                    for n in range(4):
                        if n < 2:
                            pe.wait_ge(added, b * NT + 2)
                        else:
                            pe.wait_ge(q_out, 2 * b + n - 1)
                        bank = banks[n % 2]
                        if n < 2:
                            mm = pe.matmul(bank[:, :], wqk[:, :], xb[i][:, n * HALF:(n + 1) * HALF], start=True, stop=True)
                        else:
                            for j in range(4):
                                k = 4 * (n - 2) + j
                                mm = pe.matmul(bank[:, j * P:(j + 1) * P], xb[i][:, k * P:(k + 1) * P], t.mat("WvT"),
                                               start=True, stop=True)
                        mm.then_inc(mm_p, 1)

                def scores(b, i, m):
                    g = b * NT + m
                    if m < 2:
                        pe.wait_ge(q_out, 2 * b + 2)
                    pe.wait_ge(exped, g + 1)
                    lhsT = q[i][:, m * P:(m + 1) * P]
                    keys = (m + 1) * P
                    for k0 in range(0, keys, HALF):
                        n = min(HALF, keys - k0)
                        diagonal = k0 + n == keys
                        pe.matmul(s_ps[m % 2][:, k0:k0 + n], lhsT, xb[i][:, k0:k0 + n], start=True, stop=not diagonal)
                    mm = pe.matmul(s_ps[m % 2][:, k0:keys], identb[:, :], future[:, HALF - n:], start=False, stop=True)
                    mm.then_inc(mm_s, 1)

                def values(b, i, m):
                    g = b * NT + m
                    pe.wait_ge(scaled, g + 1)
                    pe.wait_ge(tout, g + 1)
                    for k in range(m + 1):
                        tr = pe.transpose(t_ps[:, k * P:(k + 1) * P], prob[m % 2][:, k * P:(k + 1) * P], t.mat("ident"))
                    tr.then_inc(turned, 1)
                    if m == 0:
                        pe.wait_ge(v_out, 2 * b + 2)
                    pe.wait_ge(tout, g + 1 + 1)
                    pe.wait_ge(added, g + 1)
                    for k in range(m + 1):
                        mm = pe.matmul(banks[m % 2][:, 0:P], v[i][:, k, :], probT[m % 2][:, k, :],
                                       start=(k == 0), stop=(k == m))
                    mm.then_inc(mm_o, 1)

                def body(b, i):
                    project(b, i)
                    scores(b, i, 0)
                    for m in range(NT):
                        if m + 1 < NT:
                            scores(b, i, m + 1)
                        values(b, i, m)
                pairs(pe, body)

            @block.vector
            def _(dve):
                dve.wait_ge(mm_p, 1)
                dve.tensor_copy(wqk[:, :], o_ps[:, 0:P]).then_inc(wdone, 1)

                def topmost(b, i, m):
                    g = b * NT + m
                    dve.wait_ge(mm_s, g + 1)
                    dve.tensor_reduce(peak[:, m:m + 1], s_ps[m % 2][:, 0:(m + 1) * P], AX_X, ALU.max).then_inc(maxed, 1)
                    dve.wait_ge(maxed, g + 1)
                    dve.tensor_scalar(top[:, m:m + 1], peak[:, m:m + 1], -SCALE, None, ALU.mult).then_inc(topped, 1)

                def scale(b, i, m):
                    g = b * NT + m
                    dve.wait_ge(exped, g + 1 + 2)
                    dve.reciprocal(inv[:, m:m + 1], total[:, m:m + 1]).then_inc(inverted, 1)
                    dve.wait_ge(inverted, g + 1)
                    pr = prob[m % 2][:, 0:(m + 1) * P]
                    dve.tensor_scalar(pr, pr, inv[:, m:m + 1], None, ALU.mult).then_inc(scaled, 1)

                def finish(b, i, m):
                    g = b * NT + m
                    dve.wait_ge(mm_o, g + 1 + 2)
                    r = t.resid[:, bass.ds(b * T + m * P, P)]
                    dve.tensor_tensor(r, banks[m % 2][:, 0:P], r, ALU.add).then_inc(added, 1)

                def body(b, i):
                    for n in range(2, 4):
                        dve.wait_ge(mm_p, 4 * b + n + 1 + 1)
                        dve.tensor_copy(v[i][:, 4 * n - 8:4 * n - 4, :], banks[n % 2][:, :]).then_inc(v_out, 1)
                    topmost(b, i, 0)
                    for m in range(NT):
                        if m + 1 < NT:
                            topmost(b, i, m + 1)
                        scale(b, i, m)
                        if m:
                            finish(b, i, m - 1)
                    finish(b, i, NT - 1)
                pairs(dve, body)

            @block.scalar
            def _(act):
                def exp(b, i, m):
                    g = b * NT + m
                    act.wait_ge(topped, g + 1 + 2)
                    act.wait_ge(turned, g + 1)
                    act.activation(prob[m % 2][:, 0:(m + 1) * P], s_ps[m % 2][:, 0:(m + 1) * P], ACT.Exp,
                                   bias=top[:, m:m + 1], scale=SCALE, accum_out=total[:, m:m + 1]).then_inc(exped, 1)

                def turn(b, i, m):
                    g = b * NT + m
                    act.wait_ge(turned, g + 1 + 2)
                    act.wait_ge(mm_o, g + 1)
                    act.activation(probT[m % 2][:, 0:m + 1, :], t_ps[:, 0:(m + 1) * P], ACT.Copy).then_inc(tout, 1)

                def body(b, i):
                    for n in range(2):
                        act.wait_ge(mm_p, 4 * b + n + 1 + 1)
                        act.activation(q[i][:, n * HALF:(n + 1) * HALF], banks[n % 2][:, :], ACT.Copy).then_inc(q_out, 1)
                    exp(b, i, 0)
                    for m in range(NT):
                        if m + 1 < NT:
                            exp(b, i, m + 1)
                        turn(b, i, m)
                pairs(act, body)


def moe(nc, t, router, gate_up, down, sel):
    NE, F = 16, 256
    with ExitStack() as ctx:
        def sb(name, shape, dt=F32):
            return ctx.enter_context(nc.sbuf_tensor("m_" + name, shape, dt))

        def sem(name):
            return ctx.enter_context(nc.semaphore("m_" + name))

        def psum(name, shape):
            return ctx.enter_context(nc.psum_tensor("m_" + name, shape, F32))

        w_router = sb("w_router", [P, NE])
        w_gu = sb("w_gu", [P, NE, 2, F])
        w_down = sb("w_down", [P, NE, 2, P])
        w_sel_in = sb("w_sel_in", [P, NE, P])
        w_sel = sb("w_sel", [P, NE, P], BF16)
        iota = sb("iota", [P, NE])
        xb = [sb(f"xb{i}", [P, T]) for i in range(2)]
        logit = sb("logit", [P, NT, NE])
        top = sb("top", [P, NT, 8])
        index = sb("index", [P, NT, 8], U32)
        indexf = sb("indexf", [P, NT, 8])
        wt = sb("wt", [P, 3, NT])
        pick = sb("pick", [P, 2, NT, NE])
        comb = sb("comb", [P, NT, NE])
        high = sb("high", [P, 2, NT, NE], BF16)
        left = sb("left", [P, NT, NE])
        split = sb("split", [P, NT, P])
        combT = sb("combT", [P, T], BF16)
        silu = sb("silu", [P, 2, HALF])
        prod = sb("prod", [P, 2, HALF])
        hid = sb("hid", [P, 2, HALF])
        g_ps = [psum(f"g{i}", [P, HALF]) for i in range(2)]
        u_ps = [psum(f"u{i}", [P, HALF]) for i in range(2)]
        ce_ps = [psum(f"ce{i}", [P, HALF]) for i in range(2)]
        y_ps = psum("y", [P, HALF])
        r_ps = psum("r", [P, HALF])
        loaded, const, woke, waited, copied, prepared = sem("loaded"), sem("const"), sem("woke"), sem("waited"), sem("copied"), sem("prepared")
        mm_r, route, expd, turned, tout = sem("mm_r"), sem("route"), sem("expd"), sem("turned"), sem("tout")
        mm_gu, silu_done, prod_done, hid_done, mm_down, added = (
            sem("mm_gu"), sem("silu_done"), sem("prod_done"), sem("hid_done"), sem("mm_down"), sem("added"))
        UNITS = 2 * NE * 2
        ROUTE = 3 * NT + 12
        with nc.Block() as block:
            @block.sync
            def _(sp):
                for dst, src in ((w_router[:, :], router), (w_gu[:, :, :, :], gate_up), (w_down[:, :, :, :], down),
                                 (w_sel_in[:, :, :], sel)):
                    sp.dma_start(dst, src).then_inc(loaded, 16)

            @block.gpsimd
            def _(pool):
                pool.iota(iota[:, :], pattern=[[1, NE]], base=0, channel_multiplier=0,
                          allow_small_or_imprecise_dtypes=True).then_inc(const, 1)
                pool.sem_inc(hid_done, 2)
                pool.sem_inc(mm_down, 2)
                pool.sem_inc(added, 1)
                pool.sem_inc(tout, 1)

                def body(b, i):
                    pool.wait_ge(mm_down, b * UNITS + 1)
                    pool.sem_inc(woke, 1)
                    pool.tensor_copy(xb[i][:, :], t.xn[:, bass.ds(b * T, T)]).then_inc(copied, 1)
                pairs(pool, body)

            @block.tensor
            def _(pe):
                pe.wait_ge(loaded, 64)
                pe.wait_ge(prepared, 2)

                def gate_up_mm(b, i, k):
                    h, e, f = k // (2 * NE), k // 2 % NE, k % 2
                    x = xb[i][:, h * HALF:(h + 1) * HALF]
                    pe.wait_ge(hid_done, b * UNITS + k + 1)
                    pe.matmul(g_ps[k % 2][:, :], w_gu[:, e, 0, f * P:(f + 1) * P], x, start=True, stop=True)
                    mm = pe.matmul(u_ps[k % 2][:, :], w_gu[:, e, 1, f * P:(f + 1) * P], x, start=True, stop=True)
                    if f == 0:
                        mm = pe.matmul(ce_ps[e % 2][:, :], w_sel[:, e, :], combT[:, h * HALF:(h + 1) * HALF],
                                       start=True, stop=True)
                    mm.then_inc(mm_gu, 1)

                def down_mm(b, i, k):
                    h, e, f = k // (2 * NE), k // 2 % NE, k % 2
                    pe.wait_ge(hid_done, b * UNITS + k + 1 + 2)
                    if e == 0 and f == 0:
                        pe.wait_ge(added, 2 * b + h + 1)
                    pe.matmul(y_ps[:, :], w_down[:, e, f, :], hid[:, k % 2, :], start=(e + f == 0),
                              stop=(e == NE - 1 and f == 1)).then_inc(mm_down, 1)

                def body(b, i):
                    pe.wait_ge(copied, b + 1)
                    pe.wait_ge(tout, 2 * b + 1)
                    for j in range(NT):
                        mm = pe.matmul(r_ps[:, j * NE:(j + 1) * NE], xb[i][:, j * P:(j + 1) * P], w_router[:, :],
                                       start=True, stop=True)
                    mm.then_inc(mm_r, 1)
                    pe.wait_ge(route, (b + 1) * ROUTE)
                    for h in range(2):
                        pe.wait_ge(tout, 2 * b + h + 1)
                        for j in range(4):
                            tr = pe.transpose(r_ps[:, j * P:(j + 1) * P], split[:, 4 * h + j, :], t.mat("ident"))
                        tr.then_inc(turned, 1)
                    pe.wait_ge(tout, 2 * b + 2 + 1)
                    for k in range(UNITS):
                        gate_up_mm(b, i, k)
                        if k:
                            down_mm(b, i, k - 1)
                    down_mm(b, i, UNITS - 1)
                pairs(pe, body)

            @block.vector
            def _(dve):
                dve.wait_ge(const, 1)
                dve.wait_ge(loaded, 64)
                dve.tensor_copy(w_sel[:, :, :], w_sel_in[:, :, :]).then_inc(prepared, 1)
                dve.memset(split[:, :, :], 0.0).then_inc(prepared, 1)
                dve.wait_ge(prepared, 2)

                def routing(b):
                    n = b * ROUTE
                    dve.wait_ge(mm_r, b + 1)
                    dve.tensor_copy(logit[:, :, :], r_ps[:, 0:NT * NE]).then_inc(route, 1)
                    dve.wait_ge(route, n + 1)
                    dve.sem_inc(waited, 1)
                    for j in range(NT):
                        dve.max(top[:, j, :], logit[:, j, :]).then_inc(route, 1)
                    dve.wait_ge(route, n + 1 + NT)
                    dve.sem_inc(waited, 1)
                    for j in range(NT):
                        dve.max_index(index[:, j, :], top[:, j, :], logit[:, j, :]).then_inc(route, 1)
                    dve.wait_ge(route, n + 1 + 2 * NT)
                    dve.tensor_copy(indexf[:, :, :], index[:, :, :]).then_inc(route, 1)
                    dve.tensor_tensor(wt[:, 0, :], top[:, :, 1], top[:, :, 0], ALU.subtract).then_inc(route, 1)
                    dve.wait_ge(expd, b + 1)
                    dve.tensor_scalar(wt[:, 0, :], wt[:, 2, :], 1.0, None, ALU.add).then_inc(route, 1)
                    dve.wait_ge(route, n + 4 + 2 * NT)
                    dve.reciprocal(wt[:, 1, :], wt[:, 0, :]).then_inc(route, 1)
                    dve.wait_ge(route, n + 5 + 2 * NT)
                    dve.tensor_tensor(wt[:, 2, :], wt[:, 2, :], wt[:, 1, :], ALU.mult).then_inc(route, 1)
                    dve.wait_ge(route, n + 6 + 2 * NT)
                    for j in range(NT):
                        for c in range(2):
                            ts = dve.tensor_scalar(pick[:, c, j, :], iota[:, :], indexf[:, j, c:c + 1],
                                                   wt[:, 1 + c, j:j + 1], ALU.is_equal, ALU.mult)
                        ts.then_inc(route, 1)

                def body(b, i):
                    routing(b)
                    dve.wait_ge(route, b * ROUTE + 6 + 3 * NT)
                    dve.tensor_tensor(comb[:, :, :], pick[:, 0, :, :], pick[:, 1, :, :], ALU.add).then_inc(route, 1)
                    n = b * ROUTE + 7 + 3 * NT
                    dve.wait_ge(route, n)
                    dve.tensor_copy(high[:, 0, :, :], comb[:, :, :]).then_inc(route, 1)
                    dve.wait_ge(route, n + 1)
                    dve.tensor_tensor(left[:, :, :], comb[:, :, :], high[:, 0, :, :], ALU.subtract).then_inc(route, 1)
                    dve.wait_ge(route, n + 2)
                    dve.tensor_copy(high[:, 1, :, :], left[:, :, :]).then_inc(route, 1)
                    dve.wait_ge(route, n + 3)
                    dve.tensor_copy(split[:, :, 0:NE], high[:, 0, :, :])
                    dve.tensor_copy(split[:, :, 32:32 + NE], high[:, 1, :, :]).then_inc(route, 1)
                    dve.tensor_tensor(split[:, :, 64:64 + NE], left[:, :, :], high[:, 1, :, :], ALU.subtract).then_inc(route, 1)
                    for h in range(2):
                        dve.wait_ge(turned, 2 * b + h + 1)
                        dve.tensor_copy(combT[:, h * HALF:(h + 1) * HALF], r_ps[:, :]).then_inc(tout, 1)
                    for k in range(UNITS):
                        h, e = k // (2 * NE), k // 2 % NE
                        g = b * UNITS + k
                        dve.wait_ge(silu_done, g + 1)
                        dve.tensor_tensor(prod[:, k % 2, :], u_ps[k % 2][:, :], silu[:, k % 2, :], ALU.mult
                                          ).then_inc(prod_done, 1)
                        dve.wait_ge(prod_done, g + 1)
                        dve.wait_ge(mm_down, g + 1)
                        dve.tensor_tensor(hid[:, k % 2, :], ce_ps[e % 2][:, :], prod[:, k % 2, :], ALU.mult
                                          ).then_inc(hid_done, 1)
                        if k % (2 * NE) == 0 and k:
                            finish(b, h - 1)
                    finish(b, 1)

                def finish(b, h):
                    dve.wait_ge(mm_down, b * UNITS + (h + 1) * 2 * NE + 2)
                    r = t.resid[:, bass.ds(b * T + h * HALF, HALF)]
                    dve.tensor_tensor(r, y_ps[:, :], r, ALU.add).then_inc(added, 1)
                pairs(dve, body)

            @block.scalar
            def _(act):
                def body(b, i):
                    act.wait_ge(route, b * ROUTE + 3 + 2 * NT)
                    act.activation(wt[:, 2, :], wt[:, 0, :], ACT.Exp).then_inc(expd, 1)
                    for k in range(UNITS):
                        g = b * UNITS + k
                        act.wait_ge(mm_gu, g + 1)
                        act.wait_ge(hid_done, g + 1)
                        act.activation(silu[:, k % 2, :], g_ps[k % 2][:, :], ACT.Silu).then_inc(silu_done, 1)
                pairs(act, body)


def spill_residual(nc, t, d_resid, back):
    with nc.semaphore(f"spilled{back}") as spilled, nc.Block() as block:
        @block.sync
        def _(sp):
            for b in range(B):
                dram, sbuf = d_resid[:, b * T:(b + 1) * T], t.resid[:, b * T:(b + 1) * T]
                sp.dma_start(*((sbuf, dram) if back else (dram, sbuf))).then_inc(spilled, 16)
            sp.wait_ge(spilled, 16 * B)


D = 4
NB = 4
HH = NB * HEADS
H3 = 3 * HH
JM = T // D
CHUNK = 16
QUADS = CHUNK // D
SEG = 128
WIN = CHUNK + D - 1
WQ = D * NB * D
OP = SEG + D - 1 + 1
TAU = 0.1
TINY = 1e-16


class Semaphores:

    def __init__(self, nc, tag):
        self.nc, self.tag, self.taken = nc, tag, []

    def __call__(self, name):
        self.taken.append(self.nc.alloc_semaphore(self.tag + name))
        return self.taken[-1]

    def give_back(self):
        self.nc.clear_and_free_semaphores(self.taken)
        self.nc.all_engine_barrier()


class Scan:

    def __init__(self, nc, ctx):
        def sb(name, shape, dt=F32):
            return ctx.enter_context(nc.sbuf_tensor("s_" + name, shape, dt))
        self.w3 = sb("w3", [P, 3 * P])
        self.head_mask = sb("head_mask", [P, HEADS])
        self.lanes = sb("lanes", [P, D, H3])
        self.col = sb("col", [P, 8])
        self.inv = sb("inv", [P, T + SEG + D])
        self.causal = sb("causal", [P, 32, 32])
        self.sel = sb("sel", [H3, 2 * NB, P], BF16)
        self.wo = sb("wo", [P, 2, P])
        self.ik = sb("ik", [P, NB, D, JM])
        self.iv = sb("iv", [P, D, 2, HH, HD + 1])
        self.O = sb("O", [P, 2 * NB, D * (OP + 1)])
        self.Mw = sb("Mw", [H3, D * (OP + 1)])
        self.Mseg = sb("Mseg", [P, SEG])

    def add_work(self, nc, ctx, grp):
        def sb(name, shape, dt=F32):
            return ctx.enter_context(nc.sbuf_tensor(f"s{grp}_" + name, shape, dt))
        self.iqm = [sb(f"iqm{i}", [P, NB, WIN, HEADS]) for i in range(2)]
        self.scratch = sb("scratch", [P, 6, HALF])
        self.Y = sb("Y", [P, CHUNK, 1 + JM])
        self.E = sb("E", [P, 2, D, 2 * P])
        self.mx = sb("mx", [P, D])
        self.negm = sb("negm", [P, 2, CHUNK])
        self.W = sb("W", [P, 2, WQ * SEG // D])
        self.warg = sb("warg", [P, 2, D, SEG])
        self.mx_full = sb("mx_full", [H3, D - 1, SEG])
        self.F = sb("F", [H3, D, SEG])
        self.parts = sb("parts", [H3, D, SEG], BF16)


def scan_projection(nc, t, s, grp):
    with ExitStack() as ctx:
        def sb(name, shape, dt=F32):
            return ctx.enter_context(nc.sbuf_tensor(f"p{grp}_{name}", shape, dt))

        sem = Semaphores(nc, f"p{grp}_")
        ctx.callback(sem.give_back)

        NG = 3 * HEADS
        z = [sb(f"z{i}", [P, NG, HD]) for i in range(2)]
        mx = sb("mx", [P, NG])
        den = sb("den", [P, NG])
        rden = sb("rden", [P, NG])
        soft = [sb(f"soft{i}", [P, NG, HD]) for i in range(2)]
        z_ps = [ctx.enter_context(nc.psum_tensor(f"p{grp}_zp{i}", [P, HALF // HD, HD], F32))[:, 0:NG, :] for i in range(2)]
        t_ps = [ctx.enter_context(nc.psum_tensor(f"p{grp}_tp{i}", [P, 4, P], F32)) for i in range(2)]
        mm, maxed, less, expd, summed, recip, done, turned, out = (
            sem("mm"), sem("maxed"), sem("less"), sem("expd"), sem("summed"), sem("recip"), sem("done"),
            sem("turned"), sem("out"))
        tiles = [(b, rho, jt) for b in range(NB) for rho in range(D) for jt in range(2)]

        def tokens(tile):
            b, rho, jt = tile
            c0 = (grp * NB + b) * T + jt * P * D + rho
            return t.xn[:, c0:c0 + (P - 1) * D + 1:D]

        with nc.Block() as block:
            @block.tensor
            def _(pe):
                def project(n):
                    if n >= 2:
                        pe.wait_ge(less, n - 1)
                    pe.matmul(z_ps[n % 2][:, :, :], tokens(tiles[n]), s.w3[:, :], start=True, stop=True).then_inc(mm, 1)

                def turn(n):
                    pe.wait_ge(done, 2 * n + 1)
                    if n >= 2:
                        pe.wait_ge(out, n - 1)
                    for m in range(2):
                        tr = pe.transpose(t_ps[n % 2][:, m, :], soft[n % 2][:, m * HEADS:(m + 1) * HEADS, :], t.mat("ident"))
                    tr.then_inc(turned, 1)
                project(0)
                for n in range(len(tiles)):
                    if n + 1 < len(tiles):
                        project(n + 1)
                    turn(n)

            @block.vector
            def _(dve):
                for k in range(2):
                    dve.memset(s.iv[:, 2 * k:2 * k + 2, :, :, HD:HD + 1], 1.0)

                def second(n):
                    dve.wait_ge(expd, n + 1)
                    if n:
                        dve.wait_ge(done, 2 * n)
                    dve.tensor_reduce(den[:, :], z[n % 2][:, :, :], AX_X, ALU.add).then_inc(summed, 1)
                    dve.wait_ge(summed, n + 1)
                    dve.reciprocal(rden[:, :], den[:, :]).then_inc(recip, 1)
                    dve.wait_ge(recip, n + 1)
                    if n >= 2:
                        dve.wait_ge(turned, n - 1)
                    b, rho, jt = tiles[n]
                    Q = 2 * HEADS
                    dve.scalar_tensor_tensor(soft[n % 2][:, 0:Q, :], z[n % 2][:, 0:Q, :], TINY,
                                             rden[:, 0:Q].unsqueeze(2).to_broadcast([P, Q, HD]), ALU.max, ALU.mult
                                             ).then_inc(done, 1)
                    dve.scalar_tensor_tensor(s.iv[:, rho, jt, b * HEADS:(b + 1) * HEADS, 0:HD], z[n % 2][:, Q:NG, :], TINY,
                                             rden[:, Q:NG].unsqueeze(2).to_broadcast([P, HEADS, HD]), ALU.max, ALU.mult
                                             ).then_inc(done, 1)
                for n in range(len(tiles)):
                    dve.wait_ge(mm, n + 1)
                    if n:
                        dve.wait_ge(less, n)
                    if n >= 2:
                        dve.wait_ge(done, 2 * (n - 1))
                    dve.tensor_reduce(mx[:, :], z_ps[n % 2][:, :, :], AX_X, ALU.max).then_inc(maxed, 1)
                    dve.wait_ge(maxed, n + 1)
                    dve.tensor_tensor(z[n % 2][:, :, :], z_ps[n % 2][:, :, :],
                                      mx[:, :].unsqueeze(2).to_broadcast([P, NG, HD]), ALU.subtract).then_inc(less, 1)
                    if n:
                        second(n - 1)
                second(len(tiles) - 1)

            @block.scalar
            def _(act):
                def store(n):
                    b, rho, jt = tiles[n]
                    act.wait_ge(turned, n + 1)
                    act.activation(tokens(tiles[n]), t_ps[n % 2][:, 0, :], ACT.Copy)
                    act.activation(s.ik[:, b, rho, jt * P:(jt + 1) * P], t_ps[n % 2][:, 1, :], ACT.Copy).then_inc(out, 1)
                for n in range(len(tiles)):
                    act.wait_ge(less, n + 1)
                    act.activation(z[n % 2][:, :, :], z[n % 2][:, :, :], ACT.Exp, scale=1 / TAU).then_inc(expd, 1)
                    if n:
                        store(n - 1)
                store(len(tiles) - 1)


def scan_segment(nc, t, s, grp, seg):
    tail = seg == T // SEG
    JT = 1 if seg < 4 else 2
    K = min(32 * (seg + 1), JM)
    quads = 1 if tail else QUADS
    chunks = 1 if tail else SEG // CHUNK
    row0 = seg * SEG
    tag = f"g{grp}s{seg}_"
    with ExitStack() as ctx:
        def sb(name, shape, dt=F32):
            return ctx.enter_context(nc.sbuf_tensor(tag + name, shape, dt))

        sem = Semaphores(nc, tag)
        ctx.callback(sem.give_back)

        def psum(name, shape):
            return ctx.enter_context(nc.psum_tensor(tag + name, shape, F32))

        iqm, Y, E = s.iqm, s.Y, s.E
        mx, negm, W = s.mx, s.negm, s.W
        Pv = t.resid[:, :].rearrange("p (k a n r b i h) -> p k a n r b i h", k=2, a=2, n=QUADS, r=D, b=NB, i=D)
        x_ps = [psum(f"x{i}", [P, D, JT * P]) for i in range(2)]
        p_ps = [psum(f"p{i}", [P, D, P]) for i in range(2)]
        o_ps = psum("o", [P, 2 * NB, CHUNK, D])
        masked_q, turned, y_done, causal_done, mx_done, negm_done = (
            sem("masked_q"), sem("turned"), sem("y_done"), sem("causal_done"),
            sem("mx_done"), sem("negm_done"))
        exp_done, back, p_done, av_mm, o_out, m_copied, arg_done, w_done, zeroed, woke = (
            sem("exp_done"), sem("back"), sem("p_done"), sem("av_mm"), sem("o_out"), sem("m_copied"),
            sem("arg_done"), sem("w_done"), sem("zeroed"), sem("woke"))
        ZEROED = 5 if seg == 0 else 1
        xs = quads * D

        def run(eng, body):
            body(0, 0, 0)
            if chunks > 1:
                body(1, 1, 1)
                with eng.Fori(1, chunks // 2) as pair:
                    body(2 * pair, 0, 2)
                    body(2 * pair + 1, 1, 2)

        def before(q, i, k, n):
            return (q, i, k - n) if k >= n else (q - 1, 1 - i, k - n + quads)

        last = (chunks - 1, (chunks - 1) % 2, quads - 1)

        with nc.Block() as block:
            @block.gpsimd
            def _(pool):
                pool.sem_inc(m_copied, 2)

                def mask(q, i):
                    pool.wait_ge(turned, quads * (q - 1) + 8)
                    for b in range(NB):
                        c0 = (grp * NB + b) * T + row0 + XPAD - (D - 1)
                        iq = t.xnp[:, bass.ds(c0 + CHUNK * q, WIN)]
                        pt = pool.tensor_tensor(iqm[i][:, b, :, :], iq.unsqueeze(2).to_broadcast([P, WIN, HEADS]),
                                                s.head_mask[:, :].unsqueeze(1).to_broadcast([P, WIN, HEADS]), ALU.mult)
                    pt.then_inc(masked_q, 1)

                def keep(q, i):
                    pool.wait_ge(negm_done, quads * (q + 1) + 1)
                    pool.sem_inc(woke, 1)
                    pool.tensor_copy(s.Mseg[:, bass.ds(CHUNK * q, xs)], negm[:, i, 0:xs]).then_inc(m_copied, 1)
                mask(0, 0)

                def body(q, i, age):
                    if not tail:
                        mask(q + 1, 1 - i)
                    keep(q, i)
                run(pool, body)

            @block.tensor
            def _(pe):
                pe.sem_inc(turned, 8)
                pe.sem_inc(back, 2 * JT)
                pe.sem_inc(av_mm, 2)

                def scores(q, i, k):
                    if k == 0:
                        pe.wait_ge(masked_q, q + 1)
                    pe.wait_ge(y_done, 4 * (quads * q + k) + 4)
                    for rho in range(D):
                        step = D * k + rho
                        for b in range(NB):
                            mm = pe.matmul(x_ps[k % 2][32 * b:32 * (b + 1), rho, 0:K], iqm[i][:, b, step:step + D, :],
                                           s.ik[:, b, rho, 0:K], start=True, stop=True)
                    mm.then_inc(turned, 1)

                def turn_back(q, i, k):
                    g = quads * q + k
                    pe.wait_ge(exp_done, 4 * (g + 1) + 16)
                    for jt in range(JT):
                        pe.wait_ge(p_done, JT * g + jt + 1)
                        for rho in range(D):
                            tr = pe.transpose(p_ps[(JT * k + jt) % 2][:, rho, :],
                                              E[:, k % 2, rho, jt * P:(jt + 1) * P], t.mat("ident"))
                        tr.then_inc(back, 1)

                def values(q, i, part):
                    if part == 0:
                        pe.wait_ge(p_done, JT * quads * (q + 1) + 2)
                        pe.wait_ge(o_out, q + 1)
                    for b in (2 * part, 2 * part + 1):
                        for rho in range(D):
                            for jt in range(JT):
                                for h4 in range(4):
                                    hh = 4 * b + h4
                                    mm = pe.matmul(o_ps[32 * h4:32 * h4 + HD + 1, b, rho:CHUNK:D, :],
                                                   s.iv[:, rho, jt, hh, :],
                                                   Pv[:, i, jt, :, rho, b // 2, :, 4 * (b % 2) + h4],
                                                   start=jt == 0, stop=jt == JT - 1)
                    if part == 3:
                        mm.then_inc(av_mm, 1)

                pe.wait_ge(zeroed, ZEROED)
                scores(0, 0, 0)

                def body(q, i, age):
                    for k in range(quads):
                        if not tail:
                            if k < quads - 1:
                                scores(q, i, k + 1)
                            else:
                                scores(q + 1, 1 - i, 0)
                        if quads * age + k >= 2:
                            turn_back(*before(q, i, k, 2))
                        if k >= 2 and age:
                            values(q - 1, 1 - i, k - 2)
                        if k < 2 and age == 2:
                            values(q - 2, i, k + 2)
                run(pe, body)
                if not tail:
                    values(chunks - 2, 1 - last[1], 2)
                    values(chunks - 2, 1 - last[1], 3)
                    turn_back(*before(*last, 1))
                turn_back(*last)
                for part in range(4):
                    values(chunks - 1, last[1], part)

            @block.vector
            def _(dve):
                dve.sem_inc(y_done, 8)
                dve.sem_inc(p_done, 2)
                dve.sem_inc(negm_done, 1)
                dve.memset(o_ps[:, :, :, :], 0.0).then_inc(zeroed, 1)
                if seg == 0:
                    dve.memset(E[:, :, :, :], 0.0).then_inc(zeroed, 1)
                    dve.memset(Y[:, :, :], 0.0).then_inc(zeroed, 1)
                    dve.memset(s.O[:, :, :], 0.0).then_inc(zeroed, 1)
                    dve.memset(s.Mw[:, :], 0.0).then_inc(zeroed, 1)
                dve.wait_ge(zeroed, ZEROED)
                for jt in range(JT):
                    for rho in range(D):
                        n = jt * D + rho
                        dve.tensor_scalar(s.warg[:, jt, rho, :], s.inv[:, row0 + rho:row0 + rho + SEG],
                                          s.col[:, n:n + 1], 10.0, ALU.mult, ALU.min).then_inc(arg_done, 1)

                def recur(q, i, k, rho, first):
                    g = quads * q + k
                    slot = D * k + rho
                    if rho:
                        dve.wait_ge(y_done, 8 + 4 * g + rho)
                    else:
                        dve.wait_ge(turned, g + 1 + 8)
                        dve.wait_ge(exp_done, 4 * g + 4)
                        if not first:
                            dve.wait_ge(causal_done, g)
                    c0 = 1 if rho else 0
                    dve.scalar_tensor_tensor(Y[:, slot, 1:1 + K], Y[:, (slot - 1) % CHUNK, c0:c0 + K], 1.0,
                                             x_ps[k % 2][:, rho, 0:K], ALU.add, ALU.mult).then_inc(y_done, 1)

                def mask_future(q, i, k):
                    g = quads * q + k
                    dve.wait_ge(y_done, 8 + 4 * (g + 1))
                    w = Y[:, D * k:D * (k + 1), 1 + K - 32:1 + K]
                    dve.tensor_tensor(w, w, s.causal[:, bass.ds(QUADS * q + k, 1), :].to_broadcast([P, D, 32]), ALU.min
                                      ).then_inc(causal_done, 1)

                def maximum(q, i, k):
                    g = quads * q + k
                    if tail:
                        dve.wait_ge(y_done, 8 + 4 * (g + 1))
                    else:
                        dve.wait_ge(causal_done, g + 1)
                    dve.wait_ge(negm_done, g + 1)
                    dve.tensor_reduce(mx[:, :], Y[:, D * k:D * (k + 1), 1:1 + K], AX_X, ALU.max).then_inc(mx_done, 1)

                def negate(q, i, k):
                    g = quads * q + k
                    dve.wait_ge(mx_done, g + 1)
                    if k == 0:
                        dve.wait_ge(m_copied, q + 1)
                    dve.tensor_scalar(negm[:, i, D * k:D * (k + 1)], mx[:, :], 0.0, -1 / TAU, ALU.max, ALU.mult
                                      ).then_inc(negm_done, 1)

                def weigh(q, i, k, jt):
                    g = quads * q + k
                    dve.wait_ge(back, JT * g + jt + 1 + 2 * JT)
                    if k == 0 and jt == 0:
                        dve.wait_ge(av_mm, q + 1)
                    w = W[:, jt, bass.ds(WQ * (QUADS * q + k), WQ)]
                    dve.tensor_tensor(Pv[:, i, jt, k, :, :, :, :].rearrange("p r b i h -> p (r b i) h"),
                                      p_ps[(JT * k + jt) % 2][:, :, :].rearrange("p r (c h) -> p (r c) h", h=HEADS),
                                      w.unsqueeze(2).to_broadcast([P, WQ, HEADS]), ALU.mult).then_inc(p_done, 1)

                dve.wait_ge(w_done, D * JT)

                def body(q, i, age):
                    for k in range(quads):
                        n = quads * age + k
                        recur(q, i, k, 0, n == 0)
                        if n >= 1:
                            maximum(*before(q, i, k, 1))
                        recur(q, i, k, 1, False)
                        if n >= 1:
                            negate(*before(q, i, k, 1))
                        recur(q, i, k, 2, False)
                        if n >= 2:
                            weigh(*before(q, i, k, 2), 0)
                        recur(q, i, k, 3, False)
                        if n >= 2 and JT == 2:
                            weigh(*before(q, i, k, 2), 1)
                        if not tail:
                            mask_future(q, i, k)
                run(dve, body)
                maximum(*last)
                negate(*last)
                for quad in ([] if tail else [before(*last, 1)]) + [last]:
                    for jt in range(JT):
                        weigh(*quad, jt)

            @block.scalar
            def _(act):
                act.sem_inc(exp_done, 16)
                act.sem_inc(o_out, 1)
                act.wait_ge(zeroed, ZEROED)
                for jt in range(JT):
                    for rho in range(D):
                        act.wait_ge(arg_done, jt * D + rho + 1)
                        act.activation(W[:, jt, :].rearrange("p (u r b i) -> p u r b i", r=D, b=NB, i=D)[:, :, rho, :, :],
                                       s.warg[:, jt, rho, :].rearrange("p (u i) -> p u i", i=D).unsqueeze(2)
                                       .to_broadcast([P, SEG // D, NB, D]), ACT.Exp).then_inc(w_done, 1)

                def exps(q, i, k):
                    g = quads * q + k
                    act.wait_ge(negm_done, g + 1 + 1)
                    act.wait_ge(back, JT * (g + 1))
                    for rho in range(D):
                        act.activation(E[:, k % 2, rho, 0:K], Y[:, D * k + rho, 1:1 + K], ACT.Exp,
                                       bias=negm[:, i, 4 * k + rho:4 * k + rho + 1], scale=1 / TAU).then_inc(exp_done, 1)

                def output(q, i):
                    act.wait_ge(av_mm, q + 1 + 2)
                    view = s.O[:, :, :].rearrange("p g (i w) -> p g w i", i=D)
                    act.activation(view[:, :, bass.ds(D - 1 + CHUNK * q, CHUNK), :], o_ps[:, :, :, :], ACT.Copy
                                   ).then_inc(o_out, 1)

                def body(q, i, age):
                    for k in range(quads):
                        if k == 1 and age == 2:
                            output(q - 2, i)
                        exps(q, i, k)
                run(act, body)
                if not tail:
                    output(chunks - 2, 1 - last[1])
                output(chunks - 1, last[1])


def scan_finish(nc, t, s, grp, seg, d_resid):
    tail = seg == T // SEG
    tag = f"f{grp}s{seg}_"
    n_steps = D if tail else SEG
    w0 = D - 1 if seg == 0 else 0
    w1 = D - 1 if tail else SEG
    NBUF = 3
    with ExitStack() as ctx:
        def sb(name, shape, dt=F32):
            return ctx.enter_context(nc.sbuf_tensor(tag + name, shape, dt))

        sem = Semaphores(nc, tag)
        ctx.callback(sem.give_back)

        def psum(name, shape):
            return ctx.enter_context(nc.psum_tensor(tag + name, shape, F32))

        full = s.mx_full
        F = s.F
        tmp = [s.scratch[:, k, :].rearrange("p (i w) -> p i w", i=D) for k in range(NBUF)]
        r = s.scratch[:, 3, :].rearrange("p (b w) -> p b w", b=NB)
        o = s.scratch[:, 4, :].rearrange("p (b w) -> p b w", b=NB)
        rd = s.scratch[:, 5, :].rearrange("p (b w) -> p b w", b=NB)
        m_ps = psum("m", [H3, D, SEG])
        f_ps = [psum(f"f{i}", [P, D, SEG]) for i in range(NBUF)]
        num = psum("num", [P, NB, SEG])
        den = psum("den", [P, NB, SEG])
        loaded, stored = sem("loaded"), sem("stored")
        split = sem("split")
        moved, mins, less, f_done, spread, scaled, half, summed, mm, rec, quot, added, shifted = (
            sem("moved"), sem("mins"), sem("less"), sem("f_done"), sem("spread"), sem("scaled"), sem("half"),
            sem("summed"), sem("mm"), sem("rec"), sem("quot"), sem("added"), sem("shifted"))
        by_step = lambda ap: ap.rearrange("p (i w) -> p i w", i=D)
        rows = s.Mw[:, 0:D * OP].rearrange("p (i w) -> p i w", i=D)
        res = d_resid[:, :].rearrange("p (b c) -> p b c", b=B)[:, grp * NB:(grp + 1) * NB,
                                                             seg * SEG - (D - 1) + w0:seg * SEG - (D - 1) + w1]
        with nc.Block() as block:
            @block.sync
            def _(sp):
                sp.dma_start(r[:, :, w0:w1], res).then_inc(loaded, 16)
                sp.wait_ge(added, 1)
                sp.dma_start(res, r[:, :, w0:w1]).then_inc(stored, 16)
                sp.wait_ge(stored, 16)

            @block.tensor
            def _(pe):
                for i in range(D):
                    mm_ = pe.matmul(m_ps[:, i, 0:n_steps], s.lanes[:, i, :], s.Mseg[:, 0:n_steps],
                                    start=True, stop=True)
                mm_.then_inc(mm, 1)
                pe.wait_ge(split, 6)

                def spread_out(g):
                    if g >= NBUF:
                        pe.wait_ge(scaled, g - NBUF + 1)
                    pe.matmul(f_ps[g % NBUF][:, :, :], s.sel[:, g, :], s.parts[:, :, :], start=True, stop=True).then_inc(spread, 1)

                for g in range(NBUF - 1):
                    spread_out(g)
                for g in range(2 * NB):
                    if g + NBUF - 1 < 2 * NB:
                        spread_out(g + NBUF - 1)
                    pe.wait_ge(summed, g + 1)
                    b, hg = g // 2, g % 2
                    pe.matmul(num[:, b, :], s.wo[:, hg, :], tmp[g % NBUF][:, 0, :], start=hg == 0, stop=hg == 1)
                    mm_ = pe.matmul(den[:, b, :], t.mat(f"den{hg}"), tmp[g % NBUF][:, 0, :], start=hg == 0, stop=hg == 1)
                    mm_.then_inc(mm, 1)

            @block.vector
            def _(dve):
                dve.wait_ge(mm, 1)
                dve.tensor_copy(by_step(s.Mw[:, :])[:, :, D - 1:D - 1 + n_steps], m_ps[:, :, 0:n_steps]).then_inc(moved, 1)
                dve.wait_ge(moved, 1)
                dve.tensor_tensor(full[:, 0, :], rows[:, 0, 3:3 + SEG], rows[:, 1, 3:3 + SEG], ALU.min).then_inc(mins, 1)
                dve.tensor_tensor(full[:, 1, :], rows[:, 2, 3:3 + SEG], rows[:, 3, 3:3 + SEG], ALU.min).then_inc(mins, 1)
                dve.wait_ge(mins, 2)
                dve.tensor_tensor(full[:, 2, :], full[:, 0, :], full[:, 1, :], ALU.min).then_inc(mins, 1)
                dve.wait_ge(mins, 3)
                dve.tensor_tensor(F[:, :, :], full[:, 2:3, :].to_broadcast([H3, D, SEG]), rows[:, :, 3:3 + SEG],
                                  ALU.subtract).then_inc(less, 1)
                Fp = s.parts
                dve.wait_ge(f_done, 1)
                dve.tensor_copy(Fp[:, :, :], F[:, :, :]).then_inc(split, 1)
                dve.wait_ge(split, 1)
                for p0 in (HH, 2 * HH):
                    dve.tensor_tensor(F[p0:p0 + HH, :, :], F[p0:p0 + HH, :, :], Fp[p0:p0 + HH, :, :], ALU.subtract).then_inc(split, 1)
                dve.wait_ge(split, 3)
                for p0 in (HH, 2 * HH):
                    cp = dve.tensor_copy(Fp[p0:p0 + HH, :, :], F[p0:p0 + HH, :, :])
                cp.then_inc(split, 1)
                dve.wait_ge(split, 4)
                dve.tensor_tensor(F[2 * HH:H3, :, :], F[2 * HH:H3, :, :], Fp[2 * HH:H3, :, :], ALU.subtract).then_inc(split, 1)
                dve.wait_ge(split, 5)
                dve.tensor_copy(Fp[2 * HH:H3, :, :], F[2 * HH:H3, :, :]).then_inc(split, 1)
                for g in range(2 * NB):
                    dve.wait_ge(spread, g + 1)
                    if g >= NBUF:
                        dve.wait_ge(mm, g - NBUF + 2)
                    o_rows = s.O[:, g, 0:D * OP].rearrange("p (i w) -> p i w", i=D)
                    dve.tensor_tensor(tmp[g % NBUF][:, :, :], f_ps[g % NBUF][:, :, :], o_rows[:, :, 3:3 + SEG], ALU.mult
                                      ).then_inc(scaled, 1)
                dve.wait_ge(mm, 1 + 2 * NB)
                dve.reciprocal(rd[:, :, w0:w1], den[:, :, w0:w1]).then_inc(rec, 1)
                dve.wait_ge(rec, 1)
                dve.tensor_tensor(o[:, :, w0:w1], num[:, :, w0:w1], rd[:, :, w0:w1], ALU.mult).then_inc(quot, 1)
                dve.wait_ge(quot, 1)
                dve.wait_ge(loaded, 16)
                dve.tensor_tensor(r[:, :, w0:w1], o[:, :, w0:w1], r[:, :, w0:w1], ALU.add).then_inc(added, 1)
                if not tail:
                    dve.tensor_copy(by_step(s.Mw[:, :])[:, :, 0:D - 1], by_step(s.Mw[:, :])[:, :, SEG:SEG + D - 1]
                                    ).then_inc(shifted, 1)
                    ov = s.O[:, :, :].rearrange("p g (i w) -> p g i w", i=D)
                    dve.tensor_copy(ov[:, :, :, 0:D - 1], ov[:, :, :, SEG:SEG + D - 1]).then_inc(shifted, 1)

            @block.gpsimd
            def _(pool):
                for g in range(2 * NB):
                    x = tmp[g % NBUF]
                    pool.wait_ge(scaled, g + 1)
                    pool.tensor_tensor(x[:, 0:2, :], x[:, 0:2, :], x[:, 2:4, :], ALU.add).then_inc(half, 1)
                    pool.wait_ge(half, g + 1)
                    pool.tensor_tensor(x[:, 0, :], x[:, 0, :], x[:, 1, :], ALU.add).then_inc(summed, 1)

            @block.scalar
            def _(act):
                act.wait_ge(less, 1)
                act.activation(F[:, :, :], F[:, :, :], ACT.Exp).then_inc(f_done, 1)


def layer3_attention(nc, t, io, d_resid):
    spill_residual(nc, t, d_resid, 0)
    with ExitStack() as ctx:
        s = Scan(nc, ctx)
        sel_in = ctx.enter_context(nc.sbuf_tensor("s_sel_in", [H3, 2 * NB, P], F32))
        loads = [(s.w3[:, :], io["w3"]), (s.head_mask[:, :], io["head_mask"]), (s.lanes[:, :, :], io["lanes"]), (s.col[:, :], io["col"]),
                 (s.inv[:, :], io["inv"]), (s.causal[:, :, :], io["causal"]), (sel_in[:, :, :], io["spread"]),
                 (s.wo[:, :, :], io["wo"])]
        with nc.semaphore("s_loaded") as loaded, nc.semaphore("s_woke") as woke, nc.Block() as block:
            @block.sync
            def _(sp):
                for dst, src in loads:
                    sp.dma_start(dst, src).then_inc(loaded, 16)
                sp.wait_ge(loaded, 16 * len(loads))

            @block.gpsimd
            def _(pool):
                pool.memset(t.xnp[:, 0:XPAD], 0.0)
                pool.memset(t.xnp[:, XPAD + N:], 0.0)
                pool.wait_ge(loaded, 16 * len(loads))
                pool.sem_inc(woke, 1)
                pool.tensor_copy(s.sel[:, :, :], sel_in[:, :, :])
        for grp in range(B // NB):
            scan_projection(nc, t, s, grp)
            with ExitStack() as work:
                s.add_work(nc, work, grp)
                for seg in range(T // SEG + 1):
                    scan_segment(nc, t, s, grp, seg)
                    scan_finish(nc, t, s, grp, seg, d_resid)
    spill_residual(nc, t, d_resid, 1)


NEX = 8
SINKHORN = 8
CLIP = 1e-6


def sinkhorn_gates(nc, t, f):
    with ExitStack() as ctx:
        def sb(name, shape, dt=F32):
            return ctx.enter_context(nc.sbuf_tensor("k_" + name, shape, dt))

        sem = Semaphores(nc, "k_")
        ctx.callback(sem.give_back)

        BE = B * NEX
        ones = sb("ones", [P, P])
        gate = sb("gate", [P, NT, B, NEX])
        rcol = sb("rcol", [P, B, NEX])
        rsum = sb("rsum", [P, NT, B])
        rrow = sb("rrow", [P, NT, B])
        G = sb("G", [BE, T])
        left = [sb(f"left{i}", [BE, T]) for i in range(2)]
        top = sb("top", [BE, 8])
        need = sb("need", [BE, 2])
        above = sb("above", [BE, T])
        equal = sb("equal", [BE, T])
        rank = sb("rank", [BE, T])
        chosen = sb("chosen", [P, NT, B, NEX])
        free = sb("free", [P, NT, B, NEX])
        rest = sb("rest", [P, NT, B, NEX])
        l_ps = ctx.enter_context(nc.psum_tensor("k_l", [P, NT, B, NEX], F32))
        c_ps = ctx.enter_context(nc.psum_tensor("k_c", [P, HALF // NEX, NEX], F32))
        g_ps = ctx.enter_context(nc.psum_tensor("k_g", [BE, T], F32))
        loaded, const, mm, step, colsum, turned, picked, chain, back = (
            sem("loaded"), sem("const"), sem("mm"), sem("step"), sem("colsum"), sem("turned"), sem("picked"), sem("chain"), sem("back"))
        with nc.Block() as block:
            @block.sync
            def _(sp):
                sp.dma_start(f.gate_w[:, :], f.io["ffn_gate"]).then_inc(loaded, 16)
                sp.dma_start(f.experts[:, :, :], f.io["ffn_experts"]).then_inc(loaded, 16)
                sp.wait_ge(loaded, 32)

            @block.gpsimd
            def _(pool):
                pool.memset(ones[:, :], 1.0).then_inc(const, 1)

            @block.tensor
            def _(pe):
                pe.wait_ge(loaded, 32)
                pe.wait_ge(const, 1)
                for b in range(B):
                    for j in range(NT):
                        c0 = b * T + j * P
                        mm_ = pe.matmul(l_ps[:, j, b, :], t.xn[:, c0:c0 + P], f.gate_w[:, :], start=True, stop=True)
                mm_.then_inc(mm, 1)
                for n in range(SINKHORN):
                    pe.wait_ge(step, n + 1)
                    for j in range(NT):
                        mm_ = pe.matmul(c_ps[:, 0:B, :], ones[:, :], gate[:, j, :, :], start=j == 0, stop=j == NT - 1)
                    mm_.then_inc(colsum, 1)
                pe.wait_ge(step, SINKHORN + 1)
                for j in range(NT):
                    tr = pe.transpose(g_ps[:, j * P:(j + 1) * P], gate[:, j, :, :], t.mat("ident"))
                tr.then_inc(turned, 1)
                pe.wait_ge(picked, 1)
                for j in range(NT):
                    tr = pe.transpose(l_ps[:, j, :, :], above[:, j * P:(j + 1) * P], t.mat("ident")[0:BE, 0:BE])
                tr.then_inc(back, 1)

            @block.vector
            def _(dve):
                dve.wait_ge(mm, 1)
                dve.tensor_scalar(gate[:, :, :, :], l_ps[:, :, :, :], CLIP, None, ALU.max).then_inc(step, 1)
                for n in range(SINKHORN):
                    dve.wait_ge(colsum, n + 1)
                    dve.reciprocal(rcol[:, :, :], c_ps[:, 0:B, :]).then_inc(chain, 1)
                    dve.wait_ge(chain, 4 * n + 1)
                    dve.tensor_tensor(gate[:, :, :, :], gate[:, :, :, :],
                                      rcol[:, :, :].unsqueeze(1).to_broadcast([P, NT, B, NEX]), ALU.mult).then_inc(chain, 1)
                    dve.wait_ge(chain, 4 * n + 2)
                    dve.tensor_reduce(rsum[:, :, :], gate[:, :, :, :], AX_X, ALU.add).then_inc(chain, 1)
                    dve.wait_ge(chain, 4 * n + 3)
                    dve.reciprocal(rrow[:, :, :], rsum[:, :, :]).then_inc(chain, 1)
                    dve.wait_ge(chain, 4 * n + 4)
                    dve.tensor_tensor(gate[:, :, :, :], gate[:, :, :, :],
                                      rrow[:, :, :].unsqueeze(3).to_broadcast([P, NT, B, NEX]), ALU.mult).then_inc(step, 1)
                    dve.wait_ge(step, n + 2)
                c = 4 * SINKHORN
                dve.wait_ge(turned, 1)
                dve.tensor_copy(G[:, :], g_ps[:, :]).then_inc(chain, 1)
                dve.wait_ge(chain, c + 1)
                c += 1
                ROUNDS = T // NEX // 8
                for n in range(ROUNDS):
                    src = left[(n - 1) % 2] if n else G
                    dve.max(top[:, :], src[:, :]).then_inc(chain, 1)
                    dve.wait_ge(chain, c + 1)
                    c += 1
                    if n < ROUNDS - 1:
                        dve.match_replace(left[n % 2][:, :], top[:, :], src[:, :], -1.0).then_inc(chain, 1)
                        dve.wait_ge(chain, c + 1)
                        c += 1
                thr = top[:, 7:8]
                dve.tensor_scalar(above[:, :], G[:, :], thr, None, ALU.is_gt).then_inc(chain, 1)
                dve.tensor_scalar(equal[:, :], G[:, :], thr, None, ALU.is_equal).then_inc(chain, 1)
                dve.wait_ge(chain, c + 2)
                dve.tensor_reduce(need[:, 0:1], above[:, :], AX_X, ALU.add).then_inc(chain, 1)
                dve.tensor_tensor_scan(rank[:, :], equal[:, :], equal[:, :], 0.0, ALU.add, ALU.max).then_inc(chain, 1)
                dve.wait_ge(chain, c + 4)
                dve.tensor_scalar(need[:, 1:2], need[:, 0:1], -1.0, T / NEX, ALU.mult, ALU.add).then_inc(chain, 1)
                dve.wait_ge(chain, c + 5)
                dve.scalar_tensor_tensor(rank[:, :], rank[:, :], need[:, 1:2], equal[:, :], ALU.is_le, ALU.mult).then_inc(chain, 1)
                dve.wait_ge(chain, c + 6)
                dve.tensor_tensor(above[:, :], above[:, :], rank[:, :], ALU.add).then_inc(picked, 1)
                c += 6
                dve.wait_ge(back, 1)
                dve.tensor_copy(chosen[:, :, :, :], l_ps[:, :, :, :]).then_inc(chain, 1)
                dve.wait_ge(chain, c + 1)
                dve.tensor_scalar(free[:, :, :, :], chosen[:, :, :, :], -1.0, 1.0, ALU.mult, ALU.add).then_inc(chain, 1)
                dve.memset(rest[:, :, :, NEX - 1:NEX], 1.0).then_inc(chain, 1)
                c += 3
                for e in range(NEX - 2, -1, -1):
                    dve.wait_ge(chain, c)
                    dve.tensor_tensor(rest[:, :, :, e], rest[:, :, :, e + 1], free[:, :, :, e + 1], ALU.mult).then_inc(chain, 1)
                    c += 1
                dve.tensor_tensor(chosen[:, :, :, :], chosen[:, :, :, :], gate[:, :, :, :], ALU.mult).then_inc(chain, 1)
                dve.wait_ge(chain, c + 1)
                dve.tensor_tensor(f.weight[:, :, :, :], chosen[:, :, :, :], rest[:, :, :, :], ALU.mult)


def routed_experts(nc, t, f):
    with ExitStack() as ctx:
        def sb(name, shape, dt=F32):
            return ctx.enter_context(nc.sbuf_tensor("e_" + name, shape, dt))

        def psum(name, shape):
            return ctx.enter_context(nc.psum_tensor("e_" + name, shape, F32))

        sem = Semaphores(nc, "e_")
        ctx.callback(sem.give_back)
        xb = [sb(f"xb{i}", [P, T]) for i in range(2)]
        prod = [sb(f"prod{i}", [P, NEX, P]) for i in range(2)]
        y_ps = [psum(f"y{i}", [P, NEX, P]) for i in range(2)]
        z_ps = [psum(f"z{i}", [P, HALF]) for i in range(2)]
        copied, mm_y, prod_done, mm_z, added, woke = (
            sem("copied"), sem("mm_y"), sem("prod_done"), sem("mm_z"), sem("added"), sem("woke"))
        with nc.Block() as block:
            @block.gpsimd
            def _(pool):
                def body(b, i):
                    pool.wait_ge(mm_y, NT * (b + 1))
                    pool.sem_inc(woke, 1)
                    pool.tensor_copy(xb[i][:, :], t.xn[:, bass.ds(b * T, T)]).then_inc(copied, 1)
                pairs(pool, body)

            @block.tensor
            def _(pe):
                pe.sem_inc(mm_y, 2 * NT)
                pe.sem_inc(mm_z, 2)

                def project(b, i, j):
                    pe.wait_ge(prod_done, NT * b + j + 1)
                    for k in range(2):
                        mm = pe.matmul(y_ps[j % 2][:, 4 * k:4 * k + 4, :], xb[i][:, j * P:(j + 1) * P],
                                       f.experts[:, 4 * k:4 * k + 4, :], start=True, stop=True)
                    mm.then_inc(mm_y, 1)

                def turn(b, i, j):
                    pe.wait_ge(prod_done, NT * b + j + 1 + 2)
                    if j % 4 == 0:
                        pe.wait_ge(added, 2 * b + j // 4 + 1)
                    for e in range(NEX):
                        mm = pe.matmul(z_ps[j // 4][:, (j % 4) * P:(j % 4 + 1) * P], prod[j % 2][:, e, :], t.mat("ident"),
                                       start=e == 0, stop=e == NEX - 1)
                    mm.then_inc(mm_z, 1)

                def body(b, i):
                    pe.wait_ge(copied, b + 1)
                    project(b, i, 0)
                    for j in range(NT):
                        if j < NT - 1:
                            project(b, i, j + 1)
                        turn(b, i, j)
                pairs(pe, body)

            @block.vector
            def _(dve):
                dve.sem_inc(prod_done, 2)
                dve.sem_inc(added, 2)

                def body(b, i):
                    for j in range(NT):
                        n = NT * b + j
                        dve.wait_ge(mm_y, n + 1 + 2 * NT)
                        dve.wait_ge(mm_z, n + 1)
                        w = f.weight[:, j, bass.ds(b, 1), :].rearrange("p a e -> p (a e)")
                        dve.tensor_tensor(prod[j % 2][:, :, :], y_ps[j % 2][:, :, :],
                                          w.unsqueeze(2).to_broadcast([P, NEX, P]), ALU.mult).then_inc(prod_done, 1)
                        if j == 5:
                            add(b, 0)
                    add(b, 1)

                def add(b, h):
                    dve.wait_ge(mm_z, NT * b + 4 * (h + 1) + 2)
                    r = t.resid[:, bass.ds(b * T + h * HALF, HALF)]
                    dve.tensor_tensor(r, z_ps[h][:, :], r, ALU.add).then_inc(added, 1)
                pairs(dve, body)


class RoutedTensors:
    def __init__(self, nc, ctx, io):
        self.io = io
        self.gate_w = ctx.enter_context(nc.sbuf_tensor("r_gate_w", [P, NEX], F32))
        self.experts = ctx.enter_context(nc.sbuf_tensor("r_experts", [P, NEX, P], F32))
        self.weight = ctx.enter_context(nc.sbuf_tensor("r_weight", [P, NT, B, NEX], F32))


def layer3_ffn(nc, t, io):
    with ExitStack() as ctx:
        f = RoutedTensors(nc, ctx, io)
        sinkhorn_gates(nc, t, f)
        routed_experts(nc, t, f)


def store_result(nc, t, out):
    with nc.semaphore("stored") as stored, nc.Block() as block:
        @block.sync
        def _(sp):
            for b in range(B):
                sp.dma_start(out[b], t.resid[:, b * T:(b + 1) * T]).then_inc(stored, 16)
            sp.wait_ge(stored, 16 * B)


class Tensors:

    def __init__(self, nc, ctx):
        def sb(name, shape, dt=F32):
            return ctx.enter_context(nc.sbuf_tensor(name, shape, dt))
        self.resid = sb("resid", [P, N])
        self.vecs = sb("vecs", [P, len(VECS)])
        self.mats = sb("mats", [P, len(MATS) * P])
        self.gscale = sb("gscale", [P, B])
        self.gshift = sb("gshift", [P, B])
        self.projb = sb("projb", [P, 1])

    def add_xn(self, nc, ctx):
        self.xnp = ctx.enter_context(nc.sbuf_tensor("xnp", [P, XPAD + N + XPAD], F32))
        self.xn = self.xnp[:, XPAD:XPAD + N]

    def vec(self, name):
        return self.vecs[:, VI[name]:VI[name] + 1]

    def mat(self, name):
        return self.mats[:, MI[name] * P:(MI[name] + 1) * P]


def build(nc, io, out):
    d_parts = nc.dram_tensor("d_parts", (2, 3, P, T), BF16, kind="Internal").ap()
    d_max = nc.dram_tensor("d_max", (MROWS, HEADS * T), BF16, kind="Internal").ap()
    d_resid = nc.dram_tensor("d_resid", (P, N), F32, kind="Internal").ap()
    with ExitStack() as ctx:
        t = Tensors(nc, ctx)
        loads = [(t.vecs[:, :], io["vecs"]), (t.mats[:, :], io["mats"])]
        loads += [(t.resid[:, b * T:(b + 1) * T], io["x"][b]) for b in range(B)]
        group_norm(nc, t, "n0", ("norm_w", "norm_b"), loads)
        layer0_attention(nc, t, d_parts, d_max)
        group_norm(nc, t, "n1", None)
        layer1_conv(nc, t)
        t.add_xn(nc, ctx)
        token_norm(nc, t, "n2", "eps5")
        layer2_attention(nc, t)
        token_norm(nc, t, "n3", "eps5")
        moe(nc, t, io["router"], io["gate_up"], io["down"], io["sel"])
        token_norm(nc, t, "n4", "eps5")
        layer3_attention(nc, t, io, d_resid)
        token_norm(nc, t, "n5", "eps5")
        layer3_ffn(nc, t, io)
        store_result(nc, t, out)


def constants():
    ident = np.eye(P, dtype=np.float32)
    gavg = np.kron(np.eye(32), np.full((4, 4), 0.25)).astype(np.float32)
    mats = {"ident": ident, "gavg": gavg}
    for hg in range(2):
        num, den = np.zeros((P, P), np.float32), np.zeros((P, P), np.float32)
        for h4 in range(4):
            for d in range(HD):
                num[32 * h4 + d, (4 * hg + h4) * HD + d] = 1
                den[32 * h4 + HD, (4 * hg + h4) * HD + d] = 1
        mats[f"num{hg}"], mats[f"den{hg}"] = num, den
    return mats


def expert_selector(NE):
    sel = np.zeros((P, NE, P), np.float32)
    for part in range(3):
        sel[32 * part + np.arange(NE), np.arange(NE), :] = 1
    return sel


def scan_constants():
    part = np.arange(P)
    col = np.stack([D * (P * jt + part) + rho for jt in range(2) for rho in range(D)], 1).astype(np.float32)
    r = np.arange(T + SEG + D) - (D - 1)
    inv = np.where(r >= 0, 10.0 / np.maximum(r + 1, 1), 0).astype(np.float32)
    u, j = np.arange(32)[:, None], np.arange(32)[None, :]
    last_row = (part // HEADS % D == D - 1)[:, None, None]
    lanes = np.zeros((NB, D, HEADS, D, 3, NB, HEADS), np.float32)
    for b in range(NB):
        for i in range(D):
            for h in range(HEADS):
                lanes[b, i, h, i, :, b, h] = 1
    causal = np.where(np.where(last_row, j <= u, j <= u - 1), np.float32(1e30), np.float32(-1e30)).astype(np.float32)
    spread = np.zeros((HH, 2 * NB, P), np.float32)
    for g in range(2 * NB):
        for h4 in range(4):
            spread[4 * g + h4, g, 32 * h4:32 * (h4 + 1)] = 1
    head_mask = np.kron(np.eye(HEADS), np.ones((HD, 1))).astype(np.float32)
    return {"col": col, "inv": np.ascontiguousarray(np.broadcast_to(inv, (P, len(inv)))), "causal": causal,
            "spread": np.concatenate([spread] * 3), "lanes": lanes.reshape(P, D, H3), "head_mask": head_mask}


def layout(inputs):
    i = {k: np.asarray(v) for k, v in inputs.items()}
    w = i["L0_conv_qkv_w"].reshape(HEADS, 3, HD, C).transpose(1, 0, 2, 3).reshape(3, C, C)
    qb = i["L0_conv_qkv_b"].reshape(HEADS, 3, HD).transpose(1, 0, 2).reshape(3, C)
    vec = {"norm_w": i["L0_conv_norm_w"], "norm_b": i["L0_conv_norm_b"], "q_b": qb[0], "k_b": qb[1], "v_b": qb[2],
           "proj_b": i["L0_conv_proj_b"], "dw_b": i["L1_conv_dw_b"], "pw_b": i["L1_conv_pw_b"]}
    for n in range(9):
        vec[f"dw{n}"] = i["L1_conv_dw_w"].reshape(C, 9)[:, n]
    for n in ("bn1", "bn2"):
        for s in "gbmv":
            vec[f"{n}_{s}"] = i[f"L1_conv_{n}_{s}"]
    vec["eps5"] = np.full(C, EPS5, np.float32)
    mats = constants()
    mats |= {"qT": w[0].T, "kT": w[1].T, "vT": w[2].T, "projT": i["L0_conv_proj_w"].T,
             "pwT": i["L1_conv_pw_w"].reshape(C, C).T,
             "Wq": i["L2_attn_Wq"], "Wk": i["L2_attn_Wk"], "WvT": i["L2_attn_Wv"].T}
    NE = i["L2_ffn_router_w"].shape[0]
    gate_up = np.stack([i["L2_ffn_gate_w"], i["L2_ffn_up_w"]]).transpose(2, 1, 0, 3)
    down = i["L2_ffn_down_w"].reshape(NE, 2, P, C).transpose(2, 0, 1, 3)
    w3 = np.concatenate([i["L3_attn_wq"], i["L3_attn_wk"], i["L3_attn_wv"]], 1)
    wo = np.zeros((P, 2, P), np.float32)
    for h in range(HEADS):
        wo[32 * (h % 4):32 * (h % 4) + HD, h // 4, h * HD:(h + 1) * HD] = i["L3_attn_wo"].reshape(HEADS, HD, HD)[h]
    return {"x": i["x"].reshape(B, C, T), "w3": np.ascontiguousarray(w3), "wo": wo, **scan_constants(),
            "ffn_gate": i["L3_ffn_gate_weight"].reshape(C, NEX),
            "ffn_experts": np.ascontiguousarray(i["L3_ffn_experts"].transpose(1, 0, 2)),
            "router": np.ascontiguousarray(i["L2_ffn_router_w"].T),
            "gate_up": np.ascontiguousarray(gate_up), "down": np.ascontiguousarray(down),
            "sel": expert_selector(NE),
            "vecs": np.ascontiguousarray(np.stack([vec[n] for n in VECS], 1)),
            "mats": np.ascontiguousarray(np.concatenate([mats[n] for n in MATS], 1))}


def kernel(**inputs):
    import concourse.bacc as bacc
    from concourse.bass_utils import run_bass_kernel_spmd

    nc = bacc.Bacc("TRN2", target_bir_lowering=False, num_devices=1)
    arrays = layout(inputs)
    io = {n: nc.dram_tensor(f"in_{n}", a.shape, mybir.dt.from_np(a.dtype), kind="ExternalInput").ap()
          for n, a in arrays.items()}
    out = nc.dram_tensor("out_0_dram", (B, C, T), F32, kind="ExternalOutput").ap()
    build(nc, io, out)
    r = run_bass_kernel_spmd(nc, [{f"in_{n}": a for n, a in arrays.items()}], core_ids=[0])
    return r.results[0]["out_0_dram"].reshape(B, C, 32, 32)
```
